# Optimizing a Trainium2 kernel written in Bass

```python
import numpy as np
import jax
import jax.numpy as jnp

def _softmax(x, axis=-1):
    return jax.nn.softmax(x, axis=axis)

def _gelu(x):
    return jax.nn.gelu(x, approximate=True)

def _silu(x):
    return jax.nn.silu(x)

def _sigmoid(x):
    return jax.nn.sigmoid(x)

def _layernorm(x, axis=-1, eps=1e-05):
    m = jnp.mean(x, axis=axis, keepdims=True)
    v = jnp.var(x, axis=axis, keepdims=True)
    return (x - m) / jnp.sqrt(v + eps)

def _scatter_add(tgt, idx, src, axis=0):
    return tgt.at[idx].add(src)

def _segment_sum(src, seg, n):
    return jax.ops.segment_sum(src, seg, n)
kernel_name = 'mk_gps_d1_gnn_r8_133dd9'

def setup_inputs(seed: int=0):
    np.random.seed(seed)
    _w = jnp.asarray

    def _rec_inputs():
        import jax
        import jax.numpy as jnp
        _gk = jax.random.key(seed)
        x = -0.0005963 + 1.001 * jax.random.normal(jax.random.fold_in(_gk, 1), (384, 1024), jnp.float32)
        src = jax.random.randint(jax.random.fold_in(_gk, 2), (6144,), 0, 384, jnp.int32)
        dst = jax.random.randint(jax.random.fold_in(_gk, 3), (6144,), 0, 384, jnp.int32)
        _o = jnp.argsort(dst, stable=True)
        src = src[_o]
        dst = dst[_o]
        edge_type_5 = jax.random.randint(jax.random.fold_in(_gk, 12), (6144,), 0, 5, jnp.int32)
        return (x, src, dst, edge_type_5)
    x, src, dst, edge_type_5 = _rec_inputs()

    def _L0_gnn_setup():
        import jax, jax.numpy as jnp
        import numpy as np
        N = 384
        E = 12288
        IN_F = 1024
        OUT_F = 1024
        H = 16
        D = OUT_F // H
        NUM_ETYPES = 4

        def _build_mask(edge_index, edge_type, edge_type_weights, dtype):
            src, dst = (edge_index[0], edge_index[1])
            w = jax.nn.softplus(edge_type_weights)
            mask = jnp.full((N, N), -jnp.inf, dtype=dtype)
            mask = mask.at[src, dst].set(w[edge_type - 1])
            diag = jnp.diagonal(mask)
            idx = jnp.arange(N)
            mask = mask.at[idx, idx].set(jnp.where(jnp.isneginf(diag), w[3], diag))
            return mask
        key = jax.random.key(seed)
        ks = jax.random.split(key, 20)
        p = lambda k, shape: jax.random.normal(k, shape, dtype=jnp.float32) * 0.02
        return {'x': jax.random.normal(ks[0], (N, IN_F), dtype=jnp.float32), 'edge_index': jax.random.randint(ks[1], (2, E), 0, N), 'edge_type': jax.random.randint(ks[2], (E,), 1, NUM_ETYPES + 1), 'edge_type_weights': jnp.ones((NUM_ETYPES,), jnp.float32) + 0.1 * jax.random.normal(ks[3], (NUM_ETYPES,), dtype=jnp.float32), 'wq': p(ks[4], (OUT_F, IN_F)), 'bq': p(ks[5], (OUT_F,)), 'wk': p(ks[6], (OUT_F, IN_F)), 'bk': p(ks[7], (OUT_F,)), 'wv': p(ks[8], (OUT_F, IN_F)), 'bv': p(ks[9], (OUT_F,)), 'wiq': p(ks[10], (OUT_F, OUT_F)), 'biq': p(ks[11], (OUT_F,)), 'wik': p(ks[12], (OUT_F, OUT_F)), 'bik': p(ks[13], (OUT_F,)), 'wiv': p(ks[14], (OUT_F, OUT_F)), 'biv': p(ks[15], (OUT_F,)), 'wo': p(ks[16], (OUT_F, OUT_F)), 'bo': p(ks[17], (OUT_F,))}
    _L0_gnn_all = _L0_gnn_setup()
    _L0_gnn_in = {k: v for k, v in _L0_gnn_all.items() if k in ('edge_type_weights', 'wq', 'bq', 'wk', 'bk', 'wv', 'bv', 'wiq', 'biq', 'wik', 'bik', 'wiv', 'biv', 'wo', 'bo')}
    del _L0_gnn_all

    def _L0_mix_setup():
        import jax, jax.numpy as jnp
        import numpy as np
        D_MODEL = 1024
        D_FF = 512
        FFN_H = int(2 * D_FF / 3)
        B, S = (4, 512)
        LN_EPS = 1e-05
        ATTN_EPS = 1e-06

        def layer_norm(x, g, b):
            mu = jnp.mean(x, axis=-1, keepdims=True)
            var = jnp.mean(jnp.square(x - mu), axis=-1, keepdims=True)
            return (x - mu) * jax.lax.rsqrt(var + LN_EPS) * g + b
        key = jax.random.key(seed)
        ks = jax.random.split(key, 16)
        s = 0.02
        return {'x': jax.random.normal(ks[0], (B, S, D_MODEL), dtype=jnp.float32), 'Wqkv': jax.random.normal(ks[1], (D_MODEL, 3 * D_MODEL), dtype=jnp.float32) * s, 'bqkv': jnp.zeros((3 * D_MODEL,), jnp.float32), 'Wg': jax.random.normal(ks[2], (D_MODEL, FFN_H), dtype=jnp.float32) * s, 'bg': jnp.zeros((FFN_H,), jnp.float32), 'Wu': jax.random.normal(ks[3], (D_MODEL, FFN_H), dtype=jnp.float32) * s, 'bu': jnp.zeros((FFN_H,), jnp.float32), 'Wd': jax.random.normal(ks[4], (FFN_H, D_MODEL), dtype=jnp.float32) * s, 'bd': jnp.zeros((D_MODEL,), jnp.float32), 'g1': jnp.ones((D_MODEL,), jnp.float32), 'b1': jnp.zeros((D_MODEL,), jnp.float32), 'g2': jnp.ones((D_MODEL,), jnp.float32), 'b2': jnp.zeros((D_MODEL,), jnp.float32)}
    _L0_mix_all = _L0_mix_setup()
    _L0_mix_in = {k: v for k, v in _L0_mix_all.items() if k in ('Wqkv', 'bqkv', 'Wg', 'bg', 'Wu', 'bu', 'Wd', 'bd', 'g1', 'b1', 'g2', 'b2')}
    del _L0_mix_all

    def _L0_ffn_setup():
        import jax, jax.numpy as jnp
        import numpy as np
        B, S, D = (4, 256, 1024)
        E, F = (8, 512)
        key = jax.random.key(seed)
        ks = jax.random.split(key, 5)
        x = jax.random.normal(ks[0], (B, S, D), dtype=jnp.float32)
        switch_w = jax.random.normal(ks[1], (D, E), dtype=jnp.float32) * D ** (-0.5)
        switch_b = jnp.zeros((E,), dtype=jnp.float32)
        w1 = jax.random.normal(ks[2], (E, D, F), dtype=jnp.float32) * D ** (-0.5)
        b1 = jnp.zeros((E, F), dtype=jnp.float32)
        w2 = jax.random.normal(ks[3], (E, F, D), dtype=jnp.float32) * F ** (-0.5)
        b2 = jnp.zeros((E, D), dtype=jnp.float32)
        return {'x': x, 'switch_w': switch_w, 'switch_b': switch_b, 'w1': w1, 'b1': b1, 'w2': w2, 'b2': b2}
    _L0_ffn_all = _L0_ffn_setup()
    _L0_ffn_in = {k: v for k, v in _L0_ffn_all.items() if k in ('switch_w', 'switch_b', 'w1', 'b1', 'w2', 'b2')}
    del _L0_ffn_all
    return {'x': x, 'src': src, 'dst': dst, 'edge_type_5': edge_type_5, 'L0_gnn_edge_type_weights': _L0_gnn_in['edge_type_weights'], 'L0_gnn_wq': _L0_gnn_in['wq'], 'L0_gnn_bq': _L0_gnn_in['bq'], 'L0_gnn_wk': _L0_gnn_in['wk'], 'L0_gnn_bk': _L0_gnn_in['bk'], 'L0_gnn_wv': _L0_gnn_in['wv'], 'L0_gnn_bv': _L0_gnn_in['bv'], 'L0_gnn_wiq': _L0_gnn_in['wiq'], 'L0_gnn_biq': _L0_gnn_in['biq'], 'L0_gnn_wik': _L0_gnn_in['wik'], 'L0_gnn_bik': _L0_gnn_in['bik'], 'L0_gnn_wiv': _L0_gnn_in['wiv'], 'L0_gnn_biv': _L0_gnn_in['biv'], 'L0_gnn_wo': _L0_gnn_in['wo'], 'L0_gnn_bo': _L0_gnn_in['bo'], 'L0_mix_Wqkv': _L0_mix_in['Wqkv'], 'L0_mix_bqkv': _L0_mix_in['bqkv'], 'L0_mix_Wg': _L0_mix_in['Wg'], 'L0_mix_bg': _L0_mix_in['bg'], 'L0_mix_Wu': _L0_mix_in['Wu'], 'L0_mix_bu': _L0_mix_in['bu'], 'L0_mix_Wd': _L0_mix_in['Wd'], 'L0_mix_bd': _L0_mix_in['bd'], 'L0_mix_g1': _L0_mix_in['g1'], 'L0_mix_b1': _L0_mix_in['b1'], 'L0_mix_g2': _L0_mix_in['g2'], 'L0_mix_b2': _L0_mix_in['b2'], 'L0_ffn_switch_w': _L0_ffn_in['switch_w'], 'L0_ffn_switch_b': _L0_ffn_in['switch_b'], 'L0_ffn_w1': _L0_ffn_in['w1'], 'L0_ffn_b1': _L0_ffn_in['b1'], 'L0_ffn_w2': _L0_ffn_in['w2'], 'L0_ffn_b2': _L0_ffn_in['b2']}

def reference(x, src, dst, edge_type_5, L0_gnn_edge_type_weights, L0_gnn_wq, L0_gnn_bq, L0_gnn_wk, L0_gnn_bk, L0_gnn_wv, L0_gnn_bv, L0_gnn_wiq, L0_gnn_biq, L0_gnn_wik, L0_gnn_bik, L0_gnn_wiv, L0_gnn_biv, L0_gnn_wo, L0_gnn_bo, L0_mix_Wqkv, L0_mix_bqkv, L0_mix_Wg, L0_mix_bg, L0_mix_Wu, L0_mix_bu, L0_mix_Wd, L0_mix_bd, L0_mix_g1, L0_mix_b1, L0_mix_g2, L0_mix_b2, L0_ffn_switch_w, L0_ffn_switch_b, L0_ffn_w1, L0_ffn_b1, L0_ffn_w2, L0_ffn_b2):
    import jax
    import jax.numpy as jnp

    def _L0_gnn_ref(x, edge_index, edge_type, edge_type_weights, wq, bq, wk, bk, wv, bv, wiq, biq, wik, bik, wiv, biv, wo, bo):
        import jax, jax.numpy as jnp
        import numpy as np
        N = 384
        E = 12288
        IN_F = 1024
        OUT_F = 1024
        H = 16
        D = OUT_F // H
        NUM_ETYPES = 4

        def _build_mask(edge_index, edge_type, edge_type_weights, dtype):
            src, dst = (edge_index[0], edge_index[1])
            w = jax.nn.softplus(edge_type_weights)
            mask = jnp.full((N, N), -jnp.inf, dtype=dtype)
            mask = mask.at[src, dst].set(w[edge_type - 1])
            diag = jnp.diagonal(mask)
            idx = jnp.arange(N)
            mask = mask.at[idx, idx].set(jnp.where(jnp.isneginf(diag), w[3], diag))
            return mask
        q = x @ wq.T + bq
        k = x @ wk.T + bk
        v = x @ wv.T + bv
        q2 = (q @ wiq.T + biq).reshape(N, H, D).transpose(1, 0, 2)
        k2 = (k @ wik.T + bik).reshape(N, H, D).transpose(1, 0, 2)
        v2 = (v @ wiv.T + biv).reshape(N, H, D).transpose(1, 0, 2)
        mask = _build_mask(edge_index, edge_type, edge_type_weights, x.dtype)
        scale = 1.0 / np.sqrt(D).astype(np.float32)
        scores = jnp.einsum('hnd,hmd->hnm', q2, k2) * scale + mask[None]
        attn = jax.nn.softmax(scores, axis=-1)
        out = jnp.einsum('hnm,hmd->hnd', attn, v2)
        out = out.transpose(1, 0, 2).reshape(N, OUT_F)
        return out @ wo.T + bo

    def _L0_mix_ref(x, Wqkv, bqkv, Wg, bg, Wu, bu, Wd, bd, g1, b1, g2, b2):
        import jax, jax.numpy as jnp
        import numpy as np
        D_MODEL = 1024
        D_FF = 512
        FFN_H = int(2 * D_FF / 3)
        B, S = (4, 512)
        LN_EPS = 1e-05
        ATTN_EPS = 1e-06

        def layer_norm(x, g, b):
            mu = jnp.mean(x, axis=-1, keepdims=True)
            var = jnp.mean(jnp.square(x - mu), axis=-1, keepdims=True)
            return (x - mu) * jax.lax.rsqrt(var + LN_EPS) * g + b
        qkv = jnp.einsum('bsd,de->bse', x, Wqkv) + bqkv
        q, k, v = jnp.split(qkv, 3, axis=-1)
        qp = jax.nn.elu(q) + 1.0
        kp = jax.nn.elu(k) + 1.0
        kv = jnp.einsum('bsd,bse->bde', kp, v)
        num = jnp.einsum('bsd,bde->bse', qp, kv)
        k_sum = jnp.sum(kp, axis=1)
        den = jnp.einsum('bsd,bd->bs', qp, k_sum)[..., None]
        attn = num / (den + ATTN_EPS)
        x = layer_norm(x + attn, g1, b1)
        gate = jnp.einsum('bsd,dh->bsh', x, Wg) + bg
        up = jnp.einsum('bsd,dh->bsh', x, Wu) + bu
        ffn = jnp.einsum('bsh,hd->bsd', jax.nn.silu(gate) * up, Wd) + bd
        return layer_norm(x + ffn, g2, b2)

    def _L0_ffn_ref(x, switch_w, switch_b, w1, b1, w2, b2):
        import jax, jax.numpy as jnp
        import numpy as np
        B, S, D = (4, 256, 1024)
        E, F = (8, 512)
        b, s, d = x.shape
        t = x.reshape(-1, d)
        logits = t @ switch_w + switch_b
        route_prob = jax.nn.softmax(logits, axis=-1)
        route_prob_max = jnp.max(route_prob, axis=-1)
        routes = jnp.argmax(route_prob, axis=-1)
        out = jnp.zeros_like(t)
        n_experts = w1.shape[0]
        for e in range(n_experts):
            h = jax.nn.gelu(t @ w1[e] + b1[e])
            y = h @ w2[e] + b2[e]
            mask = (routes == e)[:, None]
            out = jnp.where(mask, y, out)
        out = out * route_prob_max[:, None]
        return out.reshape(b, s, d)
    edge_index = jnp.stack([src, dst])
    xn = _layernorm(x, axis=-1)
    x = x + _L0_gnn_ref(xn, edge_index, edge_type_5, L0_gnn_edge_type_weights, L0_gnn_wq, L0_gnn_bq, L0_gnn_wk, L0_gnn_bk, L0_gnn_wv, L0_gnn_bv, L0_gnn_wiq, L0_gnn_biq, L0_gnn_wik, L0_gnn_bik, L0_gnn_wiv, L0_gnn_biv, L0_gnn_wo, L0_gnn_bo) + _L0_mix_ref(xn[None], L0_mix_Wqkv, L0_mix_bqkv, L0_mix_Wg, L0_mix_bg, L0_mix_Wu, L0_mix_bu, L0_mix_Wd, L0_mix_bd, L0_mix_g1, L0_mix_b1, L0_mix_g2, L0_mix_b2)[0]
    x = x + _L0_ffn_ref(_layernorm(x, axis=-1)[None], L0_ffn_switch_w, L0_ffn_switch_b, L0_ffn_w1, L0_ffn_b1, L0_ffn_w2, L0_ffn_b2)[0]
    return x

_drawn_inputs = setup_inputs


def setup_inputs(seed=0):
    import zlib

    import numpy as np

    out = dict(_drawn_inputs(seed))
    spreads = {'L0_mix_bqkv': (0.0, 0.1),
     'L0_mix_bg': (0.0, 0.8),
     'L0_mix_bu': (0.0, 0.602),
     'L0_mix_bd': (0.0, 0.1),
     'L0_mix_g1': (1.0, 0.2),
     'L0_mix_b1': (0.0, 0.1),
     'L0_mix_g2': (1.0, 0.2),
     'L0_mix_b2': (0.0, 0.1),
     'L0_ffn_switch_b': (0.0, 0.1),
     'L0_ffn_b1': (0.0, 0.637),
     'L0_ffn_b2': (0.0, 0.432)}
    factors = {'L0_gnn_edge_type_weights': 64.0,
     'L0_gnn_wq': 4.938,
     'L0_gnn_bq': 8.0,
     'L0_gnn_wk': 6.374,
     'L0_gnn_bk': 64.0,
     'L0_gnn_bv': 7.212,
     'L0_gnn_wiq': 8.0,
     'L0_gnn_biq': 33.978,
     'L0_gnn_wik': 6.004,
     'L0_gnn_bik': 64.0,
     'L0_gnn_biv': 6.297,
     'L0_gnn_bo': 4.899,
     'L0_mix_Wqkv': 2.714}
    for name, (base, spread) in spreads.items():
        noise = np.random.default_rng([zlib.crc32(name.encode()), seed]).standard_normal(out[name].shape)
        drawn = base * np.exp(spread * noise) if base else spread * noise
        out[name] = jnp.asarray(drawn.astype(out[name].dtype))
    for name, factor in factors.items():
        out[name] = (out[name] * factor).astype(out[name].dtype)
    return out
```

```python
from contextlib import ExitStack, contextmanager

import concourse.bass as bass
from concourse import mybir

ALU = mybir.AluOpType
ACT = mybir.ActivationFunctionType
F32 = mybir.dt.float32
F32R = mybir.dt.float32r
I32 = mybir.dt.int32
AX_X = mybir.AxisListType.X

P = 128
N = 384
NT = N // P
D = 1024
KT = D // P
HEADS = 16
PAIRS = HEADS // 2
DH = D // HEADS
E_EDGES = 6144
EC = E_EDGES // P
GROUP = 3
PIECES = EC // GROUP
FH = 341
FHT = 3
EXPERTS = 8
F = 512
SLOTS = (N - EXPERTS) // P + EXPERTS
RING = 4
HALF = 512
NONE = -1.0e30
PASSES = ((0, 0), (0, 1), (1, 0))

B_MQ, B_MK, B_Q, B_K, B_V, B_IQ, B_IK, B_IV, B_G, B_U = 0, 8, 16, 24, 32, 40, 48, 56, 64, 67
NBIAS = 70
C_ID, C_TRI, C_ONE, C_W8, C_SLOT, C_EXP = 0, 128, 256, 384, 392, 392 + SLOTS * EXPERTS
C_SPARE = C_EXP + 1
NCONST = C_SPARE + EC

R_LOGIT, R_MAX, R_NMAX, R_EXP, R_SUM, R_PROB, R_HOT, R_FIRST, R_RANK, R_TOTAL, R_POS = range(11)

Q_MQ, Q_MK, Q_MV, Q_GQ, Q_GK, Q_GV, Q_GU = 0, 8, 16, 24, 32, 40, 48
Q_DOWN = Q_GU + 2 * FHT
Q_PAIR = Q_DOWN + 3
Q_WO = Q_PAIR + 3 * PAIRS
Q_MOE = Q_WO + 8
QE = 8


class Tally:

    def __init__(self, n=0):
        self.n, self.i, self.per = n, None, 0

    @property
    def value(self):
        return self.n if self.i is None else self.i * self.per + self.n

    def add(self, n=1):
        self.n += n
        return self.value


@contextmanager
def repeat(engine, times, per):
    first = {t: t.n for t in per}
    with engine.Fori(0, times) as i:
        for t, n in per.items():
            t.i, t.per = i, n
        yield i
    for t, n in per.items():
        assert t.n == first[t] + n, (t.n, first[t], n)
        t.n, t.i = first[t] + n * times, None


def slot_of(q):
    if q < Q_PAIR:
        return q % RING
    if q < Q_WO:
        return 1 + (q - Q_PAIR) % 3
    return (q - Q_WO) % RING


def graph_layer(nc, x, rowb, cols, consts, later, src_rows, dst_rows, src_cols, dst_cols, type_cols,
                type_weights, w_stream, w_experts, switch_w, b12, out):
    with ExitStack() as ctx:
        def sb(name, shape, dt=F32):
            return ctx.enter_context(nc.sbuf_tensor(name, shape, dt))

        def sem(name):
            return ctx.enter_context(nc.semaphore(name))

        raw = sb("raw", [P, RING, D])
        wsp = sb("wsp", [P, 2, RING, D], F32R)
        bigs = [sb(f"big{n}", [P, 2, KT * N], F32R) for n in range(4)]
        feat = [b[:].rearrange("p h (k n) -> p h k n", k=KT) for b in bigs]
        tokv = [b[:].rearrange("p h (t d) -> p h t d", t=NT) for b in bigs]
        tok = sb("tok", [P, NT, D])
        pt = sb("pt", [P, 2, NT, N], F32R)
        work = sb("work", [P, 2 * NT * N])
        maskb = sb("maskb", [P, NT, N])
        qp = sb("qp", [P, 2, N], F32R)
        kp = sb("kp", [P, 2, N], F32R)
        vp = sb("vp", [P, 2, NT, P], F32R)
        vt = sb("vt", [P, N])
        diag = sb("diag", [P, P])
        rowbuf = sb("rowbuf", [P, 2, D])
        bias = sb("bias", [P, NBIAS])
        cst = sb("cst", [P, NCONST])
        swt = sb("swt", [P, KT, EXPERTS])
        sbias = sb("sbias", [P, NT * EXPERTS])
        ones_r = sb("ones_r", [P, 2], F32R)
        slot_hot = sb("slot_hot", [P, P], F32R)
        ei = sb("ei", [P, 3, EC], I32)
        ef = sb("ef", [P, 6, EC])
        eidx = sb("eidx", [P, EC], I32)
        tw = sb("tw", [P, 4, 4])
        dup = sb("dup", [P, EC])
        stats = sb("stats", [P, NT, 2, 6])
        mv = sb("mv", [P, NT, 2])
        rs = sb("rs", [P, NT, 2])
        half = sb("half", [P, 1])
        waited = sb("waited", [P, 1])
        den = sb("den", [P, 2 * NT])
        smx = sb("smx", [P, 2, NT])
        snm = sb("snm", [P, 2, NT])
        ssum = sb("ssum", [P, 2, NT])
        sinv = sb("sinv", [P, 2, NT])
        rt = sb("rt", [P, 11, NT * EXPERTS])
        cum = sb("cum", [P, 4, 12])
        slotc = sb("slotc", [P, SLOTS, EXPERTS])
        slote = sb("slote", [P, 3, SLOTS])
        posi = sb("posi", [P, NT], I32)
        rowi = sb("rowi", [P, SLOTS], I32)

        ident = cst[:, C_ID:C_ID + P]
        tri = cst[:, C_TRI:C_TRI + P]
        ones = cst[:, C_ONE:C_ONE + P]
        maskflat = maskb[:].rearrange("p t n -> p (t n)")
        probs = work[:].rearrange("p (s t n) -> p s t n", s=2, t=NT)
        edge_rows = [rowbuf[:].rearrange("p a b -> p (a b)")[:, 768 * n:768 * (n + 1)].bitcast(I32)
                     .rearrange("p (a b) -> p a b", a=2) for n in range(2)]
        codes = work[:, 0:N]
        junk = [work[:, N * (n + 1):N * (n + 2)] for n in range(GROUP)]
        elu_s, elu_e, elu_r = work[:, 4 * N:5 * N], work[:, 5 * N:6 * N], vt[:]
        gate, hid = work[:, 0:N], work[:, N:2 * N]
        x2t = work[:, D:2 * D]
        h_buf, y_buf = maskflat[:, 0:F], work[:, 0:D]
        spare = cst[:, C_SPARE:C_SPARE + EC]

        ps = ctx.enter_context(nc.psum_tensor("ps", [P, 8, HALF], F32))

        table = nc.dram_tensor("edge_table", [N * N + P * EC, 1], F32).ap()
        xs_dram = nc.dram_tensor("slot_x", [SLOTS * P, D], F32).ap()
        ys_dram = nc.dram_tensor("slot_y", [SLOTS * P, D], F32).ap()

        x_in = [sem(f"x_in{t}") for t in range(NT)]
        const_in, edge_in, rowb_in, b_row_in = sem("const_in"), sem("edge_in"), sem("rowb_in"), sem("b_row_in")
        piece_in = [sem(f"piece_in{n}") for n in range(2)]
        piece_done = sem("piece_done")
        raw_in = [sem(f"raw_in{n}") for n in range(RING)]
        w_hi, w_lo = sem("w_hi"), sem("w_lo")
        w_started = sem("w_started")
        acc_ready, acc_hi, acc_free = sem("acc_ready"), sem("acc_hi"), sem("acc_free")
        elu_parts, elu_hi = sem("elu_parts"), sem("elu_hi")
        elu_lo = sem("elu_lo")
        tr_ready, tr_hi, tr_free = sem("tr_ready"), sem("tr_hi"), sem("tr_free")
        tm_ready, tm_sum, tm_hi, tm_lo = sem("tm_ready"), sem("tm_sum"), sem("tm_hi"), sem("tm_lo")
        dve_step, act_step, pool_step = sem("dve_step"), sem("act_step"), sem("pool_step")
        ones_set = sem("ones_set")
        stats_done, rstd_done, xn_done = sem("stats_done"), sem("rstd_done"), sem("xn_done")
        num_ready, num_free = sem("num_ready"), sem("num_free")
        x1_done, bd_added = sem("x1_done"), sem("bd_added")
        hid_hi, hid_lo = sem("hid_hi"), sem("hid_lo")
        down_ready, down_sum, mix_done = sem("down_ready"), sem("down_sum"), sem("mix_done")
        s_ready, s_max, s_exp, s_norm = sem("s_ready"), sem("s_max"), sem("s_exp"), sem("s_norm")
        pt_ready, pt_hi, pt_lo = sem("pt_ready"), sem("pt_hi"), sem("pt_lo")
        v_sum = sem("v_sum")
        tw_arg, tw_exp, tw_one, tw_ln, tw_done = (sem("tw_arg"), sem("tw_exp"), sem("tw_one"), sem("tw_ln"),
                                                  sem("tw_done"))
        edges_done = sem("edges_done")
        table_out, later_in, scattered, mask_in = (sem("table_out"), sem("later_in"), sem("scattered"),
                                                   sem("mask_in"))
        zero_out = sem("zero_out")
        b12_in, b12_hi, b12_lo = sem("b12_in"), sem("b12_hi"), sem("b12_lo")
        wo_ready, wo_sum = sem("wo_ready"), sem("wo_sum")
        x2_done, x2t_ready, x2t_copied, logits_ready = (
            sem("x2_done"), sem("x2t_ready"), sem("x2t_copied"), sem("logits_ready"))
        lmax_done, lexp_done, hot_done, count_ready, route_done, pos_done = (
            sem("lmax_done"), sem("lexp_done"), sem("hot_done"), sem("count_ready"), sem("route_done"),
            sem("pos_done"))
        xs_out, hott_ready, hott_copied, b2_ready, b2_added = (
            sem("xs_out"), sem("hott_ready"), sem("hott_copied"), sem("b2_ready"), sem("b2_added"))
        slot_set, xs_in = sem("slot_set"), sem("xs_in")
        h_ready, h_act, ht_ready, ht_hi, ht_lo = (sem("h_ready"), sem("h_act"), sem("ht_ready"),
                                                  sem("ht_hi"), sem("ht_lo"))
        y_ready, y_half0, y_half1, y_out = sem("y_ready"), sem("y_half0"), sem("y_half1"), sem("y_out")
        yg_in = [sem(f"yg_in{t}") for t in range(NT)]
        sum_done, out_done = sem("sum_done"), sem("out_done")

        block = ctx.enter_context(nc.Block())

        def set_banks(t):
            return ps[:, 2 + 2 * t:4 + 2 * t, :].rearrange("p a (b c) -> p (a b) c", c=P)

        def whole(a):
            return ps[:, a:a + 2, :].rearrange("p a b -> p (a b)")

        @block.sync
        def _(sp):
            for t in range(NT):
                sp.dma_start(tok[:, t, :], x[t * P:(t + 1) * P, :]).then_inc(x_in[t], 16)
            sp.dma_start(cst[:], consts).then_inc(const_in, 16)
            sp.dma_start(bias[:], cols).then_inc(const_in, 16)

            def load(row, slot, split):
                if split is not None:
                    sp.wait_ge(w_lo, split)
                sp.dma_start(raw[:, slot, :], w_stream[bass.ds(row, P), :]).then_inc(raw_in[slot], 16)

            def load_piece(first, buf, read):
                for k, r in enumerate((src_rows, dst_rows)):
                    if read is not None:
                        sp.wait_ge(piece_done, read)
                    sp.dma_start(edge_rows[buf][:, k, :],
                                 r[bass.ds(first, N)].partition_broadcast(P)).then_inc(piece_in[buf], 16)

            for q in range(RING):
                load(q * P, q, None)
            for j in range(2):
                load_piece(j * N, j, None)
            with sp.Fori(0, (Q_MV - RING) // RING) as i:
                for j in range(RING):
                    row = sp.snap(i * (RING * P) + (RING + j) * P)
                    first = sp.snap(i * (RING * N) + (2 + j) * N)
                    load(row, j, i * RING + (j + 1))
                    load_piece(first, j % 2, i * RING + (j + 1))
            for n in range(2 + Q_MV - RING, PIECES):
                load_piece(n * N, n % 2, n - 1)
            with sp.Fori(0, (Q_GU - Q_MV) // RING) as i:
                for j in range(RING):
                    row = sp.snap(i * (RING * P) + (Q_MV + j) * P)
                    load(row, j, i * RING + (Q_MV + j - RING + 1))
            for q in range(Q_GU, Q_PAIR):
                load(q * P, slot_of(q), q - RING + 1)
            with sp.Fori(0, PAIRS) as i:
                for j in range(3):
                    row = sp.snap(i * (3 * P) + (Q_PAIR + j) * P)
                    load(row, 1 + j, i * 3 + (Q_PAIR + j - 2))
            for q in range(Q_WO, Q_MOE):
                load(q * P, slot_of(q), q - RING + 1)

            def expert_rows(s, first):
                r = sp.value_load(rowi[0:1, bass.ds(s, 1)], min_val=0, max_val=(EXPERTS - 1) * QE * P)
                return [sp.snap(r + (first + j) * P) for j in range(4)]

            def load_expert(row, j, split):
                sp.wait_ge(w_lo, split)
                sp.dma_start(raw[:, j, :], w_experts[bass.ds(row, P), :]).then_inc(raw_in[j], 16)

            sp.wait_ge(route_done, 1)
            for j, row in enumerate(expert_rows(0, 0)):
                load_expert(row, j, Q_MOE - RING + 1 + j)
            with sp.Fori(0, SLOTS - 1) as i:
                rows = expert_rows(i + 1, 0) + expert_rows(i, 4)
                for j, row in enumerate(rows):
                    load_expert(row, j % RING, i * QE + (Q_MOE + 1 + j))
            for j, row in enumerate(expert_rows(SLOTS - 1, 4)):
                load_expert(row, j, Q_MOE + QE * (SLOTS - 1) + 1 + j)

            for t in range(NT):
                sp.wait_ge(sum_done, t + 1)
                sp.dma_start(out[t * P:(t + 1) * P, :], tok[:, t, :]).then_inc(out_done, 16)
            sp.wait_ge(out_done, 16 * NT)

        @block.gpsimd
        def _(pool):
            step, rows_in = Tally(), Tally()
            R_BV, R_G1, R_B1, R_BD, R_G2, R_B2, R_BO, R_SW = range(8)

            def then(ins):
                ins.then_inc(pool_step, 1)
                pool.wait_ge(pool_step, step.add())

            def load_row(k, buf):
                pool.dma_start(rowbuf[:, buf, :], rowb[k].partition_broadcast(P)).then_inc(rowb_in, 16)
                rows_in.add(16)

            for k, r in enumerate((src_cols, dst_cols, type_cols)):
                pool.dma_start(ei[:, k, :], r).then_inc(edge_in, 16)
            pool.dma_start(tw[:, 0, :], type_weights.partition_broadcast(P)).then_inc(edge_in, 16)
            pool.dma_start(sbias[:], rowb[R_SW, 0:NT * EXPERTS].partition_broadcast(P)).then_inc(edge_in, 16)
            pool.dma_start(swt[:], switch_w).then_inc(edge_in, 16)
            then(nc.gpsimd.memset(half[:], -0.5))

            def rstd(t, n):
                pool.wait_ge(stats_done, n + 1)
                then(nc.gpsimd.tensor_scalar(rs[:, t, 0:1], mv[:, t, 1:2], 1e-5, None, ALU.add))
                nc.gpsimd.tensor_tensor(rs[:, t, 1:2], rs[:, t, 0:1], half[:], ALU.pow).then_inc(rstd_done, 1)

            for t in range(NT):
                rstd(t, t)

            then(nc.gpsimd.memset(maskb[:], NONE))
            for t in range(NT):
                then(nc.gpsimd.affine_select(out=maskb[:, t, :], in_=maskb[:, t, :], compare_op=ALU.not_equal,
                                             fill=0.0, base=t * P, pattern=[[-1, N]], channel_multiplier=1))
            pool.wait_ge(const_in, 32)
            pool.wait_ge(tw_done, 1)
            then(nc.gpsimd.tensor_scalar(diag[:], ident, tw[:, 3, 3:4], None, ALU.mult))
            for t in range(NT):
                blk = maskb[:, t, t * P:(t + 1) * P]
                then(nc.gpsimd.tensor_tensor(blk, blk, diag[:], ALU.add))
            pool.dma_start(table[0:N * N, :].rearrange("(t p n) o -> p t (n o)", t=NT, p=P),
                           maskb[:]).then_inc(table_out, 16)
            pool.wait_ge(table_out, 16)
            pool.dma_start(maskb[:], later).then_inc(later_in, 16)

            pool.wait_ge(edges_done, 1)
            for g in range(PIECES):
                for k in range(GROUP):
                    c = g * GROUP + k
                    pool.indirect_dma_start(
                        out=table, out_offset=bass.IndirectOffsetOnAxis(ap=eidx[:, c:c + 1], axis=0),
                        in_=ef[:, 3, c:c + 1], in_offset=None).then_inc(scattered, 16)
                pool.wait_ge(scattered, 16 * GROUP * (g + 1))
            pool.dma_start(maskb[:], table[0:N * N, :].rearrange("(t p n) o -> p t (n o)", t=NT, p=P))\
                .then_inc(mask_in, 16)

            pool.wait_ge(tm_sum, 2 * NT)
            load_row(R_G1, 0)
            load_row(R_B1, 1)
            pool.wait_ge(rowb_in, rows_in.value)
            for t in range(NT):
                rstd(t, NT + t)
                pool.wait_ge(rstd_done, NT + t + 1)
                row = tok[:, t, :]
                then(nc.gpsimd.tensor_scalar(row, row, mv[:, t, 0:1], rs[:, t, 1:2], ALU.subtract, ALU.mult))
                then(nc.gpsimd.tensor_tensor(row, row, rowbuf[:, 0, :], ALU.mult))
                nc.gpsimd.tensor_tensor(row, row, rowbuf[:, 1, :], ALU.add).then_inc(x1_done, 1)
            pool.wait_ge(x1_done, NT)
            load_row(R_BD, 0)
            pool.wait_ge(rowb_in, rows_in.value)
            for t in range(NT):
                pool.wait_ge(tr_ready, NT + t + 1)
                nc.gpsimd.tensor_tensor(tok[:, t, :], tok[:, t, :], rowbuf[:, 0, :], ALU.add)\
                    .then_inc(bd_added, 1)
            pool.wait_ge(bd_added, NT)
            then(nc.gpsimd.memset(rowbuf[:, 0, :], 0.0))
            for s in range(SLOTS):
                pool.dma_start(xs_dram[s * P:(s + 1) * P, :], rowbuf[:, 0, :]).then_inc(zero_out, 16)
            pool.wait_ge(zero_out, 16 * SLOTS)
            load_row(R_G2, 0)
            load_row(R_B2, 1)
            pool.wait_ge(rowb_in, rows_in.value)
            for t in range(NT):
                rstd(t, 2 * NT + t)
                pool.wait_ge(rstd_done, 2 * NT + t + 1)
                row = tok[:, t, :]
                then(nc.gpsimd.tensor_scalar(row, row, mv[:, t, 0:1], rs[:, t, 1:2], ALU.subtract, ALU.mult))
                then(nc.gpsimd.tensor_tensor(row, row, rowbuf[:, 0, :], ALU.mult))
                then(nc.gpsimd.tensor_tensor(row, row, rowbuf[:, 1, :], ALU.add))
            load_row(R_BO, 0)
            for t in range(NT):
                row = tok[:, t, :]
                pool.dma_start(rowbuf[:, 1, :], x[t * P:(t + 1) * P, :]).then_inc(rowb_in, 16)
                rows_in.add(16)
                pool.wait_ge(rowb_in, rows_in.value)
                then(nc.gpsimd.tensor_tensor(row, row, rowbuf[:, 0, :], ALU.add))
                nc.gpsimd.tensor_tensor(row, row, rowbuf[:, 1, :], ALU.add).then_inc(mix_done, 1)
                pool.wait_ge(mix_done, t + 1)

            pool.wait_ge(pt_ready, HEADS)
            pool.dma_start(work[0:EXPERTS, 0:F + D], b12).then_inc(b12_in, 16)

            for t in range(NT):
                rstd(t, 3 * NT + t)
            pool.wait_ge(zero_out, 16 * SLOTS)
            pool.wait_ge(pos_done, 1)
            for t in range(NT):
                pool.wait_ge(x2_done, t + 1)
                src = rowbuf[:, t, :] if t < 2 else work[:, 0:D]
                pool.indirect_dma_start(
                    out=xs_dram, out_offset=bass.IndirectOffsetOnAxis(ap=posi[:, t:t + 1], axis=0),
                    in_=src, in_offset=None).then_inc(xs_out, 16)
            pool.wait_ge(y_out, 16 * SLOTS)
            for t in range(NT):
                dst = rowbuf[:, t, :] if t < 2 else work[:, 0:D]
                pool.indirect_dma_start(
                    out=dst, out_offset=None, in_=ys_dram,
                    in_offset=bass.IndirectOffsetOnAxis(ap=posi[:, t:t + 1], axis=0)).then_inc(yg_in[t], 16)

        @block.scalar
        def _(act):
            q_no = Tally()
            used = [Tally() for _ in range(RING)]
            acc = Tally()
            everyone = slice(0, P)

            def prep(slot):
                act.wait_ge(raw_in[slot], used[slot].add(16))
                if q_no.i is not None or q_no.n >= RING:
                    act.wait_ge(w_started, q_no.value - 1)
                nc.scalar.activation(wsp[:, 0, slot, :], raw[:, slot, :], ACT.Copy).then_inc(w_hi, 1)
                q_no.add()

            def acc_part(dst, rows, b):
                bank = acc.n % 2
                act.wait_ge(acc_ready, acc.add())
                nc.scalar.activation(dst, ps[rows, bank, 0:N], ACT.Identity, bias=b).then_inc(acc_hi, 1)

            turn = {q_no: RING, acc: RING, **{u: 16 for u in used}}

            act.wait_ge(tw_arg, 1)
            nc.scalar.activation(tw[:, 1, :], tw[:, 1, :], ACT.Exp).then_inc(tw_exp, 1)
            act.wait_ge(tw_one, 1)
            nc.scalar.activation(tw[:, 1, :], tw[:, 1, :], ACT.Ln).then_inc(tw_ln, 1)

            prep(0)
            prep(1)
            for t in range(NT):
                act.wait_ge(tr_ready, t + 1)
                nc.scalar.activation(feat[0][:, 0, :, t * P:(t + 1) * P], set_banks(t), ACT.Copy).then_inc(tr_hi, 1)
            act.wait_ge(const_in, 32)

            def elu_step(m, j):
                bank = acc.n % 2
                if acc.i is not None or acc.n:
                    act.wait_ge(acc_free, acc.value)
                act.wait_ge(acc_ready, acc.add())
                b = bias[:, bass.ds(m + B_MQ, 1)]
                nc.scalar.activation(elu_e, ps[:, bank, 0:N], ACT.Exp, bias=b).then_inc(elu_parts, 1)
                nc.scalar.activation(elu_r, ps[:, bank, 0:N], ACT.Relu, bias=b).then_inc(elu_parts, 1)
                prep((j + 2) % RING)
                act.wait_ge(acc_free, acc.value)
                return acc.n

            def elu_hi_part(big, m):
                nc.scalar.activation(feat[big][:, 0, bass.ds(m, 1), :], elu_s, ACT.Copy).then_inc(elu_hi, 1)

            for j in range(RING):
                elu_step(j, j)
                elu_hi_part(1, j)
            with repeat(act, 1, turn) as i:
                for j in range(RING):
                    elu_step(i * RING + (RING + j), j)
                    elu_hi_part(1, i * RING + (RING + j))
            with repeat(act, 2, turn) as i:
                for j in range(RING):
                    elu_step(i * RING + (2 * RING + j), j)
                    elu_hi_part(2, i * RING + j)

            act.wait_ge(piece_done, PIECES)
            act.dma_start(rowbuf[:, 1, :], rowb[0].partition_broadcast(P)).then_inc(b_row_in, 16)
            for h in range(2):
                for j in range(RING):
                    prep((j + 2) % RING)
                for t in range(NT):
                    act.wait_ge(tm_sum, h * NT + t + 1)
                    nc.scalar.activation(tokv[3][:, 0, t, h * HALF:(h + 1) * HALF],
                                         work[:, t * HALF:(t + 1) * HALF], ACT.Copy).then_inc(tm_hi, 1)

            for mt in range(NT):
                acc_part(pt[:, 0, mt, :], everyone, 0.0)

            for n, b0 in enumerate((B_Q, B_K, B_V)):
                with repeat(act, 2, turn) as i:
                    for j in range(RING):
                        m = i * RING + j
                        acc_part(feat[1 + n][:, 0, bass.ds(m, 1), :], everyone, bias[:, bass.ds(m + b0, 1)])
                        prep((j + 2) % RING)

            for t in range(NT):
                act.wait_ge(tr_ready, NT + t + 1)
                nc.scalar.activation(feat[0][:, 0, :, t * P:(t + 1) * P], set_banks(t), ACT.Copy).then_inc(tr_hi, 1)

            for m in range(FHT):
                bank = acc.n % 2
                act.wait_ge(acc_free, acc.value)
                act.wait_ge(acc_ready, acc.add())
                nc.scalar.activation(gate, ps[:, bank, 0:N], ACT.Silu, bias=bias[:, B_G + m:B_G + m + 1])\
                    .then_inc(acc_free, 1)
                prep(slot_of(q_no.n))
                act.wait_ge(acc_free, acc.add())
                nc.scalar.activation(pt[:, 0, m, :], hid, ACT.Copy).then_inc(hid_hi, 1)
                prep(slot_of(q_no.n))
            prep(slot_of(q_no.n))
            prep(slot_of(q_no.n))
            act.wait_ge(down_ready, NT)
            prep(slot_of(q_no.n))

            exp_no, pt_no = Tally(), Tally()

            def exps(s):
                act.wait_ge(s_max, exp_no.add())
                for t in range(NT):
                    nc.scalar.activation(probs[:, s, t, :], probs[:, s, t, :], ACT.Exp,
                                         bias=snm[:, s, t:t + 1], scale=DH ** -0.5,
                                         accum_out=ssum[:, s, t:t + 1]).then_inc(s_exp, 1)

            def pt_part(s):
                act.wait_ge(pt_ready, pt_no.add())
                nc.scalar.activation(pt[:, 0, :, :], ps[:, 2 + 3 * s:5 + 3 * s, 0:N], ACT.Copy).then_inc(pt_hi, 1)

            def head_rows(s):
                return slice(s * DH, (s + 1) * DH)

            def pair(p, first, last):
                if not first:
                    exps(0)
                    exps(1)
                acc_part(qp[:, 0, :], everyone, bias[:, bass.ds(p + B_IQ, 1)])
                prep(3)
                if not first:
                    pt_part(0)
                acc_part(kp[:, 0, :], everyone, bias[:, bass.ds(p + B_IK, 1)])
                prep(0 if last else 1)
                if not first:
                    acc_part(feat[0][head_rows(0), 0, bass.ds(p - 1, 1), :], head_rows(0), 0.0)
                    pt_part(1)
                acc.add()
                prep(1 if last else 2)
                if not first:
                    acc_part(feat[0][head_rows(1), 0, bass.ds(p - 1, 1), :], head_rows(1), 0.0)
                bank = acc.n % 2
                act.wait_ge(acc_ready, acc.add())
                nc.scalar.activation(vp[:, 0, :, :], ps[:, bank, 0:N].rearrange("p (t d) -> p t d", t=NT),
                                     ACT.Copy).then_inc(acc_hi, 1)

            pair(0, True, False)
            with repeat(act, PAIRS - 2, {q_no: 3, acc: 6, exp_no: 2, pt_no: 2,
                                         used[1]: 16, used[2]: 16, used[3]: 16}) as i:
                pair(i + 1, False, False)
            pair(PAIRS - 1, False, True)
            exps(0)
            exps(1)
            for s in range(2):
                pt_part(s)
                acc_part(feat[0][head_rows(s), 0, PAIRS - 1, :], head_rows(s), 0.0)

            for q in range(Q_WO + 2, Q_MOE):
                prep(slot_of(q))
            act.wait_ge(b12_in, 16)
            nc.scalar.activation(bigs[3][0:EXPERTS, 0, 0:F + D], work[0:EXPERTS, 0:F + D], ACT.Copy)\
                .then_inc(b12_hi, 1)

            for t in range(NT):
                act.wait_ge(x2t_ready, t + 1)
                if t:
                    act.wait_ge(logits_ready, t)
                nc.scalar.activation(x2t, whole(2), ACT.Copy).then_inc(x2t_copied, 1)
            act.wait_ge(lmax_done, 1)
            for t in range(NT):
                sl = slice(t * EXPERTS, (t + 1) * EXPERTS)
                nc.scalar.activation(rt[:, R_EXP, sl], rt[:, R_LOGIT, sl], ACT.Exp,
                                     bias=rt[:, R_NMAX, t:t + 1], accum_out=rt[:, R_SUM, t:t + 1])\
                    .then_inc(lexp_done, 1)
            act.wait_ge(hott_ready, 1)
            nc.scalar.activation(pt[0:EXPERTS, 0, 0, :], ps[0:EXPERTS, 1, 0:N], ACT.Copy).then_inc(hott_copied, 1)

            xt, h_no, y_no, ht = Tally(2 * NT), Tally(), Tally(), Tally()
            act.wait_ge(xs_out, 16 * NT)
            act.dma_start(rowbuf[:, 0, :], xs_dram[0:P, :]).then_inc(xs_in, 16)

            def split_slot():
                act.wait_ge(tr_ready, xt.add())
                nc.scalar.activation(bigs[1][:, 0, 0:D], whole(2), ACT.Copy).then_inc(tr_hi, 1)

            def prep_x(slot):
                act.wait_ge(raw_in[slot], used[slot].add(16))
                act.wait_ge(w_started, q_no.value - 2)
                nc.scalar.activation(wsp[:, 0, slot, :], raw[:, slot, :], ACT.Copy).then_inc(w_hi, 1)
                q_no.add()

            def gelu():
                act.wait_ge(h_ready, h_no.add())
                nc.scalar.activation(h_buf, ps[:, 0, :], ACT.Gelu_apprx_tanh).then_inc(h_act, 1)

            def split_hidden():
                act.wait_ge(ht_ready, ht.add())
                nc.scalar.activation(bigs[2][:, 0, 0:F], ps[:, 1, :], ACT.Copy).then_inc(ht_hi, 1)

            def first_half_of_y(i):
                act.wait_ge(y_ready, y_no.add())
                if not isinstance(i, int) or i:
                    act.wait_ge(y_out, i * 16)
                nc.scalar.activation(y_buf[:, 0:HALF], ps[:, 4, :], ACT.Copy).then_inc(y_half0, 1)

            def store_y(i):
                row = i * P if isinstance(i, int) else act.snap(i * P)
                act.wait_ge(y_half0, y_no.value)
                act.wait_ge(y_half1, y_no.value)
                act.dma_start(ys_dram[bass.ds(row, P), :], y_buf).then_inc(y_out, 16)

            prep_x(0)
            prep_x(1)
            split_slot()
            act.dma_start(rowbuf[:, 0, :], xs_dram[P:2 * P, :]).then_inc(xs_in, 16)
            for j in (2, 3, 0, 1):
                prep_x(j)
            gelu()
            split_slot()
            split_hidden()

            def slot_turn(i, last):
                if not last:
                    row = i * P + 2 * P if isinstance(i, int) else act.snap(i * P + 2 * P)
                    act.dma_start(rowbuf[:, 0, :], xs_dram[bass.ds(row, P), :]).then_inc(xs_in, 16)
                for j in (2, 3, 0, 1):
                    prep_x(j)
                gelu()
                if not last:
                    split_slot()
                for j in (2, 3, 0, 1):
                    prep_x(j)
                first_half_of_y(i)
                split_hidden()
                store_y(i)

            slot_turn(0, False)
            with repeat(act, SLOTS - 3, {q_no: QE, xt: 1, h_no: 1, y_no: 1, ht: 1,
                                         **{u: 32 for u in used}}) as i:
                slot_turn(i + 1, False)
            slot_turn(SLOTS - 2, True)
            prep_x(2)
            prep_x(3)
            first_half_of_y(SLOTS - 1)
            store_y(SLOTS - 1)

        @block.vector
        def _(dve):
            q_no, step = Tally(), Tally()
            acc, hi_no = Tally(), Tally()
            everyone = slice(0, P)

            def then(ins):
                ins.then_inc(dve_step, 1)
                dve.wait_ge(dve_step, step.add())

            def lo(dst, value, hi):
                return nc.vector.tensor_tensor(dst, value, hi.bitcast(F32), ALU.subtract)

            def prep(slot):
                dve.wait_ge(w_hi, q_no.add())
                lo(wsp[:, 1, slot, :], raw[:, slot, :], wsp[:, 0, slot, :]).then_inc(w_lo, 1)

            def acc_part(dst, hi, rows, b):
                bank = acc.n % 2
                acc.add()
                dve.wait_ge(acc_hi, hi_no.add())
                nc.vector.scalar_tensor_tensor(out=dst, in0=ps[rows, bank, 0:N], scalar=b, in1=hi.bitcast(F32),
                                               op0=ALU.add, op1=ALU.subtract).then_inc(acc_free, 1)

            def statistics(t):
                for c in range(2):
                    ins = nc.vector.bn_stats(stats[:, t, c, :], tok[:, t, c * HALF:(c + 1) * HALF])
                then(ins)
                nc.vector.bn_aggr(mv[:, t, :], stats[:, t, :, :].rearrange("p a b -> p (a b)"))\
                    .then_inc(stats_done, 1)

            turn = {q_no: RING, acc: RING, hi_no: RING}

            nc.vector.memset(ones_r[:].bitcast(F32), 1.0).then_inc(ones_set, 1)
            for t in range(NT):
                dve.wait_ge(x_in[t], 16)
                statistics(t)
            for t in range(NT):
                dve.wait_ge(rstd_done, t + 1)
                nc.vector.tensor_scalar(tok[:, t, :], tok[:, t, :], mv[:, t, 0:1], rs[:, t, 1:2],
                                        ALU.subtract, ALU.mult).then_inc(xn_done, 1)

            dve.wait_ge(edge_in, 96)
            then(nc.vector.tensor_scalar(tw[:, 2, :], tw[:, 0, :], -1.0, None, ALU.mult))
            nc.vector.tensor_tensor(tw[:, 1, :], tw[:, 0, :], tw[:, 2, :], ALU.min).then_inc(tw_arg, 1)
            dve.wait_ge(tw_exp, 1)
            nc.vector.tensor_scalar(tw[:, 1, :], tw[:, 1, :], 1.0, None, ALU.add).then_inc(tw_one, 1)
            dve.wait_ge(tw_ln, 1)
            then(nc.vector.scalar_tensor_tensor(out=tw[:, 2, :], in0=tw[:, 0, :], scalar=0.0, in1=tw[:, 1, :],
                                                op0=ALU.max, op1=ALU.add))
            nc.vector.tensor_scalar(tw[:, 3, :], tw[:, 2, :], DH ** 0.5, None, ALU.mult).then_inc(tw_done, 1)
            dve.wait_ge(tw_done, 1)
            then(nc.vector.scalar_tensor_tensor(out=ef[:, 0, :], in0=ei[:, 0, :], scalar=float(N), in1=ei[:, 1, :],
                                                op0=ALU.mult, op1=ALU.add))
            for k, w in ((0, 3), (1, 0), (2, 1), (3, 2), (4, 3)):
                dst = ef[:, 3, :] if k == 0 else ef[:, 1, :]
                then(nc.vector.tensor_scalar(dst, ei[:, 2, :], float(k), tw[:, 3, w:w + 1], ALU.is_equal, ALU.mult))
                if k:
                    then(nc.vector.tensor_tensor(ef[:, 3, :], ef[:, 3, :], ef[:, 1, :], ALU.add))

            prep(0)
            prep(1)
            for t in range(NT):
                dve.wait_ge(tr_hi, t + 1)
                hi = feat[0][:, 0, :, t * P:(t + 1) * P]
                lo(feat[0][:, 1, :, t * P:(t + 1) * P], set_banks(t), hi).then_inc(tr_free, 1)

            parts, elus, pieces = Tally(), Tally(), Tally()
            piece_no = [Tally(), Tally()]

            def elu_step(big, m, j, c):
                acc.add()
                dve.wait_ge(elu_parts, parts.add(2))
                if elus.i is not None or elus.n:
                    dve.wait_ge(elu_lo, elus.value)
                nc.vector.scalar_tensor_tensor(out=elu_s, in0=elu_e, scalar=1.0, in1=elu_r,
                                               op0=ALU.min, op1=ALU.add).then_inc(acc_free, 1)
                prep((j + 2) % RING)
                dve.wait_ge(elu_hi, elus.add())
                lo(feat[big][:, 1, bass.ds(m, 1), :], elu_s, feat[big][:, 0, bass.ds(m, 1), :]).then_inc(elu_lo, 1)
                buf = j % 2
                dve.wait_ge(piece_in[buf], piece_no[buf].add(32))
                then(nc.vector.scalar_tensor_tensor(out=codes, in0=edge_rows[buf][:, 0, :], scalar=float(N),
                                                    in1=edge_rows[buf][:, 1, :], op0=ALU.mult, op1=ALU.add))
                for k in range(GROUP):
                    ins = nc.vector.scalar_tensor_tensor(
                        out=junk[k][:, k * P:N], in0=codes[:, k * P:N], scalar=ef[:, 0, bass.ds(c + k, 1)],
                        in1=maskb[:, k, k * P:N], op0=ALU.is_equal, op1=ALU.mult,
                        accum_out=dup[:, bass.ds(c + k, 1)])
                ins.then_inc(piece_done, 1)
                dve.wait_ge(piece_done, pieces.add())

            dve.wait_ge(later_in, 16)
            elu_turn = {q_no: RING, acc: RING, parts: 2 * RING, elus: RING, pieces: RING, step: RING,
                        piece_no[0]: 64, piece_no[1]: 64}
            for j in range(RING):
                elu_step(1, j, j, j * GROUP)
            with repeat(dve, 1, elu_turn) as i:
                for j in range(RING):
                    elu_step(1, i * RING + (RING + j), j, i * (RING * GROUP) + (RING + j) * GROUP)
            with repeat(dve, 2, elu_turn) as i:
                for j in range(RING):
                    elu_step(2, i * RING + j, j, i * (RING * GROUP) + (2 * RING + j) * GROUP)

            then(nc.vector.tensor_scalar(ef[:, 1, :], dup[:], 0.0, None, ALU.is_gt))
            then(nc.vector.tensor_scalar(ef[:, 2, :], spare, 1.0, None, ALU.mult))
            then(nc.vector.tensor_tensor(ef[:, 2, :], ef[:, 2, :], ef[:, 0, :], ALU.subtract))
            then(nc.vector.tensor_tensor(ef[:, 2, :], ef[:, 2, :], ef[:, 1, :], ALU.mult))
            nc.vector.tensor_tensor(eidx[:], ef[:, 2, :], ef[:, 0, :], ALU.add).then_inc(edges_done, 1)

            for h in range(2):
                for j in range(RING):
                    prep((j + 2) % RING)
                if h == 0:
                    dve.wait_ge(b_row_in, 16)
                else:
                    dve.wait_ge(tm_lo, NT)
                for t in range(NT):
                    dve.wait_ge(tm_ready, h * NT + t + 1)
                    nc.vector.tensor_tensor(work[:, t * HALF:(t + 1) * HALF], ps[:, 2 + 3 * h + t, :],
                                            rowbuf[:, 1, h * HALF:(h + 1) * HALF], ALU.add).then_inc(tm_sum, 1)
                for t in range(NT):
                    dve.wait_ge(tm_hi, h * NT + t + 1)
                    cols_h = slice(h * HALF, (h + 1) * HALF)
                    lo(tokv[3][:, 1, t, cols_h], work[:, t * HALF:(t + 1) * HALF], tokv[3][:, 0, t, cols_h])\
                        .then_inc(tm_lo, 1)

            for mt in range(NT):
                acc_part(pt[:, 1, mt, :], pt[:, 0, mt, :], everyone, 0.0)

            for t in range(NT):
                b = 2 + 3 * (t % 2)
                dve.wait_ge(num_ready, t + 1)
                then(nc.vector.tensor_scalar(den[:, 2 * t:2 * t + 1], ps[:, b + 2, 0:1], 1e-6, None, ALU.add))
                then(nc.vector.reciprocal(den[:, 2 * t + 1:2 * t + 2], den[:, 2 * t:2 * t + 1]))
                nc.vector.scalar_tensor_tensor(out=tok[:, t, :], in0=whole(b), scalar=den[:, 2 * t + 1:2 * t + 2],
                                               in1=tok[:, t, :], op0=ALU.mult, op1=ALU.add).then_inc(num_free, 1)
                dve.wait_ge(num_free, t + 1)
                statistics(t)

            for n, b0 in enumerate((B_Q, B_K, B_V)):
                with repeat(dve, 2, turn) as i:
                    for j in range(RING):
                        m = i * RING + j
                        acc_part(feat[1 + n][:, 1, bass.ds(m, 1), :], feat[1 + n][:, 0, bass.ds(m, 1), :],
                                 everyone, bias[:, bass.ds(m + b0, 1)])
                        prep((j + 2) % RING)

            for t in range(NT):
                dve.wait_ge(tr_hi, NT + t + 1)
                hi = feat[0][:, 0, :, t * P:(t + 1) * P]
                lo(feat[0][:, 1, :, t * P:(t + 1) * P], set_banks(t), hi).then_inc(tr_free, 1)

            for m in range(FHT):
                prep(slot_of(q_no.n))
                acc.add()
                bank = acc.n % 2
                dve.wait_ge(acc_free, acc.value)
                if m:
                    dve.wait_ge(hid_lo, m)
                dve.wait_ge(acc_ready, acc.add())
                nc.vector.scalar_tensor_tensor(out=hid, in0=ps[:, bank, 0:N], scalar=bias[:, B_U + m:B_U + m + 1],
                                               in1=gate, op0=ALU.add, op1=ALU.mult).then_inc(acc_free, 1)
                prep(slot_of(q_no.n))
                dve.wait_ge(hid_hi, m + 1)
                lo(pt[:, 1, m, :], hid, pt[:, 0, m, :]).then_inc(hid_lo, 1)
            for _ in range(3):
                prep(slot_of(q_no.n))
            for t in range(NT):
                dve.wait_ge(bd_added, t + 1)
                dve.wait_ge(down_ready, t + 1)
                nc.vector.tensor_tensor(tok[:, t, :], tok[:, t, :], whole(2 + 2 * t), ALU.add).then_inc(down_sum, 1)
                dve.wait_ge(down_sum, t + 1)
                statistics(t)

            s_no, exp_no, norm_no, pt_no = Tally(), Tally(), Tally(), Tally()

            def maxima(s):
                dve.wait_ge(s_ready, s_no.add())
                nc.vector.memset(waited[:], 0.0)
                for t in range(NT):
                    ins = nc.vector.tensor_tensor_reduce(
                        out=probs[:, s, t, :], in0=ps[:, 2 + 3 * s + t, 0:N], in1=maskb[:, t, :], scale=1.0,
                        scalar=3.0 * NONE, op0=ALU.add, op1=ALU.max, accum_out=smx[:, s, t:t + 1])
                then(ins)
                nc.vector.tensor_scalar(snm[:, s, :], smx[:, s, :], -DH ** -0.5, None, ALU.mult).then_inc(s_max, 1)

            def normalise(s):
                dve.wait_ge(s_exp, exp_no.add(NT))
                then(nc.vector.reciprocal(sinv[:, s, :], ssum[:, s, :]))
                for t in range(NT):
                    ins = nc.vector.tensor_scalar(probs[:, s, t, :], probs[:, s, t, :], sinv[:, s, t:t + 1],
                                                  None, ALU.mult)
                ins.then_inc(s_norm, 1)

            def pt_part(s):
                dve.wait_ge(pt_hi, pt_no.add())
                lo(pt[:, 1, :, :], ps[:, 2 + 3 * s:5 + 3 * s, 0:N], pt[:, 0, :, :]).then_inc(pt_lo, 1)

            def head_rows(s):
                return slice(s * DH, (s + 1) * DH)

            def out_part(s, p):
                f = feat[0][head_rows(s), :, bass.ds(p, 1), :]
                acc_part(f[:, 1, :, :], f[:, 0, :, :], head_rows(s), 0.0)

            def pair(p, first, last):
                if not first:
                    normalise(0)
                acc_part(qp[:, 1, :], qp[:, 0, :], everyone, bias[:, bass.ds(p + B_IQ, 1)])
                prep(3)
                if not first:
                    normalise(1)
                    pt_part(0)
                acc_part(kp[:, 1, :], kp[:, 0, :], everyone, bias[:, bass.ds(p + B_IK, 1)])
                prep(0 if last else 1)
                if not first:
                    out_part(0, p - 1)
                    pt_part(1)
                bank = acc.n % 2
                dve.wait_ge(acc_ready, acc.add())
                nc.vector.tensor_scalar(vt[:], ps[:, bank, 0:N], bias[:, bass.ds(p + B_IV, 1)], None, ALU.add)\
                    .then_inc(acc_free, 1)
                prep(1 if last else 2)
                if not first:
                    out_part(1, p - 1)
                acc_part(vp[:, 1, :, :].rearrange("p t d -> p (t d)"), vp[:, 0, :, :].rearrange("p t d -> p (t d)"),
                         everyone, 0.0)
                maxima(0)
                maxima(1)

            dve.wait_ge(mask_in, 16)
            pair(0, True, False)
            with repeat(dve, PAIRS - 2, {q_no: 3, acc: 6, hi_no: 5, s_no: 2, exp_no: 2 * NT, pt_no: 2,
                                         step: 4}) as i:
                pair(i + 1, False, False)
            pair(PAIRS - 1, False, True)
            normalise(0)
            normalise(1)
            for s in range(2):
                pt_part(s)
                out_part(s, PAIRS - 1)

            for h in range(2):
                for j in range(RING):
                    if q_no.n < Q_MOE:
                        prep(slot_of(q_no.n))
                for t in range(NT):
                    if h == 0:
                        dve.wait_ge(mix_done, t + 1)
                    dve.wait_ge(wo_ready, h * NT + t + 1)
                    row = tok[:, t, h * HALF:(h + 1) * HALF]
                    nc.vector.tensor_tensor(row, row, ps[:, 2 + 3 * h + t, :], ALU.add).then_inc(wo_sum, 1)
            dve.wait_ge(b12_hi, 1)
            lo(bigs[3][0:EXPERTS, 1, 0:F + D], work[0:EXPERTS, 0:F + D], bigs[3][0:EXPERTS, 0, 0:F + D])\
                .then_inc(b12_lo, 1)
            for t in range(NT):
                dve.wait_ge(wo_sum, NT + t + 1)
                statistics(t)
            for t in range(NT):
                dve.wait_ge(rstd_done, 3 * NT + t + 1)
                if t == 2:
                    dve.wait_ge(b12_lo, 1)
                nc.vector.tensor_scalar(rowbuf[:, t, :] if t < 2 else work[:, 0:D], tok[:, t, :], mv[:, t, 0:1],
                                        rs[:, t, 1:2], ALU.subtract, ALU.mult).then_inc(x2_done, 1)

            def tile3(k):
                return rt[:, k, :].rearrange("p (t e) -> p t e", t=NT)

            def spread(a):
                return a.unsqueeze(2).to_broadcast([P, NT, EXPERTS])

            w8 = cst[:, C_W8:C_W8 + EXPERTS].unsqueeze(1).to_broadcast([P, NT, EXPERTS])
            dve.wait_ge(logits_ready, NT)
            then(nc.vector.tensor_tensor(rt[:, R_LOGIT, :], ps[:, 0, 0:NT * EXPERTS], sbias[:], ALU.add))
            then(nc.vector.reduce_max(rt[:, R_MAX, 0:NT], tile3(R_LOGIT), AX_X))
            nc.vector.tensor_scalar(rt[:, R_NMAX, 0:NT], rt[:, R_MAX, 0:NT], -1.0, None, ALU.mult)\
                .then_inc(lmax_done, 1)
            then(nc.vector.tensor_tensor(tile3(R_HOT), tile3(R_LOGIT), spread(rt[:, R_MAX, 0:NT]), ALU.is_equal))
            then(nc.vector.tensor_tensor(tile3(R_HOT), tile3(R_HOT), w8, ALU.mult))
            then(nc.vector.reduce_max(rt[:, R_FIRST, 0:NT], tile3(R_HOT), AX_X))
            nc.vector.tensor_tensor(tile3(R_HOT), tile3(R_HOT), spread(rt[:, R_FIRST, 0:NT]), ALU.is_equal)\
                .then_inc(hot_done, 1)
            for k in range(4):
                ins = nc.vector.memset(cum[:, k, 0:4], 0.0)
            then(ins)
            dve.wait_ge(count_ready, 1)
            n_e = ps[:, 6, NT * EXPERTS:(NT + 1) * EXPERTS]
            nblk = cum[:, 0, 4:12]
            then(nc.vector.tensor_scalar(rt[:, R_TOTAL, 0:EXPERTS], n_e, 0.0, None, ALU.add))
            tot = rt[:, R_TOTAL, 0:EXPERTS]
            then(nc.vector.tensor_scalar(nblk, tot, 0.0, None, ALU.is_gt))
            for k in range(1, NT):
                then(nc.vector.scalar_tensor_tensor(out=nblk, in0=tot, scalar=float(k * P), in1=nblk,
                                                    op0=ALU.is_gt, op1=ALU.add))
            for k in range(3):
                sh = 1 << k
                then(nc.vector.tensor_tensor(cum[:, k + 1, 4:12], cum[:, k, 4:12], cum[:, k, 4 - sh:12 - sh], ALU.add))
            end = cum[:, 3, 4:12]
            cmp = slotc[:]
            slots = cst[:, C_SLOT:C_SLOT + SLOTS * EXPERTS].rearrange("p (s e) -> p s e", s=SLOTS)
            then(nc.vector.tensor_tensor(cmp, end.unsqueeze(1).to_broadcast([P, SLOTS, EXPERTS]), slots, ALU.is_le))
            then(nc.vector.reduce_sum(slote[:, 0, :], cmp, AX_X))
            then(nc.vector.tensor_scalar(slote[:, 1, :], slote[:, 0, :], float(EXPERTS - 1), None, ALU.min))
            then(nc.vector.tensor_scalar(slote[:, 2, :], slote[:, 1, :], cst[:, C_EXP:C_EXP + 1], None, ALU.is_equal))
            nc.vector.tensor_scalar(rowi[:], slote[:, 1, :], float(QE * P), None, ALU.mult).then_inc(route_done, 1)
            first = rt[:, R_FIRST, 0:EXPERTS]
            then(nc.vector.tensor_tensor(first, end, nblk, ALU.subtract))
            then(nc.vector.tensor_scalar(first, first, float(P), None, ALU.mult))
            cnt = ps[:, 6, 0:NT * EXPERTS].rearrange("p (t e) -> p t e", t=NT)
            then(nc.vector.tensor_tensor(tile3(R_RANK), cnt, first.unsqueeze(1).to_broadcast([P, NT, EXPERTS]),
                                         ALU.add))
            then(nc.vector.tensor_tensor(tile3(R_RANK), tile3(R_RANK), tile3(R_HOT), ALU.mult))
            then(nc.vector.reduce_sum(rt[:, R_POS, 0:NT], tile3(R_RANK), AX_X))
            nc.vector.tensor_copy(posi[:], rt[:, R_POS, 0:NT]).then_inc(pos_done, 1)
            dve.wait_ge(lexp_done, NT)
            then(nc.vector.reciprocal(rt[:, R_PROB, 0:NT], rt[:, R_SUM, 0:NT]))
            for t in range(NT):
                dve.wait_ge(b2_ready, t + 1)
                nc.vector.scalar_tensor_tensor(out=tok[:, t, :], in0=whole(4), scalar=rt[:, R_PROB, t:t + 1],
                                               in1=tok[:, t, :], op0=ALU.mult, op1=ALU.add).then_inc(b2_added, 1)

            xt, y_no, ht, slot_no = Tally(2 * NT), Tally(), Tally(), Tally()

            def hot_slot(s):
                nc.vector.tensor_copy(slot_hot[0:EXPERTS, :],
                                      slote[0:EXPERTS, 2, bass.ds(s, 1)].to_broadcast([EXPERTS, P]))\
                    .then_inc(slot_set, 1)

            def split_slot():
                dve.wait_ge(tr_hi, xt.add())
                lo(bigs[1][:, 1, 0:D], whole(2), bigs[1][:, 0, 0:D]).then_inc(tr_free, 1)

            def split_hidden():
                dve.wait_ge(ht_hi, ht.add())
                lo(bigs[2][:, 1, 0:F], ps[:, 1, :], bigs[2][:, 0, 0:F]).then_inc(ht_lo, 1)

            def second_half_of_y(i):
                dve.wait_ge(y_ready, y_no.add())
                if not isinstance(i, int) or i:
                    dve.wait_ge(y_out, i * 16)
                nc.vector.tensor_copy(y_buf[:, HALF:D], ps[:, 5, :]).then_inc(y_half1, 1)

            prep(0)
            prep(1)
            split_slot()
            hot_slot(0)
            for j in (2, 3, 0, 1):
                prep(j)
            split_slot()
            hot_slot(1)
            split_hidden()

            def slot_turn(i, last):
                for j in (2, 3, 0, 1):
                    prep(j)
                if not last:
                    split_slot()
                    hot_slot(i + 2)
                for j in (2, 3, 0, 1):
                    prep(j)
                second_half_of_y(i)
                split_hidden()

            slot_turn(0, False)
            with repeat(dve, SLOTS - 3, {q_no: QE, xt: 1, y_no: 1, ht: 1}) as i:
                slot_turn(i + 1, False)
            slot_turn(SLOTS - 2, True)
            prep(2)
            prep(3)
            second_half_of_y(SLOTS - 1)

            dve.wait_ge(b2_added, NT)
            for t in range(NT):
                src = rowbuf[:, t, :] if t < 2 else work[:, 0:D]
                dve.wait_ge(yg_in[t], 16)
                nc.vector.scalar_tensor_tensor(out=tok[:, t, :], in0=src, scalar=rt[:, R_PROB, t:t + 1],
                                               in1=tok[:, t, :], op0=ALU.mult, op1=ALU.add).then_inc(sum_done, 1)

        @block.tensor
        def _(pe):
            q_no, acc = Tally(), Tally()

            def open_quarter():
                pe.wait_ge(w_lo, q_no.add())

            def open_acc():
                bank = acc.n % 2
                if acc.i is not None or acc.n >= 2:
                    pe.wait_ge(acc_free, acc.value - 1)
                acc.add()
                return bank

            def feature_major(slot, moving):
                open_quarter()
                bank = open_acc()
                for k in range(KT):
                    for n, (a, b) in enumerate(PASSES):
                        ins = nc.tensor.matmul(ps[:, bank, 0:N], wsp[:, a, slot, k * P:(k + 1) * P],
                                               moving[:, b, k, :], start=(k == 0 and n == 0),
                                               stop=(k == KT - 1 and n == 2))
                        if k == 0 and n == 0:
                            ins.then_inc(w_started, 1)
                ins.then_inc(acc_ready, 1)

            def token_major(slot, j, stationary, banks, ready):
                open_quarter()
                for t in range(NT):
                    for kk in range(2):
                        k = 2 * j + kk
                        for n, (a, b) in enumerate(PASSES):
                            ins = nc.tensor.matmul(ps[:, banks + t, :], stationary[:, b, k, t * P:(t + 1) * P],
                                                   wsp[:, a, slot, kk * HALF:(kk + 1) * HALF],
                                                   start=(k == 0 and n == 0), stop=(k == KT - 1 and n == 2))
                            if t == 0 and kk == 0 and n == 0:
                                ins.then_inc(w_started, 1)
                    if j == 3:
                        ins.then_inc(ready, 1)

            turn = {q_no: RING, acc: RING}

            pe.wait_ge(const_in, 32)
            for t in range(NT):
                pe.wait_ge(xn_done, t + 1)
                for k in range(KT):
                    ins = nc.tensor.transpose(set_banks(t)[:, k, :], tok[:, t, k * P:(k + 1) * P], ident)
                ins.then_inc(tr_ready, 1)
            pe.wait_ge(tr_free, NT)

            for m in range(1):
                for j in range(RING):
                    feature_major(j, feat[0])
            with repeat(pe, 3, turn):
                for j in range(RING):
                    feature_major(j, feat[0])
            for h in range(2):
                for j in range(RING):
                    token_major(j, j, feat[0], 2 + 3 * h, tm_ready)

            pe.wait_ge(elu_lo, 2 * KT)
            for mt in range(NT):
                bank = open_acc()
                for k in range(KT):
                    for n, (a, b) in enumerate(PASSES):
                        ins = nc.tensor.matmul(ps[:, bank, 0:N], feat[2][:, a, k, mt * P:(mt + 1) * P],
                                               feat[1][:, b, k, :], start=(k == 0 and n == 0),
                                               stop=(k == KT - 1 and n == 2))
                ins.then_inc(acc_ready, 1)
            pe.wait_ge(acc_free, acc.value)
            pe.wait_ge(tm_lo, 2 * NT)
            pe.wait_ge(ones_set, 1)
            for t in range(NT):
                b0 = 2 + 3 * (t % 2)
                if t == 2:
                    pe.wait_ge(num_free, 1)
                for mt in range(NT):
                    for a in range(2):
                        nc.tensor.matmul(ps[:, b0 + 2, 0:2], pt[:, a, mt, t * P:(t + 1) * P], ones_r[:],
                                         start=(mt == 0 and a == 0), stop=(mt == NT - 1 and a == 1))
                for h in range(2):
                    for mt in range(NT):
                        for n, (a, b) in enumerate(PASSES):
                            ins = nc.tensor.matmul(ps[:, b0 + h, :], pt[:, a, mt, t * P:(t + 1) * P],
                                                   tokv[3][:, b, mt, h * HALF:(h + 1) * HALF],
                                                   start=(mt == 0 and n == 0), stop=(mt == NT - 1 and n == 2))
                ins.then_inc(num_ready, 1)

            for _ in range(3):
                with repeat(pe, 2, turn):
                    for j in range(RING):
                        feature_major(j, feat[0])

            pe.wait_ge(num_free, NT)
            for t in range(NT):
                pe.wait_ge(x1_done, t + 1)
                for k in range(KT):
                    ins = nc.tensor.transpose(set_banks(t)[:, k, :], tok[:, t, k * P:(k + 1) * P], ident)
                ins.then_inc(tr_ready, 1)
            pe.wait_ge(tr_free, 2 * NT)
            for q in range(Q_GU, Q_DOWN):
                feature_major(slot_of(q), feat[0])
            pe.wait_ge(hid_lo, FHT)
            for t in range(NT):
                for h in range(2):
                    for k in range(FHT):
                        blk = h * FHT + k
                        slot, kk = slot_of(Q_DOWN + blk // 2), blk % 2
                        if t == 0 and kk == 0:
                            open_quarter()
                        for n, (a, b) in enumerate(PASSES):
                            ins = nc.tensor.matmul(ps[:, 2 + 2 * t + h, :], pt[:, b, k, t * P:(t + 1) * P],
                                                   wsp[:, a, slot, kk * HALF:(kk + 1) * HALF],
                                                   start=(k == 0 and n == 0), stop=(k == FHT - 1 and n == 2))
                            if t == 0 and n == 0 and kk == 0:
                                ins.then_inc(w_started, 1)
                ins.then_inc(down_ready, 1)

            pt_no, norm_no, s_no = Tally(), Tally(), Tally()

            def transpose_probs(s):
                pe.wait_ge(s_norm, norm_no.add())
                for mt in range(NT):
                    for t in range(NT):
                        ins = nc.tensor.transpose(ps[:, 2 + 3 * s + mt, t * P:(t + 1) * P],
                                                  probs[:, s, t, mt * P:(mt + 1) * P], ident)
                ins.then_inc(pt_ready, 1)

            def attend(s):
                pe.wait_ge(pt_lo, pt_no.add())
                bank = open_acc()
                for mt in range(NT):
                    for n, (a, b) in enumerate(PASSES):
                        ins = nc.tensor.matmul(ps[:, bank, 0:N], vp[:, a, mt, :], pt[:, b, mt, :],
                                               start=(mt == 0 and n == 0), stop=(mt == NT - 1 and n == 2))
                ins.then_inc(acc_ready, 1)

            def scores(s):
                rows = slice(s * DH, (s + 1) * DH)
                for t in range(NT):
                    for n, (a, b) in enumerate(PASSES):
                        ins = nc.tensor.matmul(ps[:, 2 + 3 * s + t, 0:N], qp[rows, a, t * P:(t + 1) * P],
                                               kp[rows, b, :], start=(n == 0), stop=(n == 2))
                ins.then_inc(s_ready, 1)

            def pair(first, last):
                feature_major(1, feat[1])
                if not first:
                    transpose_probs(0)
                feature_major(2, feat[2])
                if not first:
                    attend(0)
                    transpose_probs(1)
                feature_major(3, feat[3])
                if not first:
                    attend(1)
                pe.wait_ge(acc_free, acc.value if first else acc.value - 1)
                bank = open_acc()
                for mt in range(NT):
                    ins = nc.tensor.transpose(ps[:, bank, mt * P:(mt + 1) * P], vt[:, mt * P:(mt + 1) * P], ident)
                ins.then_inc(acc_ready, 1)
                for s in range(2):
                    scores(s)

            pe.wait_ge(down_sum, NT)
            pair(True, False)
            with repeat(pe, PAIRS - 2, {q_no: 3, acc: 6, norm_no: 2, pt_no: 2}):
                pair(False, False)
            pair(False, True)
            for s in range(2):
                transpose_probs(s)
                if s == 0:
                    pe.wait_ge(acc_free, acc.value)
                attend(s)

            pe.wait_ge(acc_free, acc.value)
            for h in range(2):
                for j in range(RING):
                    token_major(j, j, feat[0], 2 + 3 * h, wo_ready)

            pe.wait_ge(wo_sum, 2 * NT)
            for t in range(NT):
                pe.wait_ge(x2_done, t + 1)
                if t:
                    pe.wait_ge(x2t_copied, t)
                src = rowbuf[:, t, :] if t < 2 else work[:, 0:D]
                for k in range(KT):
                    ins = nc.tensor.transpose(whole(2)[:, k * P:(k + 1) * P], src[:, k * P:(k + 1) * P], ident)
                ins.then_inc(x2t_ready, 1)
                pe.wait_ge(x2t_copied, t + 1)
                for k in range(KT):
                    ins = nc.tensor.matmul(ps[:, 0, t * EXPERTS:(t + 1) * EXPERTS], x2t[:, k * P:(k + 1) * P],
                                           swt[:, k, :], start=(k == 0), stop=(k == KT - 1))
                ins.then_inc(logits_ready, 1)
            hot = rt[:, R_HOT, :]
            pe.wait_ge(hot_done, 1)
            for t in range(NT):
                for u in range(t + 1):
                    nc.tensor.matmul(ps[:, 6, t * EXPERTS:(t + 1) * EXPERTS], tri if u == t else ones,
                                     hot[:, u * EXPERTS:(u + 1) * EXPERTS], start=(u == 0), stop=(u == t))
            for u in range(NT):
                ins = nc.tensor.matmul(ps[:, 6, NT * EXPERTS:(NT + 1) * EXPERTS], ones,
                                       hot[:, u * EXPERTS:(u + 1) * EXPERTS], start=(u == 0), stop=(u == NT - 1))
            ins.then_inc(count_ready, 1)
            for t in range(NT):
                ins = nc.tensor.transpose(ps[0:EXPERTS, 1, t * P:(t + 1) * P],
                                          hot[:, t * EXPERTS:(t + 1) * EXPERTS], ident)
            ins.then_inc(hott_ready, 1)
            pe.wait_ge(hott_copied, 1)
            for t in range(NT):
                if t:
                    pe.wait_ge(b2_added, t)
                for h in range(2):
                    for b in range(2):
                        ins = nc.tensor.matmul(ps[:, 4 + h, :], pt[0:EXPERTS, 0, 0, t * P:(t + 1) * P],
                                               bigs[3][0:EXPERTS, b, F + h * HALF:F + (h + 1) * HALF],
                                               start=(b == 0), stop=(b == 1))
                ins.then_inc(b2_ready, 1)
            pe.wait_ge(b2_added, NT)

            xs_no, xt, slot_no, h_act_no, ht_no, y_no = Tally(), Tally(2 * NT), Tally(), Tally(), Tally(), Tally()
            xst = bigs[1][:, :, 0:D].rearrange("p h (k n) -> p h k n", k=KT)
            hts = bigs[2][:, :, 0:F].rearrange("p h (k n) -> p h k n", k=F // P)

            def load_tokens():
                pe.wait_ge(xs_in, xs_no.add(16))
                for k in range(KT):
                    ins = nc.tensor.transpose(whole(2)[:, k * P:(k + 1) * P], rowbuf[:, 0, k * P:(k + 1) * P], ident)
                ins.then_inc(tr_ready, 1)

            def up(first):
                pe.wait_ge(tr_free, xt.add())
                if not first:
                    pe.wait_ge(h_act, h_act_no.add())
                for j in range(4):
                    open_quarter()
                    for kk in range(2):
                        k = 2 * j + kk
                        for n, (a, b) in enumerate(PASSES):
                            ins = nc.tensor.matmul(ps[:, 0, :], xst[:, b, k, :],
                                                   wsp[:, a, j, kk * HALF:(kk + 1) * HALF],
                                                   start=(k == 0 and n == 0), stop=False)
                            if kk == 0 and n == 0:
                                ins.then_inc(w_started, 1)
                pe.wait_ge(slot_set, slot_no.add())
                for b in range(2):
                    ins = nc.tensor.matmul(ps[:, 0, :], slot_hot[0:EXPERTS, :], bigs[3][0:EXPERTS, b, 0:F],
                                           start=False, stop=(b == 1))
                ins.then_inc(h_ready, 1)

            def down(first):
                pe.wait_ge(ht_lo, ht_no.add())
                if not first:
                    pe.wait_ge(y_half0, y_no.add())
                    pe.wait_ge(y_half1, y_no.value)
                for j in range(4):
                    open_quarter()
                    h = j // 2
                    for kk in range(2):
                        k = 2 * (j % 2) + kk
                        for n, (a, b) in enumerate(PASSES):
                            ins = nc.tensor.matmul(ps[:, 4 + h, :], hts[:, b, k, :],
                                                   wsp[:, a, j, kk * HALF:(kk + 1) * HALF],
                                                   start=(k == 0 and n == 0), stop=(k == 3 and n == 2))
                            if kk == 0 and n == 0:
                                ins.then_inc(w_started, 1)
                ins.then_inc(y_ready, 1)

            def transpose_hidden():
                pe.wait_ge(h_act, h_act_no.value + 1)
                for k in range(F // P):
                    ins = nc.tensor.transpose(ps[:, 1, k * P:(k + 1) * P], h_buf[:, k * P:(k + 1) * P], ident)
                ins.then_inc(ht_ready, 1)

            load_tokens()
            up(True)
            load_tokens()
            transpose_hidden()

            def slot_turn(first, last):
                up(False)
                if not last:
                    load_tokens()
                down(first)
                transpose_hidden()

            slot_turn(True, False)
            with repeat(pe, SLOTS - 3, {q_no: QE, xs_no: 16, xt: 1, slot_no: 1, h_act_no: 1, ht_no: 1, y_no: 1}):
                slot_turn(False, False)
            slot_turn(False, True)
            down(False)


def _feature_quarters(w):
    k, n = w.shape
    return w.reshape(k // 128, 128, n // 128, 128).transpose(2, 1, 0, 3).reshape(-1, 1024)


def _token_quarters(w):
    k, n = w.shape
    return w.reshape(k // 256, 2, 128, n // 512, 512).transpose(3, 0, 2, 1, 4).reshape(-1, 1024)


def kernel(**inputs):
    import numpy as _np
    import concourse.bacc as _bacc
    from concourse import mybir as _mybir
    from concourse.bass_utils import run_bass_kernel_spmd as _run

    a = {k: _np.asarray(v) for k, v in inputs.items()}
    f32 = _np.float32
    g = lambda name: a["L0_gnn_" + name]
    mx = lambda name: a["L0_mix_" + name]
    ff = lambda name: a["L0_ffn_" + name]

    pad = FHT * P - FH
    wqkv = mx("Wqkv")
    wg = _np.pad(mx("Wg"), ((0, 0), (0, pad)))
    wu = _np.pad(mx("Wu"), ((0, 0), (0, pad)))
    gate_up = _np.stack([_feature_quarters(wg).reshape(FHT, P, D), _feature_quarters(wu).reshape(FHT, P, D)], 1)
    wd = _np.pad(mx("Wd"), ((0, pad), (0, 0)))
    down = wd.reshape(FHT, P, 2, HALF).transpose(2, 0, 1, 3).reshape(3, 2, P, HALF).transpose(0, 2, 1, 3)
    pairs = _np.stack([_feature_quarters(g(n).T).reshape(PAIRS, P, D) for n in ("wiq", "wik", "wiv")], 1)
    stream = _np.concatenate([
        _feature_quarters(wqkv[:, 0:D]), _feature_quarters(wqkv[:, D:2 * D]), _token_quarters(wqkv[:, 2 * D:]),
        _feature_quarters(g("wq").T), _feature_quarters(g("wk").T), _feature_quarters(g("wv").T),
        gate_up.reshape(-1, D), down.reshape(-1, D), pairs.reshape(-1, D), _token_quarters(g("wo").T)])
    w1, w2 = ff("w1"), ff("w2")
    experts = _np.concatenate(
        [_np.concatenate([_token_quarters(w1[e]), _token_quarters(w2[e])]) for e in range(EXPERTS)])

    col = lambda v: _np.pad(v, (0, -len(v) % P)).reshape(-1, P).T
    bq = mx("bqkv")
    cols = _np.concatenate([col(bq[0:D]), col(bq[D:2 * D])] + [col(g(n)) for n in
                           ("bq", "bk", "bv", "biq", "bik", "biv")] + [col(mx("bg")), col(mx("bu"))], 1)
    row8 = _np.zeros(D, f32)
    row8[0:NT * EXPERTS] = _np.tile(ff("switch_b"), NT)
    rowb = _np.stack([bq[2 * D:], mx("g1"), mx("b1"), mx("bd"), mx("g2"), mx("b2"), g("bo"), row8])

    r = _np.arange(P)
    consts = _np.concatenate([
        _np.eye(P), (r[:, None] < r[None, :]).astype(f32), _np.ones((P, P)),
        _np.tile(_np.arange(EXPERTS, 0, -1), (P, 1)),
        _np.tile(_np.repeat(_np.arange(SLOTS), EXPERTS), (P, 1)), r[:, None],
        N * N + r[:, None] + P * _np.arange(EC)[None, :]], 1).astype(f32)
    later = (_np.arange(N)[None, None, :] > (_np.arange(GROUP) * P)[None, :, None] + r[:, None, None]).astype(f32)

    c = _np.ascontiguousarray
    arrays = {
        "x": a["x"], "rowb": rowb, "cols": c(cols), "consts": consts, "later": later,
        "src_rows": a["src"], "dst_rows": a["dst"],
        "src_cols": c(a["src"].reshape(EC, P).T), "dst_cols": c(a["dst"].reshape(EC, P).T),
        "type_cols": c(a["edge_type_5"].reshape(EC, P).T), "type_weights": g("edge_type_weights"),
        "w_stream": stream, "w_experts": experts,
        "switch_w": c(ff("switch_w").reshape(KT, P, EXPERTS).transpose(1, 0, 2)),
        "b12": _np.concatenate([ff("b1"), ff("b2")], 1),
    }
    nc = _bacc.Bacc("TRN2", target_bir_lowering=False, num_devices=1)
    aps = [nc.dram_tensor("in_" + k, v.shape, _mybir.dt.from_np(v.dtype), kind="ExternalInput").ap()
           for k, v in arrays.items()]
    out = nc.dram_tensor("out_dram", (N, D), _mybir.dt.float32, kind="ExternalOutput").ap()
    graph_layer(nc, *aps, out)
    got = _run(nc, [{"in_" + k: v for k, v in arrays.items()}], core_ids=[0])
    return got.results[0]["out_dram"]
```

```python
from contextlib import ExitStack, contextmanager

import concourse.bass as bass
from concourse import mybir

ALU = mybir.AluOpType
ACT = mybir.ActivationFunctionType
F32 = mybir.dt.float32
F32R = mybir.dt.float32r
I32 = mybir.dt.int32
AX_X = mybir.AxisListType.X

P = 128
N = 384
NT = N // P
D = 1024
KT = D // P
HEADS = 16
PAIRS = HEADS // 2
DH = D // HEADS
E_EDGES = 6144
EC = E_EDGES // P
GROUP = 3
PIECES = EC // GROUP
FH = 341
FHT = 3
EXPERTS = 8
F = 512
OVER = (N - 1) // P
SLOTS = EXPERTS + OVER
RING = 4
XRING = 8
HALF = 512
NONE = -1.0e30
PASSES = ((0, 0), (0, 1), (1, 0))

B_MQ, B_MK, B_Q, B_K, B_V, B_IQ, B_IK, B_IV, B_G, B_U = 0, 8, 16, 24, 32, 40, 48, 56, 64, 67
NBIAS = 70
C_ID, C_TRI, C_ONE, C_W8, C_EID, C_SLOT = 0, 128, 256, 384, 392, 400
C_EXP = C_SLOT + OVER * EXPERTS
C_SPARE = C_EXP + 1
NCONST = C_SPARE + EC

R_LOGIT, R_MAX, R_NMAX, R_EXP, R_SUM, R_PROB, R_HOT, R_FIRST, R_RANK, R_TOTAL, R_POS = range(11)

Q_MQ, Q_MK, Q_MV, Q_GQ, Q_GK, Q_GV, Q_PAIR0 = 0, 8, 16, 24, 32, 40, 48
Q_GU = Q_PAIR0 + 2
Q_DOWN = Q_GU + 2 * FHT + 1
Q_PAIR = Q_DOWN + 3
Q_WO = Q_PAIR + 3 * (PAIRS - 1)
Q_MOE = Q_WO + 8
QE = 8


class Tally:

    def __init__(self, n=0):
        self.n, self.i, self.per = n, None, 0

    @property
    def value(self):
        return self.n if self.i is None else self.i * self.per + self.n

    def add(self, n=1):
        self.n += n
        return self.value


@contextmanager
def repeat(engine, times, per):
    first = {t: t.n for t in per}
    with engine.Fori(0, times) as i:
        for t, n in per.items():
            t.i, t.per = i, n
        yield i
    for t, n in per.items():
        assert t.n == first[t] + n, (t.n, first[t], n)
        t.n, t.i = first[t] + n * times, None


def slot_of(q):
    if q < Q_PAIR:
        return q % RING
    if q < Q_WO:
        return 1 + (q - Q_PAIR) % 3
    if q < Q_MOE:
        return (q - Q_WO) % RING
    return (q - Q_MOE + RING) % XRING


def graph_layer(nc, x, rowb, cols, consts, later, src_rows, dst_rows, src_cols, dst_cols, type_cols,
                type_weights, w_stream, w_experts, switch_w, b12, out):
    with ExitStack() as ctx:
        def sb(name, shape, dt=F32):
            return ctx.enter_context(nc.sbuf_tensor(name, shape, dt))

        def sem(name):
            return ctx.enter_context(nc.semaphore(name))

        raw = sb("raw", [P, RING, D])
        wsp = sb("wsp", [P, 2, RING, D], F32R)
        with nc.sbuf_tensor("big1", [P, 2, KT * N], F32R) as big1:
            pass
        raw_x = sb("raw_x", [P, RING, D])
        xsp = sb("xsp", [P, 2, D], F32R)
        bigs = [sb("big0", [P, 2, KT * N], F32R), big1] + [sb(f"big{n}", [P, 2, KT * N], F32R) for n in (2, 3)]
        feat = [b[:].rearrange("p h (k n) -> p h k n", k=KT) for b in bigs]
        tokv = [b[:].rearrange("p h (t d) -> p h t d", t=NT) for b in bigs]
        tok = sb("tok", [P, NT, D])
        pt = sb("pt", [P, 2, NT, N], F32R)
        work = sb("work", [P, 2 * NT * N])
        maskb = sb("maskb", [P, NT, N])
        qp = sb("qp", [P, 2, N], F32R)
        kp = sb("kp", [P, 2, N], F32R)
        vp = sb("vp", [P, 2, NT, P], F32R)
        row_buf = sb("row_buf", [P, D])
        diag = sb("diag", [P, P])
        rowbuf = sb("rowbuf", [P, 2, D])
        bias = sb("bias", [P, NBIAS])
        cst = sb("cst", [P, NCONST])
        swt = sb("swt", [P, KT, EXPERTS])
        sbias = sb("sbias", [P, NT * EXPERTS])
        ones_r = sb("ones_r", [P, 2], F32R)
        slot_hot = sb("slot_hot", [P, P], F32R)
        ei = sb("ei", [P, 3, EC], I32)
        ef = sb("ef", [P, 6, EC])
        eidx = sb("eidx", [P, EC], I32)
        tw = sb("tw", [P, 4, 4])
        dup = sb("dup", [P, EC])
        stats = sb("stats", [P, NT, 2, 6])
        mv = sb("mv", [P, NT, 2])
        rs = sb("rs", [P, NT, 2])
        half = sb("half", [P, 1])
        waited = sb("waited", [P, 1])
        den = sb("den", [P, 2 * NT])
        smx = sb("smx", [P, 2, NT])
        snm = sb("snm", [P, 2, NT])
        ssum = sb("ssum", [P, 2, NT])
        sinv = sb("sinv", [P, 2, NT])
        rt = sb("rt", [P, 11, NT * EXPERTS])
        cum = sb("cum", [P, 4, 12])
        slotc = sb("slotc", [P, OVER, EXPERTS])
        slote = sb("slote", [P, 3, SLOTS])
        posi = sb("posi", [P, NT], I32)
        rowi = sb("rowi", [P, OVER + 1], I32)

        vt = row_buf[:, 0:N]
        ident = cst[:, C_ID:C_ID + P]
        tri = cst[:, C_TRI:C_TRI + P]
        ones = cst[:, C_ONE:C_ONE + P]
        maskflat = maskb[:].rearrange("p t n -> p (t n)")
        probs = work[:].rearrange("p (s t n) -> p s t n", s=2, t=NT)
        edge_rows = [rowbuf[:].rearrange("p a b -> p (a b)")[:, 768 * n:768 * (n + 1)].bitcast(I32)
                     .rearrange("p (a b) -> p a b", a=2) for n in range(2)]
        codes = work[:, 0:N]
        junk = [work[:, N * (n + 1):N * (n + 2)] for n in range(GROUP)]
        elu_s, elu_e, elu_r = work[:, 4 * N:5 * N], work[:, 5 * N:6 * N], vt
        gate, hid = work[:, 0:N], work[:, N:2 * N]
        x2t = [work[:, D:2 * D], maskflat[:, 0:D], row_buf[:]]
        x2 = [rowbuf[:, 0, :], rowbuf[:, 1, :], work[:, 0:D]]
        hts, b12r = bigs[2][:, :, D:D + F], bigs[2][0:EXPERTS, :, D + F:D + 2 * F + D]
        h_buf, y_buf = maskflat[:, 0:F], work[:, 0:D]
        spare = cst[:, C_SPARE:C_SPARE + EC]

        ps = ctx.enter_context(nc.psum_tensor("ps", [P, 8, HALF], F32))

        table = nc.dram_tensor("edge_table", [N * N + P * EC, 1], F32).ap()
        xs_dram = nc.dram_tensor("slot_x", [SLOTS * P, D], F32).ap()
        ys_dram = nc.dram_tensor("slot_y", [SLOTS * P, D], F32).ap()

        x_in = [sem(f"x_in{t}") for t in range(NT)]
        const_in, edge_in, rowb_in, b_row_in = sem("const_in"), sem("edge_in"), sem("rowb_in"), sem("b_row_in")
        piece_in = [sem(f"piece_in{n}") for n in range(2)]
        piece_done = sem("piece_done")
        raw_in = [sem(f"raw_in{n}") for n in range(XRING)]
        w_hi, w_lo = sem("w_hi"), sem("w_lo")
        w_started = sem("w_started")
        acc_ready, acc_hi, acc_free = sem("acc_ready"), sem("acc_hi"), sem("acc_free")
        elu_parts, elu_hi = sem("elu_parts"), sem("elu_hi")
        elu_lo = sem("elu_lo")
        tr_ready, tr_hi, tr_free = sem("tr_ready"), sem("tr_hi"), sem("tr_free")
        tm_ready, tm_sum, tm_hi, tm_lo = sem("tm_ready"), sem("tm_sum"), sem("tm_hi"), sem("tm_lo")
        dve_step, act_step, pool_step = sem("dve_step"), sem("act_step"), sem("pool_step")
        ones_set = sem("ones_set")
        stats_done, rstd_done, xn_done = sem("stats_done"), sem("rstd_done"), sem("xn_done")
        num_ready, num_free = sem("num_ready"), sem("num_free")
        x1_done, bd_added = sem("x1_done"), sem("bd_added")
        hid_hi, hid_lo = sem("hid_hi"), sem("hid_lo")
        down_ready, down_sum, mix_done = sem("down_ready"), sem("down_sum"), sem("mix_done")
        s_ready, s_max, s_exp, s_norm = sem("s_ready"), sem("s_max"), sem("s_exp"), sem("s_norm")
        pt_ready, pt_hi, pt_lo = sem("pt_ready"), sem("pt_hi"), sem("pt_lo")
        v_sum = sem("v_sum")
        tw_arg, tw_exp, tw_one, tw_ln, tw_done = (sem("tw_arg"), sem("tw_exp"), sem("tw_one"), sem("tw_ln"),
                                                  sem("tw_done"))
        edges_done = sem("edges_done")
        table_out, later_in, scattered, mask_in = (sem("table_out"), sem("later_in"), sem("scattered"),
                                                   sem("mask_in"))
        zero_out = sem("zero_out")
        b12_in, b12_hi, b12_lo = sem("b12_in"), sem("b12_hi"), sem("b12_lo")
        wo_ready, wo_sum = sem("wo_ready"), sem("wo_sum")
        x2_done, x2t_ready, x2t_copied, logits_ready = (
            sem("x2_done"), sem("x2t_ready"), sem("x2t_copied"), sem("logits_ready"))
        lmax_done, lexp_done, hot_done, count_ready, route_done, pos_done = (
            sem("lmax_done"), sem("lexp_done"), sem("hot_done"), sem("count_ready"), sem("route_done"),
            sem("pos_done"))
        xs_out, hott_ready, hott_copied, b2_ready, b2_added = (
            sem("xs_out"), sem("hott_ready"), sem("hott_copied"), sem("b2_ready"), sem("b2_added"))
        slot_set, xs_in = sem("slot_set"), sem("xs_in")
        h_ready, h_act, ht_ready, ht_hi, ht_lo = (sem("h_ready"), sem("h_act"), sem("ht_ready"),
                                                  sem("ht_hi"), sem("ht_lo"))
        y_ready, y_half0, y_half1, y_out = sem("y_ready"), sem("y_half0"), sem("y_half1"), sem("y_out")
        yg_in = [sem(f"yg_in{t}") for t in range(NT)]
        sum_done, out_done = sem("sum_done"), sem("out_done")

        block = ctx.enter_context(nc.Block())

        def set_banks(t):
            return ps[:, 2 + 2 * t:4 + 2 * t, :].rearrange("p a (b c) -> p (a b) c", c=P)

        def set_banks_row(t):
            return ps[:, 2 + 2 * t:4 + 2 * t, :].rearrange("p a b -> p (a b)")

        def raw_slot(k):
            if k < RING:
                return raw[:, k, :]
            return raw_x[:, k - RING, :]

        def split_of(k, part):
            if k < RING:
                return wsp[:, part, k, :]
            big, k = (bigs[3], k - RING) if k < XRING - 1 else (bigs[2], 0)
            return big[:, part, k * D:(k + 1) * D]

        def whole(a):
            return ps[:, a:a + 2, :].rearrange("p a b -> p (a b)")

        @block.sync
        def _(sp):
            for t in range(NT):
                sp.dma_start(tok[:, t, :], x[t * P:(t + 1) * P, :]).then_inc(x_in[t], 16)
            sp.dma_start(cst[:], consts).then_inc(const_in, 16)
            sp.dma_start(bias[:], cols).then_inc(const_in, 16)

            def load(row, slot, split):
                if split is not None:
                    sp.wait_ge(w_lo, split)
                sp.dma_start(raw[:, slot, :], w_stream[bass.ds(row, P), :]).then_inc(raw_in[slot], 16)

            def load_piece(first, buf, read):
                for k, r in enumerate((src_rows, dst_rows)):
                    if read is not None:
                        sp.wait_ge(piece_done, read)
                    sp.dma_start(edge_rows[buf][:, k, :],
                                 r[bass.ds(first, N)].partition_broadcast(P)).then_inc(piece_in[buf], 16)

            for q in range(RING):
                load(q * P, q, None)
            for j in range(2):
                load_piece(j * N, j, None)
            with sp.Fori(0, (Q_MV - RING) // RING) as i:
                for j in range(RING):
                    row = sp.snap(i * (RING * P) + (RING + j) * P)
                    first = sp.snap(i * (RING * N) + (2 + j) * N)
                    load(row, j, i * RING + (j + 1))
                    load_piece(first, j % 2, i * RING + (j + 1))
            for j in range(RING):
                load((Q_MV + j) * P, j, Q_MV + j - RING + 1)
                n = 2 + Q_MV - RING + j
                if n < PIECES:
                    load_piece(n * N, n % 2, n - 1)
            with sp.Fori(0, (Q_PAIR0 - Q_MV) // RING - 1) as i:
                for j in range(RING):
                    row = sp.snap(i * (RING * P) + (Q_MV + RING + j) * P)
                    load(row, j, i * RING + (Q_MV + j + 1))
            for q in range(Q_PAIR0, Q_PAIR):
                load(q * P, slot_of(q), q - RING + 1)
            with sp.Fori(0, PAIRS - 1) as i:
                for j in range(3):
                    row = sp.snap(i * (3 * P) + (Q_PAIR + j) * P)
                    load(row, 1 + j, i * 3 + (Q_PAIR + j - 2))
            for q in range(Q_WO, Q_MOE):
                load(q * P, slot_of(q), q - RING + 1)

            def load_expert(row, k, split):
                sp.wait_ge(w_lo, split)
                sp.dma_start(raw_slot(k), w_experts[bass.ds(row, P), :]).then_inc(raw_in[k], 16)

            sp.wait_ge(w_started, Q_WO + 1)
            for j in range(RING):
                load_expert(j * P, RING + j, Q_WO)
            with sp.Fori(0, EXPERTS - 1) as i:
                for k in range(XRING):
                    first = QE + k if k < RING else k
                    row = sp.snap(i * (QE * P) + first * P)
                    load_expert(row, k, i * XRING + (Q_MOE + RING + k - XRING + 1))
            q = Q_MOE + QE * EXPERTS - RING
            for j in range(RING):
                k = slot_of(q + j)
                load_expert(((EXPERTS - 1) * QE + RING + j) * P, k, q + j - XRING + 1)

            sp.wait_ge(route_done, 1)
            over = sp.value_load(rowi[0:1, OVER:OVER + 1], min_val=0, max_val=OVER)
            with sp.If(over > 0):
                q += RING
                for o in range(OVER):
                    r = sp.value_load(rowi[0:1, o:o + 1], min_val=0, max_val=(EXPERTS - 1) * QE * P)
                    for j in range(QE):
                        row = sp.snap(r + j * P)
                        load_expert(row, slot_of(q), q - XRING + 1)
                        q += 1

            for t in range(NT):
                sp.wait_ge(sum_done, t + 1)
                sp.dma_start(out[t * P:(t + 1) * P, :], tok[:, t, :]).then_inc(out_done, 16)
            sp.wait_ge(out_done, 16 * NT)

        @block.gpsimd
        def _(pool):
            step, rows_in = Tally(), Tally()
            R_BV, R_G1, R_B1, R_BD, R_G2, R_B2, R_BO, R_SW = range(8)

            def then(ins):
                ins.then_inc(pool_step, 1)
                pool.wait_ge(pool_step, step.add())

            def load_row(k, buf):
                pool.dma_start(rowbuf[:, buf, :], rowb[k].partition_broadcast(P)).then_inc(rowb_in, 16)
                rows_in.add(16)

            for k, r in enumerate((src_cols, dst_cols, type_cols)):
                pool.dma_start(ei[:, k, :], r).then_inc(edge_in, 16)
            pool.dma_start(tw[:, 0, :], type_weights.partition_broadcast(P)).then_inc(edge_in, 16)
            pool.dma_start(sbias[:], rowb[R_SW, 0:NT * EXPERTS].partition_broadcast(P)).then_inc(edge_in, 16)
            pool.dma_start(swt[:], switch_w).then_inc(edge_in, 16)
            then(nc.gpsimd.memset(half[:], -0.5))

            def rstd(t, n):
                pool.wait_ge(stats_done, n + 1)
                then(nc.gpsimd.tensor_scalar(rs[:, t, 0:1], mv[:, t, 1:2], 1e-5, None, ALU.add))
                nc.gpsimd.tensor_tensor(rs[:, t, 1:2], rs[:, t, 0:1], half[:], ALU.pow).then_inc(rstd_done, 1)

            for t in range(NT):
                rstd(t, t)

            then(nc.gpsimd.memset(maskb[:], NONE))
            for t in range(NT):
                then(nc.gpsimd.affine_select(out=maskb[:, t, :], in_=maskb[:, t, :], compare_op=ALU.not_equal,
                                             fill=0.0, base=t * P, pattern=[[-1, N]], channel_multiplier=1))
            pool.wait_ge(const_in, 32)
            pool.wait_ge(tw_done, 1)
            then(nc.gpsimd.tensor_scalar(diag[:], ident, tw[:, 3, 3:4], None, ALU.mult))
            for t in range(NT):
                blk = maskb[:, t, t * P:(t + 1) * P]
                then(nc.gpsimd.tensor_tensor(blk, blk, diag[:], ALU.add))
            pool.dma_start(table[0:N * N, :].rearrange("(t p n) o -> p t (n o)", t=NT, p=P),
                           maskb[:]).then_inc(table_out, 16)
            pool.wait_ge(table_out, 16)
            pool.dma_start(maskb[:], later).then_inc(later_in, 16)

            pool.wait_ge(edges_done, 1)
            for g in range(PIECES):
                for k in range(GROUP):
                    c = g * GROUP + k
                    pool.indirect_dma_start(
                        out=table, out_offset=bass.IndirectOffsetOnAxis(ap=eidx[:, c:c + 1], axis=0),
                        in_=ef[:, 3, c:c + 1], in_offset=None).then_inc(scattered, 16)
                pool.wait_ge(scattered, 16 * GROUP * (g + 1))
            pool.dma_start(maskb[:], table[0:N * N, :].rearrange("(t p n) o -> p t (n o)", t=NT, p=P))\
                .then_inc(mask_in, 16)

            pool.wait_ge(tm_sum, 2 * NT)
            load_row(R_G1, 0)
            load_row(R_B1, 1)
            pool.wait_ge(rowb_in, rows_in.value)
            for t in range(NT):
                rstd(t, NT + t)
                pool.wait_ge(rstd_done, NT + t + 1)
                row = tok[:, t, :]
                then(nc.gpsimd.tensor_scalar(row, row, mv[:, t, 0:1], rs[:, t, 1:2], ALU.subtract, ALU.mult))
                then(nc.gpsimd.tensor_tensor(row, row, rowbuf[:, 0, :], ALU.mult))
                nc.gpsimd.tensor_tensor(row, row, rowbuf[:, 1, :], ALU.add).then_inc(x1_done, 1)
            pool.wait_ge(x1_done, NT)
            load_row(R_BD, 0)
            pool.wait_ge(rowb_in, rows_in.value)
            for t in range(NT):
                pool.wait_ge(tr_ready, NT + t + 1)
                nc.gpsimd.tensor_tensor(tok[:, t, :], tok[:, t, :], rowbuf[:, 0, :], ALU.add)\
                    .then_inc(bd_added, 1)
            pool.wait_ge(bd_added, NT)
            then(nc.gpsimd.memset(rowbuf[:, 0, :], 0.0))
            for s in range(SLOTS):
                pool.dma_start(xs_dram[s * P:(s + 1) * P, :], rowbuf[:, 0, :]).then_inc(zero_out, 16)
            for s in range(EXPERTS, SLOTS):
                pool.dma_start(ys_dram[s * P:(s + 1) * P, :], rowbuf[:, 0, :]).then_inc(zero_out, 16)
            pool.wait_ge(zero_out, 16 * (SLOTS + OVER))
            load_row(R_G2, 0)
            load_row(R_B2, 1)
            pool.wait_ge(rowb_in, rows_in.value)
            for t in range(NT):
                rstd(t, 2 * NT + t)
                pool.wait_ge(rstd_done, 2 * NT + t + 1)
                row = tok[:, t, :]
                then(nc.gpsimd.tensor_scalar(row, row, mv[:, t, 0:1], rs[:, t, 1:2], ALU.subtract, ALU.mult))
                then(nc.gpsimd.tensor_tensor(row, row, rowbuf[:, 0, :], ALU.mult))
                then(nc.gpsimd.tensor_tensor(row, row, rowbuf[:, 1, :], ALU.add))
            load_row(R_BO, 0)
            for t in range(NT):
                row = tok[:, t, :]
                pool.dma_start(rowbuf[:, 1, :], x[t * P:(t + 1) * P, :]).then_inc(rowb_in, 16)
                rows_in.add(16)
                pool.wait_ge(rowb_in, rows_in.value)
                then(nc.gpsimd.tensor_tensor(row, row, rowbuf[:, 0, :], ALU.add))
                nc.gpsimd.tensor_tensor(row, row, rowbuf[:, 1, :], ALU.add).then_inc(mix_done, 1)
                pool.wait_ge(mix_done, t + 1)

            pool.wait_ge(pt_ready, HEADS)
            pool.dma_start(work[0:EXPERTS, 0:F + D], b12).then_inc(b12_in, 16)

            for t in range(NT):
                rstd(t, 3 * NT + t)
            pool.wait_ge(zero_out, 16 * (SLOTS + OVER))
            pool.wait_ge(pos_done, 1)
            for t in range(NT):
                pool.wait_ge(x2_done, t + 1)
                pool.indirect_dma_start(
                    out=xs_dram, out_offset=bass.IndirectOffsetOnAxis(ap=posi[:, t:t + 1], axis=0),
                    in_=x2[t], in_offset=None).then_inc(xs_out, 16)
            pool.wait_ge(y_out, 16 * EXPERTS)
            over = pool.value_load(rowi[0:1, OVER:OVER + 1], min_val=0, max_val=OVER)
            with pool.If(over > 0):
                pool.wait_ge(y_out, 16 * SLOTS)
            for t in range(NT):
                pool.indirect_dma_start(
                    out=x2[t], out_offset=None, in_=ys_dram,
                    in_offset=bass.IndirectOffsetOnAxis(ap=posi[:, t:t + 1], axis=0)).then_inc(yg_in[t], 16)

        @block.scalar
        def _(act):
            q_no = Tally()
            used = [Tally() for _ in range(XRING)]
            acc = Tally()
            everyone = slice(0, P)

            def prep(slot):
                act.wait_ge(raw_in[slot], used[slot].add(16))
                if q_no.i is not None or q_no.n >= RING:
                    act.wait_ge(w_started, q_no.value - 1)
                nc.scalar.activation(wsp[:, 0, slot, :], raw[:, slot, :], ACT.Copy).then_inc(w_hi, 1)
                q_no.add()

            def acc_part(dst, rows, b):
                bank = acc.n % 2
                act.wait_ge(acc_ready, acc.add())
                nc.scalar.activation(dst, ps[rows, bank, 0:N], ACT.Identity, bias=b).then_inc(acc_hi, 1)

            turn = {q_no: RING, acc: RING, **{u: 16 for u in used[:RING]}}

            prep(0)
            prep(1)
            for t in range(NT):
                act.wait_ge(tr_ready, t + 1)
                nc.scalar.activation(feat[0][:, 0, :, t * P:(t + 1) * P], set_banks(t), ACT.Copy).then_inc(tr_hi, 1)
            act.wait_ge(tw_arg, 1)
            nc.scalar.activation(tw[:, 1, :], tw[:, 1, :], ACT.Exp).then_inc(tw_exp, 1)
            act.wait_ge(tw_one, 1)
            nc.scalar.activation(tw[:, 1, :], tw[:, 1, :], ACT.Ln).then_inc(tw_ln, 1)

            act.wait_ge(const_in, 32)

            def elu_step(m, j):
                bank = acc.n % 2
                if acc.i is not None or acc.n:
                    act.wait_ge(acc_free, acc.value)
                act.wait_ge(acc_ready, acc.add())
                b = bias[:, bass.ds(m + B_MQ, 1)]
                nc.scalar.activation(elu_e, ps[:, bank, 0:N], ACT.Exp, bias=b).then_inc(elu_parts, 1)
                nc.scalar.activation(elu_r, ps[:, bank, 0:N], ACT.Relu, bias=b).then_inc(elu_parts, 1)
                prep((j + 2) % RING)
                act.wait_ge(acc_free, acc.value)
                return acc.n

            def elu_hi_part(big, m):
                nc.scalar.activation(feat[big][:, 0, bass.ds(m, 1), :], elu_s, ACT.Copy).then_inc(elu_hi, 1)

            for j in range(RING):
                elu_step(j, j)
                elu_hi_part(1, j)
            with repeat(act, 1, turn) as i:
                for j in range(RING):
                    elu_step(i * RING + (RING + j), j)
                    elu_hi_part(1, i * RING + (RING + j))
            with repeat(act, 2, turn) as i:
                for j in range(RING):
                    elu_step(i * RING + (2 * RING + j), j)
                    elu_hi_part(2, i * RING + j)

            act.wait_ge(piece_done, PIECES)
            act.dma_start(rowbuf[:, 1, :], rowb[0].partition_broadcast(P)).then_inc(b_row_in, 16)
            for h in range(2):
                for j in range(RING):
                    prep((j + 2) % RING)
                for t in range(NT):
                    act.wait_ge(tm_sum, h * NT + t + 1)
                    nc.scalar.activation(tokv[3][:, 0, t, h * HALF:(h + 1) * HALF],
                                         work[:, t * HALF:(t + 1) * HALF], ACT.Copy).then_inc(tm_hi, 1)

            for mt in range(NT):
                acc_part(pt[:, 0, mt, :], everyone, 0.0)

            for n, b0 in enumerate((B_Q, B_K, B_V)):
                with repeat(act, 2, turn) as i:
                    for j in range(RING):
                        m = i * RING + j
                        acc_part(feat[1 + n][:, 0, bass.ds(m, 1), :], everyone, bias[:, bass.ds(m + b0, 1)])
                        prep((j + 2) % RING)

            for t in range(NT):
                act.wait_ge(tr_ready, NT + t + 1)
                nc.scalar.activation(feat[0][:, 0, :, t * P:(t + 1) * P], set_banks(t), ACT.Copy).then_inc(tr_hi, 1)

            acc_part(qp[:, 0, :], everyone, bias[:, B_IQ:B_IQ + 1])
            prep(slot_of(q_no.n))
            acc_part(kp[:, 0, :], everyone, bias[:, B_IK:B_IK + 1])
            prep(slot_of(q_no.n))

            for m in range(FHT):
                bank = acc.n % 2
                act.wait_ge(acc_free, acc.value)
                act.wait_ge(acc_ready, acc.add())
                nc.scalar.activation(gate, ps[:, bank, 0:N], ACT.Silu, bias=bias[:, B_G + m:B_G + m + 1])\
                    .then_inc(acc_free, 1)
                prep(slot_of(q_no.n))
                act.wait_ge(acc_free, acc.add())
                nc.scalar.activation(pt[:, 0, m, :], hid, ACT.Copy).then_inc(hid_hi, 1)
                prep(slot_of(q_no.n))
            acc.add()
            prep(slot_of(q_no.n))
            prep(slot_of(q_no.n))

            def values_hi():
                bank = acc.n % 2
                act.wait_ge(acc_ready, acc.add())
                nc.scalar.activation(vp[:, 0, :, :], ps[:, bank, 0:N].rearrange("p (t d) -> p t d", t=NT),
                                     ACT.Copy).then_inc(acc_hi, 1)

            act.wait_ge(down_ready, NT)
            prep(slot_of(q_no.n))
            values_hi()
            prep(slot_of(q_no.n))

            exp_no, pt_no = Tally(), Tally()

            def exps(s):
                act.wait_ge(s_max, exp_no.add())
                for t in range(NT):
                    nc.scalar.activation(probs[:, s, t, :], probs[:, s, t, :], ACT.Exp,
                                         bias=snm[:, s, t:t + 1], scale=DH ** -0.5,
                                         accum_out=ssum[:, s, t:t + 1]).then_inc(s_exp, 1)

            def pt_part(s):
                act.wait_ge(pt_ready, pt_no.add())
                nc.scalar.activation(pt[:, 0, :, :], ps[:, 2 + 3 * s:5 + 3 * s, 0:N], ACT.Copy).then_inc(pt_hi, 1)

            def head_rows(s):
                return slice(s * DH, (s + 1) * DH)

            def pair(p, last):
                exps(0)
                exps(1)
                acc_part(qp[:, 0, :], everyone, bias[:, bass.ds(p + B_IQ, 1)])
                prep(3)
                pt_part(0)
                acc_part(kp[:, 0, :], everyone, bias[:, bass.ds(p + B_IK, 1)])
                prep(0 if last else 1)
                acc_part(feat[0][head_rows(0), 0, bass.ds(p - 1, 1), :], head_rows(0), 0.0)
                pt_part(1)
                acc.add()
                prep(1 if last else 2)
                acc_part(feat[0][head_rows(1), 0, bass.ds(p - 1, 1), :], head_rows(1), 0.0)
                values_hi()

            with repeat(act, PAIRS - 2, {q_no: 3, acc: 6, exp_no: 2, pt_no: 2,
                                         used[1]: 16, used[2]: 16, used[3]: 16}) as i:
                pair(i + 1, False)
            pair(PAIRS - 1, True)
            exps(0)
            exps(1)
            for s in range(2):
                pt_part(s)
                acc_part(feat[0][head_rows(s), 0, PAIRS - 1, :], head_rows(s), 0.0)

            for q in range(Q_WO + 2, Q_MOE):
                prep(slot_of(q))
            act.wait_ge(b12_in, 16)
            nc.scalar.activation(b12r[:, 0, :], work[0:EXPERTS, 0:F + D], ACT.Copy).then_inc(b12_hi, 1)

            def prep_x(wait=True):
                slot = (q_no.n - Q_MOE + RING) % XRING
                act.wait_ge(raw_in[slot], used[slot].add(16))
                if wait:
                    act.wait_ge(w_started, q_no.value - (XRING - 2))
                nc.scalar.activation(split_of(slot, 0), raw_slot(slot), ACT.Copy).then_inc(w_hi, 1)
                q_no.add()

            for _ in range(RING):
                prep_x()
            act.wait_ge(wo_ready, 2 * NT)
            for _ in range(RING):
                prep_x(False)

            for t in range(NT):
                act.wait_ge(x2t_ready, t + 1)
                nc.scalar.activation(x2t[t], set_banks_row(t), ACT.Copy).then_inc(x2t_copied, 1)
            act.wait_ge(lmax_done, 1)
            for t in range(NT):
                sl = slice(t * EXPERTS, (t + 1) * EXPERTS)
                nc.scalar.activation(rt[:, R_EXP, sl], rt[:, R_LOGIT, sl], ACT.Exp,
                                     bias=rt[:, R_NMAX, t:t + 1], accum_out=rt[:, R_SUM, t:t + 1])\
                    .then_inc(lexp_done, 1)
            act.wait_ge(hott_ready, 1)
            nc.scalar.activation(pt[0:EXPERTS, 0, 0, :], ps[0:EXPERTS, 1, 0:N], ACT.Copy).then_inc(hott_copied, 1)

            xt, h_no, y_no, ht = Tally(2 * NT), Tally(), Tally(), Tally()

            def load_slot(s):
                row = s * P if isinstance(s, int) else act.snap(s * P)
                act.dma_start(rowbuf[:, 0, :], xs_dram[bass.ds(row, P), :]).then_inc(xs_in, 16)

            def split_slot():
                act.wait_ge(tr_ready, xt.add())
                nc.scalar.activation(xsp[:, 0, :], whole(2), ACT.Copy).then_inc(tr_hi, 1)

            def gelu():
                act.wait_ge(h_ready, h_no.add())
                nc.scalar.activation(h_buf, ps[:, 0, :], ACT.Gelu_apprx_tanh).then_inc(h_act, 1)

            def split_hidden():
                act.wait_ge(ht_ready, ht.add())
                nc.scalar.activation(hts[:, 0, :], ps[:, 1, :], ACT.Copy).then_inc(ht_hi, 1)

            def first_half_of_y(i):
                act.wait_ge(y_ready, y_no.add())
                if not isinstance(i, int) or i:
                    act.wait_ge(y_out, i * 16)
                nc.scalar.activation(y_buf[:, 0:HALF], ps[:, 4, :], ACT.Copy).then_inc(y_half0, 1)

            def store_y(i):
                row = i * P if isinstance(i, int) else act.snap(i * P)
                act.wait_ge(y_half0, y_no.value)
                act.wait_ge(y_half1, y_no.value)
                act.dma_start(ys_dram[bass.ds(row, P), :], y_buf).then_inc(y_out, 16)

            act.wait_ge(xs_out, 16 * NT)
            load_slot(0)
            split_slot()
            load_slot(1)
            gelu()
            split_slot()
            split_hidden()
            for _ in range(RING):
                prep_x()

            def slot_turn(i, ahead):
                if ahead:
                    load_slot(i + 2)
                gelu()
                if ahead:
                    split_slot()
                    for _ in range(RING):
                        prep_x()
                first_half_of_y(i)
                split_hidden()
                store_y(i)
                for _ in range(RING):
                    prep_x()

            slot_turn(0, True)
            with repeat(act, EXPERTS - 3, {q_no: QE, xt: 1, h_no: 1, y_no: 1, ht: 1,
                                           **{u: 16 for u in used}}) as i:
                slot_turn(i + 1, True)
            slot_turn(EXPERTS - 2, False)
            first_half_of_y(EXPERTS - 1)
            store_y(EXPERTS - 1)

            over = act.value_load(rowi[0:1, OVER:OVER + 1], min_val=0, max_val=OVER)
            with act.If(over > 0):
                for o in range(OVER):
                    load_slot(EXPERTS + o)
                    for _ in range(RING):
                        prep_x()
                    split_slot()
                    gelu()
                    split_hidden()
                    for _ in range(RING):
                        prep_x()
                    first_half_of_y(EXPERTS + o)
                    store_y(EXPERTS + o)

        @block.vector
        def _(dve):
            q_no, step = Tally(), Tally()
            acc, hi_no = Tally(), Tally()
            everyone = slice(0, P)

            def then(ins):
                ins.then_inc(dve_step, 1)
                dve.wait_ge(dve_step, step.add())

            def lo(dst, value, hi):
                return nc.vector.tensor_tensor(dst, value, hi.bitcast(F32), ALU.subtract)

            def prep(slot):
                dve.wait_ge(w_hi, q_no.add())
                lo(wsp[:, 1, slot, :], raw[:, slot, :], wsp[:, 0, slot, :]).then_inc(w_lo, 1)

            def acc_part(dst, hi, rows, b):
                bank = acc.n % 2
                acc.add()
                dve.wait_ge(acc_hi, hi_no.add())
                nc.vector.scalar_tensor_tensor(out=dst, in0=ps[rows, bank, 0:N], scalar=b, in1=hi.bitcast(F32),
                                               op0=ALU.add, op1=ALU.subtract).then_inc(acc_free, 1)

            def statistics(t):
                for c in range(2):
                    ins = nc.vector.bn_stats(stats[:, t, c, :], tok[:, t, c * HALF:(c + 1) * HALF])
                then(ins)
                nc.vector.bn_aggr(mv[:, t, :], stats[:, t, :, :].rearrange("p a b -> p (a b)"))\
                    .then_inc(stats_done, 1)

            turn = {q_no: RING, acc: RING, hi_no: RING}

            nc.vector.memset(ones_r[:].bitcast(F32), 1.0).then_inc(ones_set, 1)
            for t in range(NT):
                dve.wait_ge(x_in[t], 16)
                statistics(t)
            for t in range(NT):
                dve.wait_ge(rstd_done, t + 1)
                nc.vector.tensor_scalar(tok[:, t, :], tok[:, t, :], mv[:, t, 0:1], rs[:, t, 1:2],
                                        ALU.subtract, ALU.mult).then_inc(xn_done, 1)

            prep(0)
            prep(1)
            for t in range(NT):
                dve.wait_ge(tr_hi, t + 1)
                hi = feat[0][:, 0, :, t * P:(t + 1) * P]
                lo(feat[0][:, 1, :, t * P:(t + 1) * P], set_banks(t), hi).then_inc(tr_free, 1)

            dve.wait_ge(edge_in, 96)
            then(nc.vector.tensor_scalar(tw[:, 2, :], tw[:, 0, :], -1.0, None, ALU.mult))
            nc.vector.tensor_tensor(tw[:, 1, :], tw[:, 0, :], tw[:, 2, :], ALU.min).then_inc(tw_arg, 1)
            dve.wait_ge(tw_exp, 1)
            nc.vector.tensor_scalar(tw[:, 1, :], tw[:, 1, :], 1.0, None, ALU.add).then_inc(tw_one, 1)
            dve.wait_ge(tw_ln, 1)
            then(nc.vector.scalar_tensor_tensor(out=tw[:, 2, :], in0=tw[:, 0, :], scalar=0.0, in1=tw[:, 1, :],
                                                op0=ALU.max, op1=ALU.add))
            nc.vector.tensor_scalar(tw[:, 3, :], tw[:, 2, :], DH ** 0.5, None, ALU.mult).then_inc(tw_done, 1)
            dve.wait_ge(tw_done, 1)
            then(nc.vector.scalar_tensor_tensor(out=ef[:, 0, :], in0=ei[:, 0, :], scalar=float(N), in1=ei[:, 1, :],
                                                op0=ALU.mult, op1=ALU.add))
            for k, w in ((0, 3), (1, 0), (2, 1), (3, 2), (4, 3)):
                dst = ef[:, 3, :] if k == 0 else ef[:, 1, :]
                then(nc.vector.tensor_scalar(dst, ei[:, 2, :], float(k), tw[:, 3, w:w + 1], ALU.is_equal, ALU.mult))
                if k:
                    then(nc.vector.tensor_tensor(ef[:, 3, :], ef[:, 3, :], ef[:, 1, :], ALU.add))

            parts, elus, pieces = Tally(), Tally(), Tally()
            piece_no = [Tally(), Tally()]

            def elu_step(big, m, j, c):
                acc.add()
                dve.wait_ge(elu_parts, parts.add(2))
                if elus.i is not None or elus.n:
                    dve.wait_ge(elu_lo, elus.value)
                nc.vector.scalar_tensor_tensor(out=elu_s, in0=elu_e, scalar=1.0, in1=elu_r,
                                               op0=ALU.min, op1=ALU.add).then_inc(acc_free, 1)
                prep((j + 2) % RING)
                dve.wait_ge(elu_hi, elus.add())
                lo(feat[big][:, 1, bass.ds(m, 1), :], elu_s, feat[big][:, 0, bass.ds(m, 1), :]).then_inc(elu_lo, 1)
                buf = j % 2
                dve.wait_ge(piece_in[buf], piece_no[buf].add(32))
                then(nc.vector.scalar_tensor_tensor(out=codes, in0=edge_rows[buf][:, 0, :], scalar=float(N),
                                                    in1=edge_rows[buf][:, 1, :], op0=ALU.mult, op1=ALU.add))
                for k in range(GROUP):
                    ins = nc.vector.scalar_tensor_tensor(
                        out=junk[k][:, k * P:N], in0=codes[:, k * P:N], scalar=ef[:, 0, bass.ds(c + k, 1)],
                        in1=maskb[:, k, k * P:N], op0=ALU.is_equal, op1=ALU.mult,
                        accum_out=dup[:, bass.ds(c + k, 1)])
                ins.then_inc(piece_done, 1)
                dve.wait_ge(piece_done, pieces.add())

            dve.wait_ge(later_in, 16)
            elu_turn = {q_no: RING, acc: RING, parts: 2 * RING, elus: RING, pieces: RING, step: RING,
                        piece_no[0]: 64, piece_no[1]: 64}
            for j in range(RING):
                elu_step(1, j, j, j * GROUP)
            with repeat(dve, 1, elu_turn) as i:
                for j in range(RING):
                    elu_step(1, i * RING + (RING + j), j, i * (RING * GROUP) + (RING + j) * GROUP)
            with repeat(dve, 2, elu_turn) as i:
                for j in range(RING):
                    elu_step(2, i * RING + j, j, i * (RING * GROUP) + (2 * RING + j) * GROUP)

            then(nc.vector.tensor_scalar(ef[:, 1, :], dup[:], 0.0, None, ALU.is_gt))
            then(nc.vector.tensor_scalar(ef[:, 2, :], spare, 1.0, None, ALU.mult))
            then(nc.vector.tensor_tensor(ef[:, 2, :], ef[:, 2, :], ef[:, 0, :], ALU.subtract))
            then(nc.vector.tensor_tensor(ef[:, 2, :], ef[:, 2, :], ef[:, 1, :], ALU.mult))
            nc.vector.tensor_tensor(eidx[:], ef[:, 2, :], ef[:, 0, :], ALU.add).then_inc(edges_done, 1)

            for h in range(2):
                for j in range(RING):
                    prep((j + 2) % RING)
                if h == 0:
                    dve.wait_ge(b_row_in, 16)
                else:
                    dve.wait_ge(tm_lo, NT)
                for t in range(NT):
                    dve.wait_ge(tm_ready, h * NT + t + 1)
                    nc.vector.tensor_tensor(work[:, t * HALF:(t + 1) * HALF], ps[:, 2 + 3 * h + t, :],
                                            rowbuf[:, 1, h * HALF:(h + 1) * HALF], ALU.add).then_inc(tm_sum, 1)
                for t in range(NT):
                    dve.wait_ge(tm_hi, h * NT + t + 1)
                    cols_h = slice(h * HALF, (h + 1) * HALF)
                    lo(tokv[3][:, 1, t, cols_h], work[:, t * HALF:(t + 1) * HALF], tokv[3][:, 0, t, cols_h])\
                        .then_inc(tm_lo, 1)

            for mt in range(NT):
                acc_part(pt[:, 1, mt, :], pt[:, 0, mt, :], everyone, 0.0)

            for t in range(NT):
                b = 2 + 3 * (t % 2)
                dve.wait_ge(num_ready, t + 1)
                then(nc.vector.tensor_scalar(den[:, 2 * t:2 * t + 1], ps[:, b + 2, 0:1], 1e-6, None, ALU.add))
                then(nc.vector.reciprocal(den[:, 2 * t + 1:2 * t + 2], den[:, 2 * t:2 * t + 1]))
                nc.vector.scalar_tensor_tensor(out=tok[:, t, :], in0=whole(b), scalar=den[:, 2 * t + 1:2 * t + 2],
                                               in1=tok[:, t, :], op0=ALU.mult, op1=ALU.add).then_inc(num_free, 1)
                dve.wait_ge(num_free, t + 1)
                statistics(t)

            for n, b0 in enumerate((B_Q, B_K, B_V)):
                with repeat(dve, 2, turn) as i:
                    for j in range(RING):
                        m = i * RING + j
                        acc_part(feat[1 + n][:, 1, bass.ds(m, 1), :], feat[1 + n][:, 0, bass.ds(m, 1), :],
                                 everyone, bias[:, bass.ds(m + b0, 1)])
                        prep((j + 2) % RING)

            for t in range(NT):
                dve.wait_ge(tr_hi, NT + t + 1)
                hi = feat[0][:, 0, :, t * P:(t + 1) * P]
                lo(feat[0][:, 1, :, t * P:(t + 1) * P], set_banks(t), hi).then_inc(tr_free, 1)

            acc_part(qp[:, 1, :], qp[:, 0, :], everyone, bias[:, B_IQ:B_IQ + 1])
            prep(slot_of(q_no.n))
            acc_part(kp[:, 1, :], kp[:, 0, :], everyone, bias[:, B_IK:B_IK + 1])
            prep(slot_of(q_no.n))

            for m in range(FHT):
                prep(slot_of(q_no.n))
                acc.add()
                bank = acc.n % 2
                dve.wait_ge(acc_free, acc.value)
                if m:
                    dve.wait_ge(hid_lo, m)
                dve.wait_ge(acc_ready, acc.add())
                nc.vector.scalar_tensor_tensor(out=hid, in0=ps[:, bank, 0:N], scalar=bias[:, B_U + m:B_U + m + 1],
                                               in1=gate, op0=ALU.add, op1=ALU.mult).then_inc(acc_free, 1)
                prep(slot_of(q_no.n))
                dve.wait_ge(hid_hi, m + 1)
                lo(pt[:, 1, m, :], hid, pt[:, 0, m, :]).then_inc(hid_lo, 1)

            def values(p):
                bank = acc.n % 2
                dve.wait_ge(acc_ready, acc.add())
                nc.vector.tensor_scalar(vt, ps[:, bank, 0:N], bias[:, bass.ds(p + B_IV, 1)], None, ALU.add)\
                    .then_inc(acc_free, 1)

            def values_lo():
                acc_part(vp[:, 1, :, :].rearrange("p t d -> p (t d)"), vp[:, 0, :, :].rearrange("p t d -> p (t d)"),
                         everyone, 0.0)

            prep(slot_of(q_no.n))
            values(0)
            prep(slot_of(q_no.n))
            for t in range(NT):
                dve.wait_ge(bd_added, t + 1)
                dve.wait_ge(down_ready, t + 1)
                nc.vector.tensor_tensor(tok[:, t, :], tok[:, t, :], whole(2 + 2 * t), ALU.add).then_inc(down_sum, 1)
            prep(slot_of(q_no.n))
            values_lo()
            prep(slot_of(q_no.n))

            s_no, exp_no, norm_no, pt_no = Tally(), Tally(), Tally(), Tally()

            def maxima(s):
                dve.wait_ge(s_ready, s_no.value)
                nc.vector.memset(waited[:], 0.0)
                for t in range(NT):
                    ins = nc.vector.tensor_tensor_reduce(
                        out=probs[:, s, t, :], in0=ps[:, 2 + 3 * s + t, 0:N], in1=maskb[:, t, :], scale=1.0,
                        scalar=3.0 * NONE, op0=ALU.add, op1=ALU.max, accum_out=smx[:, s, t:t + 1])
                then(ins)
                nc.vector.tensor_scalar(snm[:, s, :], smx[:, s, :], -DH ** -0.5, None, ALU.mult).then_inc(s_max, 1)

            def normalise(s):
                dve.wait_ge(s_exp, exp_no.add(NT))
                then(nc.vector.reciprocal(sinv[:, s, :], ssum[:, s, :]))
                for t in range(NT):
                    ins = nc.vector.tensor_scalar(probs[:, s, t, :], probs[:, s, t, :], sinv[:, s, t:t + 1],
                                                  None, ALU.mult)
                ins.then_inc(s_norm, 1)

            def pt_part(s):
                dve.wait_ge(pt_hi, pt_no.add())
                lo(pt[:, 1, :, :], ps[:, 2 + 3 * s:5 + 3 * s, 0:N], pt[:, 0, :, :]).then_inc(pt_lo, 1)

            def head_rows(s):
                return slice(s * DH, (s + 1) * DH)

            def out_part(s, p):
                f = feat[0][head_rows(s), :, bass.ds(p, 1), :]
                acc_part(f[:, 1, :, :], f[:, 0, :, :], head_rows(s), 0.0)

            def pair(p, last):
                normalise(0)
                acc_part(qp[:, 1, :], qp[:, 0, :], everyone, bias[:, bass.ds(p + B_IQ, 1)])
                prep(3)
                normalise(1)
                pt_part(0)
                acc_part(kp[:, 1, :], kp[:, 0, :], everyone, bias[:, bass.ds(p + B_IK, 1)])
                prep(0 if last else 1)
                out_part(0, p - 1)
                pt_part(1)
                values(p)
                prep(1 if last else 2)
                out_part(1, p - 1)
                values_lo()
                s_no.add()
                maxima(0)
                maxima(1)

            dve.wait_ge(mask_in, 16)
            s_no.add()
            maxima(0)
            maxima(1)
            for t in range(NT):
                dve.wait_ge(down_sum, t + 1)
                statistics(t)
            with repeat(dve, PAIRS - 2, {q_no: 3, acc: 6, hi_no: 5, s_no: 1, exp_no: 2 * NT, pt_no: 2,
                                         step: 4}) as i:
                pair(i + 1, False)
            pair(PAIRS - 1, True)
            normalise(0)
            normalise(1)
            for s in range(2):
                pt_part(s)
                out_part(s, PAIRS - 1)

            for h in range(2):
                for j in range(RING):
                    if q_no.n < Q_MOE:
                        prep(slot_of(q_no.n))
                for t in range(NT):
                    if h == 0:
                        dve.wait_ge(mix_done, t + 1)
                    dve.wait_ge(wo_ready, h * NT + t + 1)
                    row = tok[:, t, h * HALF:(h + 1) * HALF]
                    nc.vector.tensor_tensor(row, row, ps[:, 2 + 3 * h + t, :], ALU.add).then_inc(wo_sum, 1)
                    dve.wait_ge(wo_sum, h * NT + t + 1)
                    ins = nc.vector.bn_stats(stats[:, t, h, :], row)
                    if h:
                        then(ins)
                        nc.vector.bn_aggr(mv[:, t, :], stats[:, t, :, :].rearrange("p a b -> p (a b)"))\
                            .then_inc(stats_done, 1)
                if h == 0:
                    dve.wait_ge(b12_hi, 1)
                    lo(b12r[:, 1, :], work[0:EXPERTS, 0:F + D], b12r[:, 0, :]).then_inc(b12_lo, 1)

            def prep_x():
                slot = (q_no.n - Q_MOE + RING) % XRING
                dve.wait_ge(w_hi, q_no.add())
                lo(split_of(slot, 1), raw_slot(slot), split_of(slot, 0)).then_inc(w_lo, 1)

            dve.wait_ge(b12_lo, 1)
            for t in range(NT):
                dve.wait_ge(rstd_done, 3 * NT + t + 1)
                nc.vector.tensor_scalar(x2[t], tok[:, t, :], mv[:, t, 0:1],
                                        rs[:, t, 1:2], ALU.subtract, ALU.mult).then_inc(x2_done, 1)
            for _ in range(2 * RING):
                prep_x()

            def tile3(k):
                return rt[:, k, :].rearrange("p (t e) -> p t e", t=NT)

            def spread(a):
                return a.unsqueeze(2).to_broadcast([P, NT, EXPERTS])

            w8 = cst[:, C_W8:C_W8 + EXPERTS].unsqueeze(1).to_broadcast([P, NT, EXPERTS])
            dve.wait_ge(logits_ready, NT)
            then(nc.vector.tensor_tensor(rt[:, R_LOGIT, :], ps[:, 0, 0:NT * EXPERTS], sbias[:], ALU.add))
            then(nc.vector.reduce_max(rt[:, R_MAX, 0:NT], tile3(R_LOGIT), AX_X))
            nc.vector.tensor_scalar(rt[:, R_NMAX, 0:NT], rt[:, R_MAX, 0:NT], -1.0, None, ALU.mult)\
                .then_inc(lmax_done, 1)
            then(nc.vector.tensor_tensor(tile3(R_HOT), tile3(R_LOGIT), spread(rt[:, R_MAX, 0:NT]), ALU.is_equal))
            then(nc.vector.tensor_tensor(tile3(R_HOT), tile3(R_HOT), w8, ALU.mult))
            then(nc.vector.reduce_max(rt[:, R_FIRST, 0:NT], tile3(R_HOT), AX_X))
            nc.vector.tensor_tensor(tile3(R_HOT), tile3(R_HOT), spread(rt[:, R_FIRST, 0:NT]), ALU.is_equal)\
                .then_inc(hot_done, 1)
            for k in range(4):
                ins = nc.vector.memset(cum[:, k, 0:4], 0.0)
            then(ins)
            then(nc.vector.tensor_scalar(slote[:, 1, 0:EXPERTS], cst[:, C_EID:C_EID + EXPERTS], 1.0, None, ALU.mult))
            dve.wait_ge(count_ready, 1)
            n_e = ps[:, 6, NT * EXPERTS:(NT + 1) * EXPERTS]
            nblk = cum[:, 0, 4:12]
            then(nc.vector.tensor_scalar(rt[:, R_TOTAL, 0:EXPERTS], n_e, 0.0, None, ALU.add))
            tot = rt[:, R_TOTAL, 0:EXPERTS]
            then(nc.vector.tensor_scalar(nblk, tot, float(P), None, ALU.is_gt))
            for k in range(2, OVER + 1):
                then(nc.vector.scalar_tensor_tensor(out=nblk, in0=tot, scalar=float(k * P), in1=nblk,
                                                    op0=ALU.is_gt, op1=ALU.add))
            for k in range(3):
                sh = 1 << k
                then(nc.vector.tensor_tensor(cum[:, k + 1, 4:12], cum[:, k, 4:12], cum[:, k, 4 - sh:12 - sh], ALU.add))
            end = cum[:, 3, 4:12]
            first = rt[:, R_FIRST, 0:EXPERTS]
            eid = cst[:, C_EID:C_EID + EXPERTS]

            def every_token(a):
                return a.unsqueeze(1).to_broadcast([P, NT, EXPERTS])

            then(nc.vector.tensor_tensor(first, end, nblk, ALU.subtract))
            then(nc.vector.tensor_tensor(first, first, eid, ALU.subtract))
            then(nc.vector.tensor_scalar(first, first, float(EXPERTS - 1), float(P), ALU.add, ALU.mult))
            then(nc.vector.tensor_scalar(rt[:, R_FIRST, EXPERTS:2 * EXPERTS], eid, float(P), None, ALU.mult))
            cnt = ps[:, 6, 0:NT * EXPERTS]
            then(nc.vector.tensor_scalar(rt[:, R_RANK, :], cnt, float(P), None, ALU.is_ge))
            then(nc.vector.tensor_tensor(tile3(R_RANK), tile3(R_RANK), every_token(first), ALU.mult))
            then(nc.vector.tensor_tensor(tile3(R_RANK), tile3(R_RANK),
                                         every_token(rt[:, R_FIRST, EXPERTS:2 * EXPERTS]), ALU.add))
            then(nc.vector.tensor_tensor(rt[:, R_RANK, :], rt[:, R_RANK, :], cnt, ALU.add))
            then(nc.vector.tensor_tensor(tile3(R_RANK), tile3(R_RANK), tile3(R_HOT), ALU.mult))
            then(nc.vector.reduce_sum(rt[:, R_POS, 0:NT], tile3(R_RANK), AX_X))
            nc.vector.tensor_copy(posi[:], rt[:, R_POS, 0:NT]).then_inc(pos_done, 1)
            over = slote[:, 0, 0:OVER]
            slots = cst[:, C_SLOT:C_SLOT + OVER * EXPERTS].rearrange("p (s e) -> p s e", s=OVER)
            then(nc.vector.tensor_tensor(slotc[:], end.unsqueeze(1).to_broadcast([P, OVER, EXPERTS]), slots,
                                         ALU.is_le))
            then(nc.vector.reduce_sum(over, slotc[:], AX_X))
            then(nc.vector.tensor_scalar(slote[:, 1, EXPERTS:SLOTS], over, float(EXPERTS - 1), None, ALU.min))
            then(nc.vector.tensor_scalar(slote[:, 2, :], slote[:, 1, :], cst[:, C_EXP:C_EXP + 1], None, ALU.is_equal))
            then(nc.vector.tensor_scalar(rowi[:, 0:OVER], slote[:, 1, EXPERTS:SLOTS], float(QE * P), None, ALU.mult))
            nc.vector.tensor_copy(rowi[:, OVER:OVER + 1], cum[:, 3, 11:12]).then_inc(route_done, 1)
            dve.wait_ge(lexp_done, NT)
            then(nc.vector.reciprocal(rt[:, R_PROB, 0:NT], rt[:, R_SUM, 0:NT]))
            for t in range(NT):
                dve.wait_ge(b2_ready, t + 1)
                nc.vector.scalar_tensor_tensor(out=tok[:, t, :], in0=whole(4), scalar=rt[:, R_PROB, t:t + 1],
                                               in1=tok[:, t, :], op0=ALU.mult, op1=ALU.add).then_inc(b2_added, 1)

            xt, y_no, ht, slot_no = Tally(2 * NT), Tally(), Tally(), Tally()

            def hot_slot(s):
                nc.vector.tensor_copy(slot_hot[0:EXPERTS, :],
                                      slote[0:EXPERTS, 2, bass.ds(s, 1)].to_broadcast([EXPERTS, P]))\
                    .then_inc(slot_set, 1)

            def split_slot():
                dve.wait_ge(tr_hi, xt.add())
                lo(xsp[:, 1, :], whole(2), xsp[:, 0, :]).then_inc(tr_free, 1)

            def split_hidden():
                dve.wait_ge(ht_hi, ht.add())
                lo(hts[:, 1, :], ps[:, 1, :], hts[:, 0, :]).then_inc(ht_lo, 1)

            def second_half_of_y(i):
                dve.wait_ge(y_ready, y_no.add())
                if not isinstance(i, int) or i:
                    dve.wait_ge(y_out, i * 16)
                nc.vector.tensor_copy(y_buf[:, HALF:D], ps[:, 5, :]).then_inc(y_half1, 1)

            hot_slot(0)
            split_slot()
            split_slot()
            dve.wait_ge(h_ready, 1)
            hot_slot(1)
            split_hidden()
            for _ in range(RING):
                prep_x()

            def slot_turn(i, ahead):
                if ahead:
                    split_slot()
                    for _ in range(RING):
                        prep_x()
                    dve.wait_ge(h_ready, hot_no.add())
                    hot_slot(i + 2)
                second_half_of_y(i)
                split_hidden()
                for _ in range(RING):
                    prep_x()

            hot_no = Tally(1)
            slot_turn(0, True)
            with repeat(dve, EXPERTS - 3, {q_no: QE, xt: 1, y_no: 1, ht: 1, hot_no: 1}) as i:
                slot_turn(i + 1, True)
            slot_turn(EXPERTS - 2, False)
            second_half_of_y(EXPERTS - 1)

            over = dve.value_load(rowi[0:1, OVER:OVER + 1], min_val=0, max_val=OVER)
            with dve.If(over > 0):
                for o in range(OVER):
                    for _ in range(RING):
                        prep_x()
                    split_slot()
                    dve.wait_ge(h_ready, hot_no.add())
                    hot_slot(EXPERTS + o)
                    split_hidden()
                    for _ in range(RING):
                        prep_x()
                    second_half_of_y(EXPERTS + o)

            dve.wait_ge(b2_added, NT)
            for t in range(NT):
                dve.wait_ge(yg_in[t], 16)
                nc.vector.scalar_tensor_tensor(out=tok[:, t, :], in0=x2[t], scalar=rt[:, R_PROB, t:t + 1],
                                               in1=tok[:, t, :], op0=ALU.mult, op1=ALU.add).then_inc(sum_done, 1)

        @block.tensor
        def _(pe):
            q_no, acc = Tally(), Tally()

            def open_quarter():
                pe.wait_ge(w_lo, q_no.add())

            def open_acc():
                bank = acc.n % 2
                if acc.i is not None or acc.n >= 2:
                    pe.wait_ge(acc_free, acc.value - 1)
                acc.add()
                return bank

            def feature_major(slot, moving):
                open_quarter()
                bank = open_acc()
                for k in range(KT):
                    for n, (a, b) in enumerate(PASSES):
                        ins = nc.tensor.matmul(ps[:, bank, 0:N], wsp[:, a, slot, k * P:(k + 1) * P],
                                               moving[:, b, k, :], start=(k == 0 and n == 0),
                                               stop=(k == KT - 1 and n == 2))
                        if k == 0 and n == 0:
                            ins.then_inc(w_started, 1)
                ins.then_inc(acc_ready, 1)

            def token_major(slot, j, stationary, banks, ready):
                open_quarter()
                for t in range(NT):
                    for kk in range(2):
                        k = 2 * j + kk
                        for n, (a, b) in enumerate(PASSES):
                            ins = nc.tensor.matmul(ps[:, banks + t, :], stationary[:, b, k, t * P:(t + 1) * P],
                                                   wsp[:, a, slot, kk * HALF:(kk + 1) * HALF],
                                                   start=(k == 0 and n == 0), stop=(k == KT - 1 and n == 2))
                            if t == 0 and kk == 0 and n == 0:
                                ins.then_inc(w_started, 1)
                    if j == 3:
                        ins.then_inc(ready, 1)

            turn = {q_no: RING, acc: RING}

            pe.wait_ge(const_in, 32)
            for t in range(NT):
                pe.wait_ge(xn_done, t + 1)
                for k in range(KT):
                    ins = nc.tensor.transpose(set_banks(t)[:, k, :], tok[:, t, k * P:(k + 1) * P], ident)
                ins.then_inc(tr_ready, 1)
            pe.wait_ge(tr_free, NT)

            for m in range(1):
                for j in range(RING):
                    feature_major(j, feat[0])
            with repeat(pe, 3, turn):
                for j in range(RING):
                    feature_major(j, feat[0])
            for h in range(2):
                for j in range(RING):
                    token_major(j, j, feat[0], 2 + 3 * h, tm_ready)

            pe.wait_ge(elu_lo, 2 * KT)
            for mt in range(NT):
                bank = open_acc()
                for k in range(KT):
                    for n, (a, b) in enumerate(PASSES):
                        ins = nc.tensor.matmul(ps[:, bank, 0:N], feat[2][:, a, k, mt * P:(mt + 1) * P],
                                               feat[1][:, b, k, :], start=(k == 0 and n == 0),
                                               stop=(k == KT - 1 and n == 2))
                ins.then_inc(acc_ready, 1)
            pe.wait_ge(acc_free, acc.value)
            pe.wait_ge(tm_lo, 2 * NT)
            pe.wait_ge(ones_set, 1)
            for t in range(NT):
                b0 = 2 + 3 * (t % 2)
                if t == 2:
                    pe.wait_ge(num_free, 1)
                for mt in range(NT):
                    for a in range(2):
                        nc.tensor.matmul(ps[:, b0 + 2, 0:2], pt[:, a, mt, t * P:(t + 1) * P], ones_r[:],
                                         start=(mt == 0 and a == 0), stop=(mt == NT - 1 and a == 1))
                for h in range(2):
                    for mt in range(NT):
                        for n, (a, b) in enumerate(PASSES):
                            ins = nc.tensor.matmul(ps[:, b0 + h, :], pt[:, a, mt, t * P:(t + 1) * P],
                                                   tokv[3][:, b, mt, h * HALF:(h + 1) * HALF],
                                                   start=(mt == 0 and n == 0), stop=(mt == NT - 1 and n == 2))
                ins.then_inc(num_ready, 1)

            for _ in range(3):
                with repeat(pe, 2, turn):
                    for j in range(RING):
                        feature_major(j, feat[0])

            pe.wait_ge(num_free, NT)
            for t in range(NT):
                pe.wait_ge(x1_done, t + 1)
                for k in range(KT):
                    ins = nc.tensor.transpose(set_banks(t)[:, k, :], tok[:, t, k * P:(k + 1) * P], ident)
                ins.then_inc(tr_ready, 1)
            feature_major(slot_of(Q_PAIR0), feat[1])
            feature_major(slot_of(Q_PAIR0 + 1), feat[2])
            pe.wait_ge(tr_free, 2 * NT)
            feature_major(slot_of(Q_GU), feat[0])
            for q in range(Q_GU + 1, Q_DOWN - 1):
                feature_major(slot_of(q), feat[0])
            feature_major(slot_of(Q_DOWN - 1), feat[3])
            values_acc = acc.value
            pe.wait_ge(hid_lo, FHT)
            for t in range(NT):
                for h in range(2):
                    for k in range(FHT):
                        blk = h * FHT + k
                        slot, kk = slot_of(Q_DOWN + blk // 2), blk % 2
                        if t == 0 and kk == 0:
                            open_quarter()
                        for n, (a, b) in enumerate(PASSES):
                            ins = nc.tensor.matmul(ps[:, 2 + 2 * t + h, :], pt[:, b, k, t * P:(t + 1) * P],
                                                   wsp[:, a, slot, kk * HALF:(kk + 1) * HALF],
                                                   start=(k == 0 and n == 0), stop=(k == FHT - 1 and n == 2))
                            if t == 0 and n == 0 and kk == 0:
                                ins.then_inc(w_started, 1)
                ins.then_inc(down_ready, 1)

            pt_no, norm_no, s_no = Tally(), Tally(), Tally()

            def transpose_probs(s):
                pe.wait_ge(s_norm, norm_no.add())
                for mt in range(NT):
                    for t in range(NT):
                        ins = nc.tensor.transpose(ps[:, 2 + 3 * s + mt, t * P:(t + 1) * P],
                                                  probs[:, s, t, mt * P:(mt + 1) * P], ident)
                ins.then_inc(pt_ready, 1)

            def attend(s):
                pe.wait_ge(pt_lo, pt_no.add())
                bank = open_acc()
                for mt in range(NT):
                    for n, (a, b) in enumerate(PASSES):
                        ins = nc.tensor.matmul(ps[:, bank, 0:N], vp[:, a, mt, :], pt[:, b, mt, :],
                                               start=(mt == 0 and n == 0), stop=(mt == NT - 1 and n == 2))
                ins.then_inc(acc_ready, 1)

            def scores():
                for t in range(NT):
                    for n, (a, b) in enumerate(PASSES):
                        for s in range(2):
                            rows = slice(s * DH, (s + 1) * DH)
                            ins = nc.tensor.matmul(ps[:, 2 + 3 * s + t, 0:N], qp[rows, a, t * P:(t + 1) * P],
                                                   kp[rows, b, :], start=(n == 0), stop=(n == 2))
                ins.then_inc(s_ready, 1)

            def transpose_values():
                bank = open_acc()
                for mt in range(NT):
                    ins = nc.tensor.transpose(ps[:, bank, mt * P:(mt + 1) * P], vt[:, mt * P:(mt + 1) * P], ident)
                ins.then_inc(acc_ready, 1)

            def pair():
                feature_major(1, feat[1])
                transpose_probs(0)
                feature_major(2, feat[2])
                attend(0)
                transpose_probs(1)
                feature_major(3, feat[3])
                attend(1)
                pe.wait_ge(acc_free, acc.value - 1)
                transpose_values()
                scores()

            pe.wait_ge(acc_free, values_acc)
            transpose_values()
            pe.wait_ge(down_sum, NT)
            scores()
            with repeat(pe, PAIRS - 2, {q_no: 3, acc: 6, norm_no: 2, pt_no: 2}):
                pair()
            pair()
            for s in range(2):
                transpose_probs(s)
                if s == 0:
                    pe.wait_ge(acc_free, acc.value)
                attend(s)

            pe.wait_ge(acc_free, acc.value)
            for h in range(2):
                for j in range(RING):
                    token_major(j, j, feat[0], 2 + 3 * h, wo_ready)

            pe.wait_ge(wo_sum, 2 * NT)
            for t in range(NT):
                pe.wait_ge(x2_done, t + 1)
                for k in range(KT):
                    ins = nc.tensor.transpose(set_banks(t)[:, k, :], x2[t][:, k * P:(k + 1) * P], ident)
                ins.then_inc(x2t_ready, 1)
            for t in range(NT):
                pe.wait_ge(x2t_copied, t + 1)
                for k in range(KT):
                    ins = nc.tensor.matmul(ps[:, 0, t * EXPERTS:(t + 1) * EXPERTS], x2t[t][:, k * P:(k + 1) * P],
                                           swt[:, k, :], start=(k == 0), stop=(k == KT - 1))
                ins.then_inc(logits_ready, 1)
            hot = rt[:, R_HOT, :]
            pe.wait_ge(hot_done, 1)
            for t in range(NT):
                for u in range(t + 1):
                    nc.tensor.matmul(ps[:, 6, t * EXPERTS:(t + 1) * EXPERTS], tri if u == t else ones,
                                     hot[:, u * EXPERTS:(u + 1) * EXPERTS], start=(u == 0), stop=(u == t))
            for u in range(NT):
                ins = nc.tensor.matmul(ps[:, 6, NT * EXPERTS:(NT + 1) * EXPERTS], ones,
                                       hot[:, u * EXPERTS:(u + 1) * EXPERTS], start=(u == 0), stop=(u == NT - 1))
            ins.then_inc(count_ready, 1)
            for t in range(NT):
                ins = nc.tensor.transpose(ps[0:EXPERTS, 1, t * P:(t + 1) * P],
                                          hot[:, t * EXPERTS:(t + 1) * EXPERTS], ident)
            ins.then_inc(hott_ready, 1)
            pe.wait_ge(hott_copied, 1)
            for t in range(NT):
                if t:
                    pe.wait_ge(b2_added, t)
                for h in range(2):
                    for b in range(2):
                        ins = nc.tensor.matmul(ps[:, 4 + h, :], pt[0:EXPERTS, 0, 0, t * P:(t + 1) * P],
                                               b12r[:, b, F + h * HALF:F + (h + 1) * HALF],
                                               start=(b == 0), stop=(b == 1))
                ins.then_inc(b2_ready, 1)
            pe.wait_ge(b2_added, NT)

            xs_no, xt, slot_no, h_act_no, ht_no, y_no = Tally(), Tally(2 * NT), Tally(), Tally(), Tally(), Tally()
            xst = xsp[:].rearrange("p h (k n) -> p h k n", k=KT)
            htk = hts.rearrange("p h (k n) -> p h k n", k=F // P)

            def load_tokens():
                pe.wait_ge(xs_in, xs_no.add(16))
                for k in range(KT):
                    ins = nc.tensor.transpose(whole(2)[:, k * P:(k + 1) * P], rowbuf[:, 0, k * P:(k + 1) * P], ident)
                ins.then_inc(tr_ready, 1)

            def up(first, base):
                pe.wait_ge(tr_free, xt.add())
                if not first:
                    pe.wait_ge(h_act, h_act_no.add())
                for j in range(4):
                    open_quarter()
                    for kk in range(2):
                        k = 2 * j + kk
                        for n, (a, b) in enumerate(PASSES):
                            ins = nc.tensor.matmul(ps[:, 0, :], xst[:, b, k, :],
                                                   split_of(base + j, a)[:, kk * HALF:(kk + 1) * HALF],
                                                   start=(k == 0 and n == 0), stop=False)
                            if kk == 0 and n == 0:
                                ins.then_inc(w_started, 1)
                pe.wait_ge(slot_set, slot_no.add())
                for b in range(2):
                    ins = nc.tensor.matmul(ps[:, 0, :], slot_hot[0:EXPERTS, :], b12r[:, b, 0:F],
                                           start=False, stop=(b == 1))
                ins.then_inc(h_ready, 1)

            def down(first, base):
                pe.wait_ge(ht_lo, ht_no.add())
                if not first:
                    pe.wait_ge(y_half0, y_no.add())
                    pe.wait_ge(y_half1, y_no.value)
                for j in range(4):
                    open_quarter()
                    h = j // 2
                    for kk in range(2):
                        k = 2 * (j % 2) + kk
                        for n, (a, b) in enumerate(PASSES):
                            ins = nc.tensor.matmul(ps[:, 4 + h, :], htk[:, b, k, :],
                                                   split_of(base + j, a)[:, kk * HALF:(kk + 1) * HALF],
                                                   start=(k == 0 and n == 0), stop=(k == 3 and n == 2))
                            if kk == 0 and n == 0:
                                ins.then_inc(w_started, 1)
                ins.then_inc(y_ready, 1)

            def transpose_hidden():
                pe.wait_ge(h_act, h_act_no.value + 1)
                for k in range(F // P):
                    ins = nc.tensor.transpose(ps[:, 1, k * P:(k + 1) * P], h_buf[:, k * P:(k + 1) * P], ident)
                ins.then_inc(ht_ready, 1)

            load_tokens()
            up(True, RING)
            load_tokens()
            transpose_hidden()

            def slot_turn(first, ahead):
                up(False, 0)
                if ahead:
                    load_tokens()
                down(first, RING)
                transpose_hidden()

            slot_turn(True, True)
            with repeat(pe, EXPERTS - 3, {q_no: QE, xs_no: 16, xt: 1, slot_no: 1, h_act_no: 1, ht_no: 1, y_no: 1}):
                slot_turn(False, True)
            slot_turn(False, False)
            down(False, 0)

            over = pe.value_load(rowi[0:1, OVER:OVER + 1], min_val=0, max_val=OVER)
            with pe.If(over > 0):
                for o in range(OVER):
                    load_tokens()
                    up(False, RING)
                    transpose_hidden()
                    down(False, 0)


def _feature_quarters(w):
    k, n = w.shape
    return w.reshape(k // 128, 128, n // 128, 128).transpose(2, 1, 0, 3).reshape(-1, 1024)


def _token_quarters(w):
    k, n = w.shape
    return w.reshape(k // 256, 2, 128, n // 512, 512).transpose(3, 0, 2, 1, 4).reshape(-1, 1024)


def kernel(**inputs):
    import numpy as _np
    import concourse.bacc as _bacc
    from concourse import mybir as _mybir
    from concourse.bass_utils import run_bass_kernel_spmd as _run

    a = {k: _np.asarray(v) for k, v in inputs.items()}
    f32 = _np.float32
    g = lambda name: a["L0_gnn_" + name]
    mx = lambda name: a["L0_mix_" + name]
    ff = lambda name: a["L0_ffn_" + name]

    pad = FHT * P - FH
    wqkv = mx("Wqkv")
    wg = _np.pad(mx("Wg"), ((0, 0), (0, pad)))
    wu = _np.pad(mx("Wu"), ((0, 0), (0, pad)))
    gate_up = _np.stack([_feature_quarters(wg).reshape(FHT, P, D), _feature_quarters(wu).reshape(FHT, P, D)], 1)
    wd = _np.pad(mx("Wd"), ((0, pad), (0, 0)))
    down = wd.reshape(FHT, P, 2, HALF).transpose(2, 0, 1, 3).reshape(3, 2, P, HALF).transpose(0, 2, 1, 3)
    pairs = _np.stack([_feature_quarters(g(n).T).reshape(PAIRS, P, D) for n in ("wiq", "wik", "wiv")], 1)
    stream = _np.concatenate([
        _feature_quarters(wqkv[:, 0:D]), _feature_quarters(wqkv[:, D:2 * D]), _token_quarters(wqkv[:, 2 * D:]),
        _feature_quarters(g("wq").T), _feature_quarters(g("wk").T), _feature_quarters(g("wv").T),
        pairs[0, 0:2].reshape(-1, D), gate_up.reshape(-1, D), pairs[0, 2], down.reshape(-1, D),
        pairs[1:].reshape(-1, D), _token_quarters(g("wo").T)])
    w1, w2 = ff("w1"), ff("w2")
    experts = _np.concatenate(
        [_np.concatenate([_token_quarters(w1[e]), _token_quarters(w2[e])]) for e in range(EXPERTS)])

    col = lambda v: _np.pad(v, (0, -len(v) % P)).reshape(-1, P).T
    bq = mx("bqkv")
    cols = _np.concatenate([col(bq[0:D]), col(bq[D:2 * D])] + [col(g(n)) for n in
                           ("bq", "bk", "bv", "biq", "bik", "biv")] + [col(mx("bg")), col(mx("bu"))], 1)
    row8 = _np.zeros(D, f32)
    row8[0:NT * EXPERTS] = _np.tile(ff("switch_b"), NT)
    rowb = _np.stack([bq[2 * D:], mx("g1"), mx("b1"), mx("bd"), mx("g2"), mx("b2"), g("bo"), row8])

    r = _np.arange(P)
    consts = _np.concatenate([
        _np.eye(P), (r[:, None] < r[None, :]).astype(f32), _np.ones((P, P)),
        _np.tile(_np.arange(EXPERTS, 0, -1), (P, 1)),
        _np.tile(_np.arange(EXPERTS), (P, 1)), _np.tile(_np.repeat(_np.arange(OVER), EXPERTS), (P, 1)), r[:, None],
        N * N + r[:, None] + P * _np.arange(EC)[None, :]], 1).astype(f32)
    later = (_np.arange(N)[None, None, :] > (_np.arange(GROUP) * P)[None, :, None] + r[:, None, None]).astype(f32)

    c = _np.ascontiguousarray
    arrays = {
        "x": a["x"], "rowb": rowb, "cols": c(cols), "consts": consts, "later": later,
        "src_rows": a["src"], "dst_rows": a["dst"],
        "src_cols": c(a["src"].reshape(EC, P).T), "dst_cols": c(a["dst"].reshape(EC, P).T),
        "type_cols": c(a["edge_type_5"].reshape(EC, P).T), "type_weights": g("edge_type_weights"),
        "w_stream": stream, "w_experts": experts,
        "switch_w": c(ff("switch_w").reshape(KT, P, EXPERTS).transpose(1, 0, 2)),
        "b12": _np.concatenate([ff("b1"), ff("b2")], 1),
    }
    nc = _bacc.Bacc("TRN2", target_bir_lowering=False, num_devices=1)
    aps = [nc.dram_tensor("in_" + k, v.shape, _mybir.dt.from_np(v.dtype), kind="ExternalInput").ap()
           for k, v in arrays.items()]
    out = nc.dram_tensor("out_dram", (N, D), _mybir.dt.float32, kind="ExternalOutput").ap()
    graph_layer(nc, *aps, out)
    got = _run(nc, [{"in_" + k: v for k, v in arrays.items()}], core_ids=[0])
    return got.results[0]["out_dram"]
```

```python
from contextlib import ExitStack, contextmanager

import concourse.bass as bass
from concourse import mybir

ALU = mybir.AluOpType
ACT = mybir.ActivationFunctionType
F32 = mybir.dt.float32
F32R = mybir.dt.float32r
I32 = mybir.dt.int32
AX_X = mybir.AxisListType.X

P = 128
N = 384
NT = N // P
D = 1024
KT = D // P
HEADS = 16
PAIRS = HEADS // 2
DH = D // HEADS
E_EDGES = 6144
EC = E_EDGES // P
GROUP = 3
PIECES = EC // GROUP
FH = 341
FHT = 3
EXPERTS = 8
F = 512
OVER = (N - 1) // P
SLOTS = EXPERTS + OVER
RING = 4
AHEAD = 6
XRING = 8
HALF = 512
NONE = -1.0e30
PASSES = ((0, 0), (0, 1), (1, 0))

B_MQ, B_MK, B_Q, B_K, B_V, B_IQ, B_IK, B_IV, B_G, B_U = 0, 8, 16, 24, 32, 40, 48, 56, 64, 67
NBIAS = 70
C_ID, C_TRI, C_ONE, C_W8, C_EID, C_SLOT = 0, 128, 256, 384, 392, 400
C_EXP = C_SLOT + OVER * EXPERTS
C_IOTA = C_EXP + 1
C_SPARE = C_IOTA + P
NCONST = C_SPARE + EC

R_LOGIT, R_MAX, R_NMAX, R_EXP, R_SUM, R_PROB, R_CAND, R_FIRST, R_RANK, R_TOTAL, R_POS = range(11)

Q_MQ, Q_MK, Q_MV, Q_GQ, Q_GK, Q_GV, Q_PAIR0 = 0, 8, 16, 24, 32, 40, 48
Q_GU = Q_PAIR0 + 2
Q_DOWN = Q_GU + 2 * FHT + 1
Q_PAIR = Q_DOWN + 3
Q_WO = Q_PAIR + 3 * (PAIRS - 1)
Q_MOE = Q_WO + 8
QE = 8


WO_ORDER = ((0, 0), (0, 1), (0, 2), (1, 0), (0, 3), (1, 1), (1, 2), (1, 3))


class Tally:

    def __init__(self, n=0):
        self.n, self.i, self.per = n, None, 0

    @property
    def value(self):
        return self.n if self.i is None else self.i * self.per + self.n

    def add(self, n=1):
        self.n += n
        return self.value


@contextmanager
def repeat(engine, times, per):
    first = {t: t.n for t in per}
    with engine.Fori(0, times) as i:
        for t, n in per.items():
            t.i, t.per = i, n
        yield i
    for t, n in per.items():
        assert t.n == first[t] + n, (t.n, first[t], n)
        t.n, t.i = first[t] + n * times, None


def slot_of(q):
    if q < Q_PAIR:
        return q % RING
    if q < Q_WO:
        return 1 + (q - Q_PAIR) % 3
    if q < Q_MOE:
        return (q - Q_WO) % RING
    return (q - Q_MOE + RING) % XRING


def graph_layer(nc, x, rowb, cols, consts, later, src_rows, dst_rows, src_cols, dst_cols, type_cols,
                type_weights, w_stream, w_experts, switch_w, b12, out):
    with ExitStack() as ctx:
        def sb(name, shape, dt=F32):
            return ctx.enter_context(nc.sbuf_tensor(name, shape, dt))

        def sem(name):
            return ctx.enter_context(nc.semaphore(name))

        raw = sb("raw", [P, RING, D])
        wsp = sb("wsp", [P, 2, RING, D], F32R)
        with nc.sbuf_tensor("big1", [P, 2, KT * N], F32R) as big1:
            pass
        raw_x = sb("raw_x", [P, RING, D])
        xsp = sb("xsp", [P, 2, D], F32R)
        with nc.sbuf_tensor("blank", [P, NT, N], F32) as blank:
            pass
        bigs = [None, big1] + [sb(f"big{n}", [P, 2, KT * N], F32R) for n in (3, 2)][::-1]
        with nc.sbuf_tensor("big0", [P, 2, KT * N], F32R) as bigs[0]:
            pass
        xs_all = sb("xs_all", [P, AHEAD, D])
        feat = [b[:].rearrange("p h (k n) -> p h k n", k=KT) for b in bigs]
        tokv = [b[:].rearrange("p h (t d) -> p h t d", t=NT) for b in bigs]
        tok = sb("tok", [P, NT, D])
        pt = sb("pt", [P, 2, NT, N], F32R)
        work = sb("work", [P, 2 * NT * N])
        maskb = sb("maskb", [P, NT, N])
        qp = sb("qp", [P, 2, N], F32R)
        kp = sb("kp", [P, 2, N], F32R)
        vp = sb("vp", [P, 2, NT, P], F32R)
        row_buf = sb("row_buf", [P, D])
        diag = sb("diag", [P, P])
        rowbuf = sb("rowbuf", [P, 2, D])
        bias = sb("bias", [P, NBIAS])
        cst = sb("cst", [P, NCONST])
        swt = sb("swt", [P, KT, EXPERTS])
        sbias = sb("sbias", [P, NT * EXPERTS])
        ones_r = sb("ones_r", [P, 2], F32R)
        ei = sb("ei", [P, 3, EC], I32)
        ef = sb("ef", [P, 6, EC])
        eidx = sb("eidx", [P, EC], I32)
        tw = sb("tw", [P, 4, 4])
        dup = sb("dup", [P, EC])
        stats = sb("stats", [P, NT, 2, 6])
        mv = sb("mv", [P, NT, 2])
        rs = sb("rs", [P, NT, 2])
        half = sb("half", [P, 1])
        width = sb("width", [P, 1], I32)
        waited = sb("waited", [P, 1])
        den = sb("den", [P, 2 * NT])
        smx = sb("smx", [P, 2, NT])
        snm = sb("snm", [P, 2, NT])
        ssum = sb("ssum", [P, 2, NT])
        sinv = sb("sinv", [P, 2, NT])
        rt = sb("rt", [P, 11, NT * EXPERTS])
        hot_r = sb("hot_r", [P, NT * EXPERTS], F32R)
        cum = sb("cum", [P, 4, 12])
        slotc = sb("slotc", [P, OVER, EXPERTS])
        slote = sb("slote", [P, 3, SLOTS])
        posi = sb("posi", [P, NT], I32)
        rowi = sb("rowi", [P, OVER + 1], I32)

        vt = row_buf[:, 0:N]
        tri_r, slot_hot = qp[:, 0, 0:2 * P], kp[:, 0, 0:P]
        ident = cst[:, C_ID:C_ID + P]
        tri = cst[:, C_TRI:C_TRI + P]
        ones = cst[:, C_ONE:C_ONE + P]
        maskflat = maskb[:].rearrange("p t n -> p (t n)")
        probs = work[:].rearrange("p (s t n) -> p s t n", s=2, t=NT)
        edge_rows = [rowbuf[:].rearrange("p a b -> p (a b)")[:, 768 * n:768 * (n + 1)].bitcast(I32)
                     .rearrange("p (a b) -> p a b", a=2) for n in range(2)]
        codes = [work[:, 0:N].bitcast(I32), work[:, N:2 * N].bitcast(I32)]
        junk = [work[:, 2 * N:3 * N], work[:, 3 * N:4 * N - P], work[:, 4 * N - P:4 * N]]
        code_part = row_buf[:, N:2 * N].bitcast(I32)
        elu_s, elu_e, elu_r = work[:, 4 * N:5 * N], work[:, 5 * N:6 * N], vt
        gate, hid = work[:, 0:N], work[:, N:2 * N]
        logits_t = code_part.bitcast(F32)[0:EXPERTS, :]
        place = maskflat[:, 0:N].rearrange("p (t n) -> p t n", t=NT)
        x2t = [work[:, D:2 * D], maskflat[:, 0:D], row_buf[:]]
        x2 = [rowbuf[:, 0, :], rowbuf[:, 1, :], work[:, 0:D]]
        hts, b12r = bigs[2][:, :, D:D + F], bigs[2][0:EXPERTS, :, D + F:D + 2 * F + D]
        h_buf, y_buf = maskflat[:, 0:F], work[:, 0:D]
        spare = cst[:, C_SPARE:C_SPARE + EC]

        ps = ctx.enter_context(nc.psum_tensor("ps", [P, 8, HALF], F32))

        table = nc.dram_tensor("edge_table", [N * N + P * EC, 1], F32).ap()
        xs_dram = nc.dram_tensor("slot_x", [SLOTS * P, D], F32).ap()
        ys_dram = nc.dram_tensor("slot_y", [SLOTS * P, D], F32).ap()

        x_in = [sem(f"x_in{t}") for t in range(NT)]
        const_in, edge_in, rowb_in, b_row_in = sem("const_in"), sem("edge_in"), sem("rowb_in"), sem("b_row_in")
        piece_in = [sem(f"piece_in{n}") for n in range(2)]
        piece_done, codes_done = sem("piece_done"), sem("codes_done")
        raw_in = [sem(f"raw_in{n}") for n in range(XRING)]
        w_hi, w_lo = sem("w_hi"), sem("w_lo")
        w_started = sem("w_started")
        acc_ready, acc_hi, acc_free = sem("acc_ready"), sem("acc_hi"), sem("acc_free")
        elu_parts, elu_hi = sem("elu_parts"), sem("elu_hi")
        elu_lo = sem("elu_lo")
        tr_ready, tr_hi, tr_free = sem("tr_ready"), sem("tr_hi"), sem("tr_free")
        tm_ready, tm_sum, tm_hi, tm_lo = sem("tm_ready"), sem("tm_sum"), sem("tm_hi"), sem("tm_lo")
        dve_step, act_step, pool_step = sem("dve_step"), sem("act_step"), sem("pool_step")
        ones_set = sem("ones_set")
        stats_done, rstd_done, xn_done = sem("stats_done"), sem("rstd_done"), sem("xn_done")
        num_ready, num_free = sem("num_ready"), sem("num_free")
        x1_done, bd_added = sem("x1_done"), sem("bd_added")
        hid_hi, hid_lo = sem("hid_hi"), sem("hid_lo")
        down_ready, down_sum, mix_done = sem("down_ready"), sem("down_sum"), sem("mix_done")
        s_ready, s_max, s_exp, s_norm = sem("s_ready"), sem("s_max"), sem("s_exp"), sem("s_norm")
        pt_ready, pt_hi, pt_lo = sem("pt_ready"), sem("pt_hi"), sem("pt_lo")
        v_sum = sem("v_sum")
        tw_arg, tw_exp, tw_one, tw_ln, tw_done = (sem("tw_arg"), sem("tw_exp"), sem("tw_one"), sem("tw_ln"),
                                                  sem("tw_done"))
        edges_done = sem("edges_done")
        table_out, later_in, scattered, mask_in = (sem("table_out"), sem("later_in"), sem("scattered"),
                                                   sem("mask_in"))
        zero_out = sem("zero_out")
        b12_in, b12_hi, b12_lo = sem("b12_in"), sem("b12_hi"), sem("b12_lo")
        wo_ready, wo_sum = sem("wo_ready"), sem("wo_sum")
        x2_done, x2t_ready, x2t_copied, logits_ready = (
            sem("x2_done"), sem("x2t_ready"), sem("x2t_copied"), sem("logits_ready"))
        lmax_done, lexp_done, hot_done, count_ready, route_done, pos_done = (
            sem("lmax_done"), sem("lexp_done"), sem("hot_done"), sem("count_ready"), sem("route_done"),
            sem("pos_done"))
        xs_out, hott_ready, hott_copied, b2_ready, b2_added = (
            sem("xs_out"), sem("hott_ready"), sem("hott_copied"), sem("b2_ready"), sem("b2_added"))
        xs_late_in = sem("xs_late_in")
        slot_set, xs_in = sem("slot_set"), sem("xs_in")
        x0_ready, x0_hi, x0_lo = sem("x0_ready"), sem("x0_hi"), sem("x0_lo")
        tri_set, lt_ready, lt_copied, place_done = (sem("tri_set"), sem("lt_ready"), sem("lt_copied"),
                                                    sem("place_done"))
        h_ready, h_act, ht_ready, ht_hi, ht_lo = (sem("h_ready"), sem("h_act"), sem("ht_ready"),
                                                  sem("ht_hi"), sem("ht_lo"))
        y_ready, y_half0, y_half1, y_out = sem("y_ready"), sem("y_half0"), sem("y_half1"), sem("y_out")
        yg_in = [sem(f"yg_in{t}") for t in range(NT)]
        sum_done, out_done = sem("sum_done"), sem("out_done")

        block = ctx.enter_context(nc.Block())

        def set_banks(t):
            return ps[:, 2 + 2 * t:4 + 2 * t, :].rearrange("p a (b c) -> p (a b) c", c=P)

        def set_banks_row(t):
            return ps[:, 2 + 2 * t:4 + 2 * t, :].rearrange("p a b -> p (a b)")

        def raw_slot(k):
            if k < RING:
                return raw[:, k, :]
            return raw_x[:, k - RING, :]

        def split_of(k, part):
            if k < RING:
                return wsp[:, part, k, :]
            big, k = (bigs[3], k - RING) if k < XRING - 1 else (bigs[2], 0)
            return big[:, part, k * D:(k + 1) * D]

        def whole(a):
            return ps[:, a:a + 2, :].rearrange("p a b -> p (a b)")

        @block.sync
        def _(sp):
            for t in range(NT):
                sp.dma_start(tok[:, t, :], x[t * P:(t + 1) * P, :]).then_inc(x_in[t], 16)
            sp.dma_start(cst[:], consts).then_inc(const_in, 16)
            sp.dma_start(bias[:], cols).then_inc(const_in, 16)

            def load(row, slot, split):
                if split is not None:
                    sp.wait_ge(w_lo, split)
                sp.dma_start(raw[:, slot, :], w_stream[bass.ds(row, P), :]).then_inc(raw_in[slot], 16)

            def load_piece(first, buf, read):
                for k, r in enumerate((src_rows, dst_rows)):
                    if read is not None:
                        sp.wait_ge(codes_done, read)
                    sp.dma_start(edge_rows[buf][:, k, :],
                                 r[bass.ds(first, N)].partition_broadcast(P)).then_inc(piece_in[buf], 16)

            for q in range(RING):
                load(q * P, q, None)
            for j in range(2):
                load_piece(j * N, j, None)
            with sp.Fori(0, (Q_MV - RING) // RING) as i:
                for j in range(RING):
                    row = sp.snap(i * (RING * P) + (RING + j) * P)
                    first = sp.snap(i * (RING * N) + (2 + j) * N)
                    load(row, j, i * RING + (j + 1))
                    load_piece(first, j % 2, i * RING + (j + 1))
            for j in range(RING):
                load((Q_MV + j) * P, j, Q_MV + j - RING + 1)
                n = 2 + Q_MV - RING + j
                if n < PIECES:
                    load_piece(n * N, n % 2, n - 1)
            with sp.Fori(0, (Q_PAIR0 - Q_MV) // RING - 1) as i:
                for j in range(RING):
                    row = sp.snap(i * (RING * P) + (Q_MV + RING + j) * P)
                    load(row, j, i * RING + (Q_MV + j + 1))
            for q in range(Q_PAIR0, Q_PAIR):
                load(q * P, slot_of(q), q - RING + 1)
            with sp.Fori(0, PAIRS - 1) as i:
                for j in range(3):
                    row = sp.snap(i * (3 * P) + (Q_PAIR + j) * P)
                    load(row, 1 + j, i * 3 + (Q_PAIR + j - 2))
            for q in range(Q_WO, Q_MOE):
                load(q * P, slot_of(q), q - RING + 1)

            def load_expert(row, k, split):
                sp.wait_ge(w_lo, split)
                sp.dma_start(raw_slot(k), w_experts[bass.ds(row, P), :]).then_inc(raw_in[k], 16)

            sp.wait_ge(w_started, Q_WO + 1)
            for j in range(RING):
                load_expert(j * P, RING + j, Q_WO)
            with sp.Fori(0, EXPERTS - 1) as i:
                for k in range(XRING):
                    first = QE + k if k < RING else k
                    row = sp.snap(i * (QE * P) + first * P)
                    load_expert(row, k, i * XRING + (Q_MOE + RING + k - XRING + 1))
            q = Q_MOE + QE * EXPERTS - RING
            for j in range(RING):
                k = slot_of(q + j)
                load_expert(((EXPERTS - 1) * QE + RING + j) * P, k, q + j - XRING + 1)

            sp.wait_ge(route_done, 1)
            over = sp.value_load(rowi[0:1, OVER:OVER + 1], min_val=0, max_val=OVER)
            with sp.If(over > 0):
                q += RING
                for o in range(OVER):
                    r = sp.value_load(rowi[0:1, o:o + 1], min_val=0, max_val=(EXPERTS - 1) * QE * P)
                    for j in range(QE):
                        row = sp.snap(r + j * P)
                        load_expert(row, slot_of(q), q - XRING + 1)
                        q += 1

            for t in range(NT):
                sp.wait_ge(sum_done, t + 1)
                sp.dma_start(out[t * P:(t + 1) * P, :], tok[:, t, :]).then_inc(out_done, 16)
            sp.wait_ge(out_done, 16 * NT)

        @block.gpsimd
        def _(pool):
            step, rows_in = Tally(), Tally()
            R_BV, R_G1, R_B1, R_BD, R_G2, R_B2, R_BO, R_SW = range(8)

            def then(ins):
                ins.then_inc(pool_step, 1)
                pool.wait_ge(pool_step, step.add())

            def load_row(k, buf):
                pool.dma_start(rowbuf[:, buf, :], rowb[k].partition_broadcast(P)).then_inc(rowb_in, 16)
                rows_in.add(16)

            def small_loads():
                for k, r in enumerate((src_cols, dst_cols, type_cols)):
                    pool.dma_start(ei[:, k, :], r).then_inc(edge_in, 16)
                pool.dma_start(tw[:, 0, :], type_weights.partition_broadcast(P)).then_inc(edge_in, 16)
                pool.dma_start(sbias[:], rowb[R_SW, 0:NT * EXPERTS].partition_broadcast(P)).then_inc(edge_in, 16)
                pool.dma_start(swt[:], switch_w).then_inc(edge_in, 16)
                pool.dma_start(maskb[:], later).then_inc(later_in, 16)

            then(nc.gpsimd.memset(half[:], -0.5))
            then(nc.gpsimd.memset(width[:], N))

            def rstd(t, n):
                pool.wait_ge(stats_done, n + 1)
                then(nc.gpsimd.tensor_scalar(rs[:, t, 0:1], mv[:, t, 1:2], 1e-5, None, ALU.add))
                nc.gpsimd.tensor_tensor(rs[:, t, 1:2], rs[:, t, 0:1], half[:], ALU.pow).then_inc(rstd_done, 1)

            for t in range(NT):
                rstd(t, t)
            small_loads()

            then(nc.gpsimd.memset(blank[:], NONE))
            for t in range(NT):
                then(nc.gpsimd.affine_select(out=blank[:, t, :], in_=blank[:, t, :], compare_op=ALU.not_equal,
                                             fill=0.0, base=t * P, pattern=[[-1, N]], channel_multiplier=1))
            pool.wait_ge(const_in, 32)
            pool.wait_ge(tw_done, 1)
            then(nc.gpsimd.tensor_scalar(diag[:], ident, tw[:, 3, 3:4], None, ALU.mult))
            for t in range(NT):
                blk = blank[:, t, t * P:(t + 1) * P]
                then(nc.gpsimd.tensor_tensor(blk, blk, diag[:], ALU.add))
            pool.dma_start(table[0:N * N, :].rearrange("(t p n) o -> p t (n o)", t=NT, p=P),
                           blank[:]).then_inc(table_out, 16)
            seen = [Tally(), Tally()]

            def codes_step(buf, read):
                pool.wait_ge(piece_in[buf], seen[buf].add(32))
                if read is not None:
                    pool.wait_ge(piece_done, read)
                then(nc.gpsimd.tensor_tensor(code_part, edge_rows[buf][:, 0, :], width[:].to_broadcast([P, N]),
                                             ALU.mult))
                nc.gpsimd.tensor_tensor(codes[buf], code_part, edge_rows[buf][:, 1, :], ALU.add)\
                    .then_inc(codes_done, 1)
                pool.wait_ge(codes_done, codes_no.add())

            codes_no = Tally()
            for j in range(2):
                codes_step(j, None)
            with repeat(pool, PIECES // 2 - 1, {step: 2, codes_no: 2, seen[0]: 32, seen[1]: 32}) as i:
                for j in range(2):
                    codes_step(j, i * 2 + (j + 1))
            pool.wait_ge(table_out, 16)

            pool.wait_ge(edges_done, 1)
            for g in range(PIECES):
                for k in range(GROUP):
                    c = g * GROUP + k
                    pool.indirect_dma_start(
                        out=table, out_offset=bass.IndirectOffsetOnAxis(ap=eidx[:, c:c + 1], axis=0),
                        in_=ef[:, 3, c:c + 1], in_offset=None).then_inc(scattered, 16)
                pool.wait_ge(scattered, 16 * GROUP * (g + 1))
            pool.dma_start(maskb[:], table[0:N * N, :].rearrange("(t p n) o -> p t (n o)", t=NT, p=P))\
                .then_inc(mask_in, 16)

            pool.wait_ge(tm_sum, 2 * NT)
            load_row(R_G1, 0)
            load_row(R_B1, 1)
            pool.wait_ge(rowb_in, rows_in.value)
            for t in range(NT):
                rstd(t, NT + t)
                pool.wait_ge(rstd_done, NT + t + 1)
                row = tok[:, t, :]
                then(nc.gpsimd.tensor_scalar(row, row, mv[:, t, 0:1], rs[:, t, 1:2], ALU.subtract, ALU.mult))
                then(nc.gpsimd.tensor_tensor(row, row, rowbuf[:, 0, :], ALU.mult))
                nc.gpsimd.tensor_tensor(row, row, rowbuf[:, 1, :], ALU.add).then_inc(x1_done, 1)
            pool.wait_ge(x1_done, NT)
            load_row(R_BD, 0)
            pool.wait_ge(rowb_in, rows_in.value)
            for t in range(NT):
                pool.wait_ge(tr_ready, NT + t + 1)
                nc.gpsimd.tensor_tensor(tok[:, t, :], tok[:, t, :], rowbuf[:, 0, :], ALU.add)\
                    .then_inc(bd_added, 1)
            pool.wait_ge(bd_added, NT)
            then(nc.gpsimd.memset(rowbuf[:, 0, :], 0.0))
            for s in range(SLOTS):
                pool.dma_start(xs_dram[s * P:(s + 1) * P, :], rowbuf[:, 0, :]).then_inc(zero_out, 16)
            for s in range(EXPERTS, SLOTS):
                pool.dma_start(ys_dram[s * P:(s + 1) * P, :], rowbuf[:, 0, :]).then_inc(zero_out, 16)
            pool.wait_ge(zero_out, 16 * (SLOTS + OVER))
            load_row(R_G2, 0)
            load_row(R_B2, 1)
            pool.wait_ge(rowb_in, rows_in.value)
            for t in range(NT):
                rstd(t, 2 * NT + t)
                pool.wait_ge(rstd_done, 2 * NT + t + 1)
                row = tok[:, t, :]
                then(nc.gpsimd.tensor_scalar(row, row, mv[:, t, 0:1], rs[:, t, 1:2], ALU.subtract, ALU.mult))
                then(nc.gpsimd.tensor_tensor(row, row, rowbuf[:, 0, :], ALU.mult))
                then(nc.gpsimd.tensor_tensor(row, row, rowbuf[:, 1, :], ALU.add))
            load_row(R_BO, 0)
            for t in range(NT):
                row = tok[:, t, :]
                pool.dma_start(rowbuf[:, 1, :], x[t * P:(t + 1) * P, :]).then_inc(rowb_in, 16)
                rows_in.add(16)
                pool.wait_ge(rowb_in, rows_in.value)
                then(nc.gpsimd.tensor_tensor(row, row, rowbuf[:, 0, :], ALU.add))
                nc.gpsimd.tensor_tensor(row, row, rowbuf[:, 1, :], ALU.add).then_inc(mix_done, 1)
                pool.wait_ge(mix_done, t + 1)

            pool.wait_ge(pt_ready, HEADS)
            pool.dma_start(work[0:EXPERTS, 0:F + D], b12).then_inc(b12_in, 16)

            pool.wait_ge(b12_hi, 1)
            nc.gpsimd.tensor_tensor(b12r[:, 1, :], work[0:EXPERTS, 0:F + D], b12r[:, 0, :].bitcast(F32), ALU.subtract)\
                .then_inc(b12_lo, 1)
            for t in range(NT):
                rstd(t, 3 * NT + t)
            pool.wait_ge(zero_out, 16 * (SLOTS + OVER))
            pool.wait_ge(pos_done, 1)
            for t in range(NT):
                pool.wait_ge(x2_done, t + 1)
                pool.indirect_dma_start(
                    out=xs_dram, out_offset=bass.IndirectOffsetOnAxis(ap=posi[:, t:t + 1], axis=0),
                    in_=x2[t], in_offset=None).then_inc(xs_out, 16)
            pool.wait_ge(y_out, 16 * EXPERTS)
            over = pool.value_load(rowi[0:1, OVER:OVER + 1], min_val=0, max_val=OVER)
            with pool.If(over > 0):
                pool.wait_ge(y_out, 16 * SLOTS)
            for t in range(NT):
                pool.indirect_dma_start(
                    out=x2[t], out_offset=None, in_=ys_dram,
                    in_offset=bass.IndirectOffsetOnAxis(ap=posi[:, t:t + 1], axis=0)).then_inc(yg_in[t], 16)

        @block.scalar
        def _(act):
            q_no = Tally()
            used = [Tally() for _ in range(XRING)]
            acc = Tally()
            everyone = slice(0, P)

            def prep(slot):
                act.wait_ge(raw_in[slot], used[slot].add(16))
                if q_no.i is not None or q_no.n >= RING:
                    act.wait_ge(w_started, q_no.value - 1)
                nc.scalar.activation(wsp[:, 0, slot, :], raw[:, slot, :], ACT.Copy).then_inc(w_hi, 1)
                q_no.add()

            def acc_part(dst, rows, b):
                bank = acc.n % 2
                act.wait_ge(acc_ready, acc.add())
                nc.scalar.activation(dst, ps[rows, bank, 0:N], ACT.Identity, bias=b).then_inc(acc_hi, 1)

            turn = {q_no: RING, acc: RING, **{u: 16 for u in used[:RING]}}

            prep(0)
            for t in range(NT):
                act.wait_ge(tr_ready, t + 1)
                nc.scalar.activation(feat[0][:, 0, :, t * P:(t + 1) * P], set_banks(t), ACT.Copy).then_inc(tr_hi, 1)
            prep(1)
            act.wait_ge(tw_arg, 1)
            nc.scalar.activation(tw[:, 1, :], tw[:, 1, :], ACT.Exp).then_inc(tw_exp, 1)
            act.wait_ge(tw_one, 1)
            nc.scalar.activation(tw[:, 1, :], tw[:, 1, :], ACT.Ln).then_inc(tw_ln, 1)

            act.wait_ge(const_in, 32)

            def elu_step(m, j):
                bank = acc.n % 2
                if acc.i is not None or acc.n:
                    act.wait_ge(acc_free, acc.value)
                act.wait_ge(acc_ready, acc.add())
                b = bias[:, bass.ds(m + B_MQ, 1)]
                nc.scalar.activation(elu_e, ps[:, bank, 0:N], ACT.Exp, bias=b).then_inc(elu_parts, 1)
                nc.scalar.activation(elu_r, ps[:, bank, 0:N], ACT.Relu, bias=b).then_inc(elu_parts, 1)
                prep((j + 2) % RING)
                act.wait_ge(acc_free, acc.value)
                return acc.n

            def elu_hi_part(big, m):
                nc.scalar.activation(feat[big][:, 0, bass.ds(m, 1), :], elu_s, ACT.Copy).then_inc(elu_hi, 1)

            for j in range(RING):
                elu_step(j, j)
                elu_hi_part(1, j)
            with repeat(act, 1, turn) as i:
                for j in range(RING):
                    elu_step(i * RING + (RING + j), j)
                    elu_hi_part(1, i * RING + (RING + j))
            with repeat(act, 2, turn) as i:
                for j in range(RING):
                    elu_step(i * RING + (2 * RING + j), j)
                    elu_hi_part(2, i * RING + j)

            act.wait_ge(codes_done, PIECES)
            act.wait_ge(table_out, 16)
            act.dma_start(rowbuf[:, 1, :], rowb[0].partition_broadcast(P)).then_inc(b_row_in, 16)
            for h in range(2):
                for j in range(RING):
                    prep((j + 2) % RING)
                for t in range(NT):
                    act.wait_ge(tm_sum, h * NT + t + 1)
                    nc.scalar.activation(tokv[3][:, 0, t, h * HALF:(h + 1) * HALF],
                                         work[:, t * HALF:(t + 1) * HALF], ACT.Copy).then_inc(tm_hi, 1)

            for mt in range(NT):
                acc_part(pt[:, 0, mt, :], everyone, 0.0)

            for n, b0 in enumerate((B_Q, B_K, B_V)):
                with repeat(act, 2, turn) as i:
                    for j in range(RING):
                        m = i * RING + j
                        acc_part(feat[1 + n][:, 0, bass.ds(m, 1), :], everyone, bias[:, bass.ds(m + b0, 1)])
                        prep((j + 2) % RING)

            for t in range(NT):
                act.wait_ge(tr_ready, NT + t + 1)
                nc.scalar.activation(feat[0][:, 0, :, t * P:(t + 1) * P], set_banks(t), ACT.Copy).then_inc(tr_hi, 1)

            acc_part(qp[:, 0, :], everyone, bias[:, B_IQ:B_IQ + 1])
            prep(slot_of(q_no.n))
            acc_part(kp[:, 0, :], everyone, bias[:, B_IK:B_IK + 1])
            prep(slot_of(q_no.n))

            for m in range(FHT):
                bank = acc.n % 2
                act.wait_ge(acc_free, acc.value)
                act.wait_ge(acc_ready, acc.add())
                nc.scalar.activation(gate, ps[:, bank, 0:N], ACT.Silu, bias=bias[:, B_G + m:B_G + m + 1])\
                    .then_inc(acc_free, 1)
                prep(slot_of(q_no.n))
                act.wait_ge(acc_free, acc.add())
                nc.scalar.activation(pt[:, 0, m, :], hid, ACT.Copy).then_inc(hid_hi, 1)
                prep(slot_of(q_no.n))
            acc.add()
            prep(slot_of(q_no.n))
            prep(slot_of(q_no.n))

            def values_hi():
                bank = acc.n % 2
                act.wait_ge(acc_ready, acc.add())
                nc.scalar.activation(vp[:, 0, :, :], ps[:, bank, 0:N].rearrange("p (t d) -> p t d", t=NT),
                                     ACT.Copy).then_inc(acc_hi, 1)

            act.wait_ge(down_ready, NT)
            prep(slot_of(q_no.n))
            values_hi()
            prep(slot_of(q_no.n))

            exp_no, pt_no = Tally(), Tally()

            def exps(s):
                act.wait_ge(s_max, exp_no.add())
                for t in range(NT):
                    nc.scalar.activation(probs[:, s, t, :], probs[:, s, t, :], ACT.Exp,
                                         bias=snm[:, s, t:t + 1], scale=DH ** -0.5,
                                         accum_out=ssum[:, s, t:t + 1]).then_inc(s_exp, 1)

            def pt_part(s, bank=None):
                b = 2 + 3 * s if bank is None else bank
                act.wait_ge(pt_ready, pt_no.add())
                nc.scalar.activation(pt[:, 0, :, :], ps[:, b:b + 3, 0:N], ACT.Copy).then_inc(pt_hi, 1)

            def head_rows(s):
                return slice(s * DH, (s + 1) * DH)

            def pair(p, last):
                exps(0)
                exps(1)
                acc_part(qp[:, 0, :], everyone, bias[:, bass.ds(p + B_IQ, 1)])
                pt_part(0)
                prep(3)
                acc_part(kp[:, 0, :], everyone, bias[:, bass.ds(p + B_IK, 1)])
                prep(0 if last else 1)
                acc_part(feat[0][head_rows(0), 0, bass.ds(p - 1, 1), :], head_rows(0), 0.0)
                pt_part(1)
                acc.add()
                prep(1 if last else 2)
                acc_part(feat[0][head_rows(1), 0, bass.ds(p - 1, 1), :], head_rows(1), 0.0)
                values_hi()

            with repeat(act, PAIRS - 2, {q_no: 3, acc: 6, exp_no: 2, pt_no: 2,
                                         used[1]: 16, used[2]: 16, used[3]: 16}) as i:
                pair(i + 1, False)
            pair(PAIRS - 1, True)
            exps(0)
            exps(1)
            for s in range(2):
                prep(slot_of(q_no.n))
                pt_part(s, 2)
                acc_part(feat[0][head_rows(s), 0, PAIRS - 1, :], head_rows(s), 0.0)

            for q in range(Q_WO + 4, Q_MOE):
                prep(slot_of(q))
            act.wait_ge(b12_in, 16)
            nc.scalar.activation(b12r[:, 0, :], work[0:EXPERTS, 0:F + D], ACT.Copy).then_inc(b12_hi, 1)

            def prep_x(wait=True):
                slot = (q_no.n - Q_MOE + RING) % XRING
                act.wait_ge(raw_in[slot], used[slot].add(16))
                if wait:
                    act.wait_ge(w_started, q_no.value - (XRING - 2))
                nc.scalar.activation(split_of(slot, 0), raw_slot(slot), ACT.Copy).then_inc(w_hi, 1)
                q_no.add()

            for _ in range(RING):
                prep_x()
            act.wait_ge(wo_ready, 2 * NT)
            for _ in range(RING):
                prep_x(False)

            nc.scalar.activation(tri_r, cst[:, C_TRI:C_TRI + 2 * P], ACT.Copy).then_inc(tri_set, 1)
            for t in range(NT):
                act.wait_ge(x2t_ready, t + 1)
                nc.scalar.activation(x2t[t], set_banks_row(t), ACT.Copy).then_inc(x2t_copied, 1)
            act.wait_ge(lt_ready, 1)
            nc.scalar.activation(logits_t, ps[0:EXPERTS, 0, 0:N], ACT.Copy).then_inc(lt_copied, 1)
            act.wait_ge(lmax_done, 1)
            for t in range(NT):
                sl = slice(t * EXPERTS, (t + 1) * EXPERTS)
                nc.scalar.activation(rt[:, R_EXP, sl], rt[:, R_LOGIT, sl], ACT.Exp,
                                     bias=rt[:, R_NMAX, t:t + 1], accum_out=rt[:, R_SUM, t:t + 1])\
                    .then_inc(lexp_done, 1)
            act.wait_ge(hott_ready, 1)
            nc.scalar.activation(pt[0:EXPERTS, 0, 0, :], ps[0:EXPERTS, 1, 0:N], ACT.Copy).then_inc(hott_copied, 1)

            xt, h_no, y_no, ht = Tally(2 * NT), Tally(), Tally(), Tally()

            def load_slot(s):
                row = s * P if isinstance(s, int) else act.snap(s * P)
                act.dma_start(rowbuf[:, 0, :], xs_dram[bass.ds(row, P), :]).then_inc(xs_late_in, 16)

            def split_first(h):
                act.wait_ge(x0_ready, h + 1)
                nc.scalar.activation(xsp[:, 0, h * HALF:(h + 1) * HALF], ps[:, 2 + h, :], ACT.Copy).then_inc(x0_hi, 1)

            def split_slot():
                act.wait_ge(tr_ready, xt.add())
                nc.scalar.activation(xsp[:, 0, :], whole(2), ACT.Copy).then_inc(tr_hi, 1)

            def gelu():
                act.wait_ge(h_ready, h_no.add())
                nc.scalar.activation(h_buf, ps[:, 0, :], ACT.Gelu_apprx_tanh).then_inc(h_act, 1)

            def split_hidden():
                act.wait_ge(ht_ready, ht.add())
                nc.scalar.activation(hts[:, 0, :], ps[:, 1, :], ACT.Copy).then_inc(ht_hi, 1)

            def first_half_of_y(i):
                act.wait_ge(y_ready, y_no.add())
                if not isinstance(i, int) or i:
                    act.wait_ge(y_out, i * 16)
                nc.scalar.activation(y_buf[:, 0:HALF], ps[:, 4, :], ACT.Copy).then_inc(y_half0, 1)

            def store_y(i):
                row = i * P if isinstance(i, int) else act.snap(i * P)
                act.wait_ge(y_half0, y_no.value)
                act.wait_ge(y_half1, y_no.value)
                act.dma_start(ys_dram[bass.ds(row, P), :], y_buf).then_inc(y_out, 16)

            split_first(0)
            split_first(1)
            act.wait_ge(xs_out, 16 * NT)
            act.dma_start(xs_all[:], xs_dram[P:(1 + AHEAD) * P, :].rearrange("(s p) d -> p s d", p=P))\
                .then_inc(xs_in, 16)
            load_slot(EXPERTS - 1)
            for _ in range(RING - 1):
                prep_x()
            gelu()
            split_slot()
            split_hidden()
            prep_x()

            def slot_turn(i, ahead):
                gelu()
                if ahead:
                    split_slot()
                    for _ in range(RING):
                        prep_x()
                first_half_of_y(i)
                split_hidden()
                store_y(i)
                for _ in range(RING):
                    prep_x()

            slot_turn(0, True)
            with repeat(act, EXPERTS - 3, {q_no: QE, xt: 1, h_no: 1, y_no: 1, ht: 1,
                                           **{u: 16 for u in used}}) as i:
                slot_turn(i + 1, True)
            slot_turn(EXPERTS - 2, False)
            first_half_of_y(EXPERTS - 1)
            store_y(EXPERTS - 1)

            over = act.value_load(rowi[0:1, OVER:OVER + 1], min_val=0, max_val=OVER)
            with act.If(over > 0):
                for o in range(OVER):
                    load_slot(EXPERTS + o)
                    for _ in range(RING):
                        prep_x()
                    split_slot()
                    gelu()
                    split_hidden()
                    for _ in range(RING):
                        prep_x()
                    first_half_of_y(EXPERTS + o)
                    store_y(EXPERTS + o)

        @block.vector
        def _(dve):
            q_no, step = Tally(), Tally()
            acc, hi_no = Tally(), Tally()
            everyone = slice(0, P)

            def then(ins):
                ins.then_inc(dve_step, 1)
                dve.wait_ge(dve_step, step.add())

            def lo(dst, value, hi):
                return nc.vector.tensor_tensor(dst, value, hi.bitcast(F32), ALU.subtract)

            def prep(slot):
                dve.wait_ge(w_hi, q_no.add())
                lo(wsp[:, 1, slot, :], raw[:, slot, :], wsp[:, 0, slot, :]).then_inc(w_lo, 1)

            def acc_part(dst, hi, rows, b):
                bank = acc.n % 2
                acc.add()
                dve.wait_ge(acc_hi, hi_no.add())
                nc.vector.scalar_tensor_tensor(out=dst, in0=ps[rows, bank, 0:N], scalar=b, in1=hi.bitcast(F32),
                                               op0=ALU.add, op1=ALU.subtract).then_inc(acc_free, 1)

            def statistics(t):
                for c in range(2):
                    ins = nc.vector.bn_stats(stats[:, t, c, :], tok[:, t, c * HALF:(c + 1) * HALF])
                then(ins)
                nc.vector.bn_aggr(mv[:, t, :], stats[:, t, :, :].rearrange("p a b -> p (a b)"))\
                    .then_inc(stats_done, 1)

            turn = {q_no: RING, acc: RING, hi_no: RING}

            nc.vector.memset(ones_r[:].bitcast(F32), 1.0).then_inc(ones_set, 1)
            for t in range(NT + 1):
                if t < NT:
                    dve.wait_ge(x_in[t], 16)
                    statistics(t)
                if t:
                    u = t - 1
                    dve.wait_ge(rstd_done, u + 1)
                    nc.vector.tensor_scalar(tok[:, u, :], tok[:, u, :], mv[:, u, 0:1], rs[:, u, 1:2],
                                            ALU.subtract, ALU.mult).then_inc(xn_done, 1)

            prep(0)
            for t in range(NT):
                dve.wait_ge(tr_hi, t + 1)
                hi = feat[0][:, 0, :, t * P:(t + 1) * P]
                lo(feat[0][:, 1, :, t * P:(t + 1) * P], set_banks(t), hi).then_inc(tr_free, 1)
            prep(1)

            dve.wait_ge(edge_in, 96)
            then(nc.vector.tensor_scalar(tw[:, 2, :], tw[:, 0, :], -1.0, None, ALU.mult))
            nc.vector.tensor_tensor(tw[:, 1, :], tw[:, 0, :], tw[:, 2, :], ALU.min).then_inc(tw_arg, 1)
            dve.wait_ge(tw_exp, 1)
            nc.vector.tensor_scalar(tw[:, 1, :], tw[:, 1, :], 1.0, None, ALU.add).then_inc(tw_one, 1)
            dve.wait_ge(tw_ln, 1)
            then(nc.vector.scalar_tensor_tensor(out=tw[:, 2, :], in0=tw[:, 0, :], scalar=0.0, in1=tw[:, 1, :],
                                                op0=ALU.max, op1=ALU.add))
            nc.vector.tensor_scalar(tw[:, 3, :], tw[:, 2, :], DH ** 0.5, None, ALU.mult).then_inc(tw_done, 1)
            dve.wait_ge(tw_done, 1)
            then(nc.vector.scalar_tensor_tensor(out=ef[:, 0, :], in0=ei[:, 0, :], scalar=float(N), in1=ei[:, 1, :],
                                                op0=ALU.mult, op1=ALU.add))
            for k, w in ((0, 3), (1, 0), (2, 1), (3, 2), (4, 3)):
                dst = ef[:, 3, :] if k == 0 else ef[:, 1, :]
                then(nc.vector.tensor_scalar(dst, ei[:, 2, :], float(k), tw[:, 3, w:w + 1], ALU.is_equal, ALU.mult))
                if k:
                    then(nc.vector.tensor_tensor(ef[:, 3, :], ef[:, 3, :], ef[:, 1, :], ALU.add))

            parts, elus, pieces = Tally(), Tally(), Tally()

            def elu_step(big, m, j, c):
                acc.add()
                dve.wait_ge(elu_parts, parts.add(2))
                if elus.i is not None or elus.n:
                    dve.wait_ge(elu_lo, elus.value)
                nc.vector.scalar_tensor_tensor(out=elu_s, in0=elu_e, scalar=1.0, in1=elu_r,
                                               op0=ALU.min, op1=ALU.add).then_inc(acc_free, 1)
                prep((j + 2) % RING)
                dve.wait_ge(elu_hi, elus.add())
                lo(feat[big][:, 1, bass.ds(m, 1), :], elu_s, feat[big][:, 0, bass.ds(m, 1), :]).then_inc(elu_lo, 1)
                buf = j % 2
                dve.wait_ge(codes_done, pieces.value + 1)
                for k in range(GROUP):
                    ins = nc.vector.scalar_tensor_tensor(
                        out=junk[k], in0=codes[buf][:, k * P:N], scalar=ef[:, 0, bass.ds(c + k, 1)],
                        in1=maskb[:, k, k * P:N], op0=ALU.is_equal, op1=ALU.mult,
                        accum_out=dup[:, bass.ds(c + k, 1)])
                ins.then_inc(piece_done, 1)
                dve.wait_ge(piece_done, pieces.add())

            dve.wait_ge(later_in, 16)
            elu_turn = {q_no: RING, acc: RING, parts: 2 * RING, elus: RING, pieces: RING}
            for j in range(RING):
                elu_step(1, j, j, j * GROUP)
            with repeat(dve, 1, elu_turn) as i:
                for j in range(RING):
                    elu_step(1, i * RING + (RING + j), j, i * (RING * GROUP) + (RING + j) * GROUP)
            with repeat(dve, 2, elu_turn) as i:
                for j in range(RING):
                    elu_step(2, i * RING + j, j, i * (RING * GROUP) + (2 * RING + j) * GROUP)

            then(nc.vector.tensor_scalar(ef[:, 1, :], dup[:], 0.0, None, ALU.is_gt))
            then(nc.vector.tensor_scalar(ef[:, 2, :], spare, 1.0, None, ALU.mult))
            then(nc.vector.tensor_tensor(ef[:, 2, :], ef[:, 2, :], ef[:, 0, :], ALU.subtract))
            then(nc.vector.tensor_tensor(ef[:, 2, :], ef[:, 2, :], ef[:, 1, :], ALU.mult))
            nc.vector.tensor_tensor(eidx[:], ef[:, 2, :], ef[:, 0, :], ALU.add).then_inc(edges_done, 1)

            for h in range(2):
                for j in range(RING):
                    prep((j + 2) % RING)
                if h == 0:
                    dve.wait_ge(b_row_in, 16)
                else:
                    dve.wait_ge(tm_lo, NT)
                for t in range(NT):
                    dve.wait_ge(tm_ready, h * NT + t + 1)
                    nc.vector.tensor_tensor(work[:, t * HALF:(t + 1) * HALF], ps[:, 2 + 3 * h + t, :],
                                            rowbuf[:, 1, h * HALF:(h + 1) * HALF], ALU.add).then_inc(tm_sum, 1)
                for t in range(NT):
                    dve.wait_ge(tm_hi, h * NT + t + 1)
                    cols_h = slice(h * HALF, (h + 1) * HALF)
                    lo(tokv[3][:, 1, t, cols_h], work[:, t * HALF:(t + 1) * HALF], tokv[3][:, 0, t, cols_h])\
                        .then_inc(tm_lo, 1)

            for mt in range(NT):
                acc_part(pt[:, 1, mt, :], pt[:, 0, mt, :], everyone, 0.0)

            for t in range(NT):
                b = 2 + 3 * (t % 2)
                dve.wait_ge(num_ready, t + 1)
                then(nc.vector.tensor_scalar(den[:, 2 * t:2 * t + 1], ps[:, b + 2, 0:1], 1e-6, None, ALU.add))
                then(nc.vector.reciprocal(den[:, 2 * t + 1:2 * t + 2], den[:, 2 * t:2 * t + 1]))
                nc.vector.scalar_tensor_tensor(out=tok[:, t, :], in0=whole(b), scalar=den[:, 2 * t + 1:2 * t + 2],
                                               in1=tok[:, t, :], op0=ALU.mult, op1=ALU.add).then_inc(num_free, 1)
                dve.wait_ge(num_free, t + 1)
                statistics(t)

            for n, b0 in enumerate((B_Q, B_K, B_V)):
                with repeat(dve, 2, turn) as i:
                    for j in range(RING):
                        m = i * RING + j
                        acc_part(feat[1 + n][:, 1, bass.ds(m, 1), :], feat[1 + n][:, 0, bass.ds(m, 1), :],
                                 everyone, bias[:, bass.ds(m + b0, 1)])
                        prep((j + 2) % RING)

            for t in range(NT):
                dve.wait_ge(tr_hi, NT + t + 1)
                hi = feat[0][:, 0, :, t * P:(t + 1) * P]
                lo(feat[0][:, 1, :, t * P:(t + 1) * P], set_banks(t), hi).then_inc(tr_free, 1)

            acc_part(qp[:, 1, :], qp[:, 0, :], everyone, bias[:, B_IQ:B_IQ + 1])
            prep(slot_of(q_no.n))
            acc_part(kp[:, 1, :], kp[:, 0, :], everyone, bias[:, B_IK:B_IK + 1])
            prep(slot_of(q_no.n))

            for m in range(FHT):
                prep(slot_of(q_no.n))
                acc.add()
                bank = acc.n % 2
                dve.wait_ge(acc_free, acc.value)
                if m:
                    dve.wait_ge(hid_lo, m)
                dve.wait_ge(acc_ready, acc.add())
                nc.vector.scalar_tensor_tensor(out=hid, in0=ps[:, bank, 0:N], scalar=bias[:, B_U + m:B_U + m + 1],
                                               in1=gate, op0=ALU.add, op1=ALU.mult).then_inc(acc_free, 1)
                prep(slot_of(q_no.n))
                dve.wait_ge(hid_hi, m + 1)
                lo(pt[:, 1, m, :], hid, pt[:, 0, m, :]).then_inc(hid_lo, 1)

            def values(p):
                bank = acc.n % 2
                dve.wait_ge(acc_ready, acc.add())
                nc.vector.tensor_scalar(vt, ps[:, bank, 0:N], bias[:, bass.ds(p + B_IV, 1)], None, ALU.add)\
                    .then_inc(acc_free, 1)

            def values_lo():
                acc_part(vp[:, 1, :, :].rearrange("p t d -> p (t d)"), vp[:, 0, :, :].rearrange("p t d -> p (t d)"),
                         everyone, 0.0)

            prep(slot_of(q_no.n))
            values(0)
            prep(slot_of(q_no.n))
            for t in range(NT):
                dve.wait_ge(bd_added, t + 1)
                dve.wait_ge(down_ready, t + 1)
                nc.vector.tensor_tensor(tok[:, t, :], tok[:, t, :], whole(2 + 2 * t), ALU.add).then_inc(down_sum, 1)
            prep(slot_of(q_no.n))
            values_lo()
            prep(slot_of(q_no.n))

            s_no, exp_no, norm_no, pt_no = Tally(), Tally(), Tally(), Tally()

            def maxima(s):
                dve.wait_ge(s_ready, s_no.value)
                nc.vector.memset(waited[:], 0.0)
                for t in range(NT):
                    ins = nc.vector.tensor_tensor_reduce(
                        out=probs[:, s, t, :], in0=ps[:, 2 + 3 * s + t, 0:N], in1=maskb[:, t, :], scale=1.0,
                        scalar=3.0 * NONE, op0=ALU.add, op1=ALU.max, accum_out=smx[:, s, t:t + 1])
                then(ins)
                nc.vector.tensor_scalar(snm[:, s, :], smx[:, s, :], -DH ** -0.5, None, ALU.mult).then_inc(s_max, 1)

            def normalise(s):
                dve.wait_ge(s_exp, exp_no.add(NT))
                then(nc.vector.reciprocal(sinv[:, s, :], ssum[:, s, :]))
                for t in range(NT):
                    ins = nc.vector.tensor_scalar(probs[:, s, t, :], probs[:, s, t, :], sinv[:, s, t:t + 1],
                                                  None, ALU.mult)
                ins.then_inc(s_norm, 1)

            def pt_part(s, bank=None):
                b = 2 + 3 * s if bank is None else bank
                dve.wait_ge(pt_hi, pt_no.add())
                lo(pt[:, 1, :, :], ps[:, b:b + 3, 0:N], pt[:, 0, :, :]).then_inc(pt_lo, 1)

            def head_rows(s):
                return slice(s * DH, (s + 1) * DH)

            def out_part(s, p):
                f = feat[0][head_rows(s), :, bass.ds(p, 1), :]
                acc_part(f[:, 1, :, :], f[:, 0, :, :], head_rows(s), 0.0)

            def residual_statistics(t):
                dve.wait_ge(down_sum, t + 1)
                statistics(t)

            def pair(p, second, last):
                normalise(0)
                acc_part(qp[:, 1, :], qp[:, 0, :], everyone, bias[:, bass.ds(p + B_IQ, 1)])
                pt_part(0)
                normalise(1)
                prep(3)
                if second:
                    residual_statistics(0)
                acc_part(kp[:, 1, :], kp[:, 0, :], everyone, bias[:, bass.ds(p + B_IK, 1)])
                prep(0 if last else 1)
                if second:
                    residual_statistics(1)
                out_part(0, p - 1)
                pt_part(1)
                values(p)
                prep(1 if last else 2)
                if second:
                    residual_statistics(2)
                out_part(1, p - 1)
                values_lo()
                s_no.add()
                maxima(0)
                maxima(1)

            dve.wait_ge(mask_in, 16)
            s_no.add()
            maxima(0)
            maxima(1)
            pair(1, True, False)
            with repeat(dve, PAIRS - 3, {q_no: 3, acc: 6, hi_no: 5, s_no: 1, exp_no: 2 * NT, pt_no: 2,
                                         step: 4}) as i:
                pair(i + 2, False, False)
            pair(PAIRS - 1, False, True)
            normalise(0)
            normalise(1)
            for s in range(2):
                prep(slot_of(q_no.n))
                pt_part(s, 2)
                out_part(s, PAIRS - 1)

            def prep_x():
                slot = (q_no.n - Q_MOE + RING) % XRING
                dve.wait_ge(w_hi, q_no.add())
                lo(split_of(slot, 1), raw_slot(slot), split_of(slot, 0)).then_inc(w_lo, 1)

            def projected(h, t):
                dve.wait_ge(wo_ready, h * NT + t + 1)
                row = tok[:, t, h * HALF:(h + 1) * HALF]
                nc.vector.tensor_tensor(row, row, ps[:, 5 - 3 * h + t, :], ALU.add).then_inc(wo_sum, 1)
                dve.wait_ge(wo_sum, h * NT + t + 1)
                ins = nc.vector.bn_stats(stats[:, t, h, :], row)
                if h:
                    then(ins)
                    nc.vector.bn_aggr(mv[:, t, :], stats[:, t, :, :].rearrange("p a b -> p (a b)"))\
                        .then_inc(stats_done, 1)

            def normalised(t):
                dve.wait_ge(rstd_done, 3 * NT + t + 1)
                nc.vector.tensor_scalar(x2[t], tok[:, t, :], mv[:, t, 0:1],
                                        rs[:, t, 1:2], ALU.subtract, ALU.mult).then_inc(x2_done, 1)

            for q in range(Q_WO + 4, Q_MOE):
                prep(slot_of(q))
            for t in range(NT):
                dve.wait_ge(mix_done, t + 1)
                projected(0, t)
            for _ in range(2):
                prep_x()
            projected(1, 0)
            projected(1, 1)
            normalised(0)
            projected(1, 2)
            normalised(1)
            dve.wait_ge(b12_lo, 1)
            normalised(2)
            for _ in range(2):
                prep_x()

            hot3 = hot_r[:].bitcast(F32).rearrange("p (t e) -> p t e", t=NT)

            def tile3(k):
                return rt[:, k, :].rearrange("p (t e) -> p t e", t=NT)

            def spread(a):
                return a.unsqueeze(2).to_broadcast([P, NT, EXPERTS])

            w8 = cst[:, C_W8:C_W8 + EXPERTS].unsqueeze(1).to_broadcast([P, NT, EXPERTS])
            dve.wait_ge(logits_ready, 1)
            then(nc.vector.tensor_tensor(rt[:, R_LOGIT, :], ps[:, 1, 0:NT * EXPERTS], sbias[:], ALU.add))
            then(nc.vector.reduce_max(rt[:, R_MAX, 0:NT], tile3(R_LOGIT), AX_X))
            nc.vector.tensor_scalar(rt[:, R_NMAX, 0:NT], rt[:, R_MAX, 0:NT], -1.0, None, ALU.mult)\
                .then_inc(lmax_done, 1)
            then(nc.vector.tensor_tensor(tile3(R_CAND), tile3(R_LOGIT), spread(rt[:, R_MAX, 0:NT]), ALU.is_equal))
            then(nc.vector.tensor_tensor(tile3(R_CAND), tile3(R_CAND), w8, ALU.mult))
            then(nc.vector.reduce_max(rt[:, R_FIRST, 0:NT], tile3(R_CAND), AX_X))
            nc.vector.tensor_tensor(hot_r[:].rearrange("p (t e) -> p t e", t=NT), tile3(R_CAND),
                                    spread(rt[:, R_FIRST, 0:NT]), ALU.is_equal).then_inc(hot_done, 1)
            dve.wait_ge(hot_done, 1)
            for k in range(4):
                ins = nc.vector.memset(cum[:, k, 0:4], 0.0)
            then(ins)
            eid = cst[:, C_EID:C_EID + EXPERTS]
            then(nc.vector.tensor_scalar(slote[:, 2, 0:EXPERTS], eid, cst[:, C_EXP:C_EXP + 1], None, ALU.is_equal))
            then(nc.vector.tensor_scalar(rt[:, R_FIRST, EXPERTS:2 * EXPERTS], eid, float(P), None, ALU.mult))
            then(nc.vector.tensor_scalar(rt[:, R_TOTAL, 0:EXPERTS], eid, -float(P), float(P * (EXPERTS - 1)),
                                         ALU.mult, ALU.add))

            def hot_slot(s):
                nc.vector.tensor_copy(slot_hot[0:EXPERTS, :],
                                      slote[0:EXPERTS, 2, bass.ds(s, 1)].to_broadcast([EXPERTS, P]))\
                    .then_inc(slot_set, 1)

            hot_slot(0)
            dve.wait_ge(lexp_done, NT)
            then(nc.vector.reciprocal(rt[:, R_PROB, 0:NT], rt[:, R_SUM, 0:NT]))
            dve.wait_ge(count_ready, 1)
            n_e = ps[:, 6, NT * EXPERTS:(NT + 1) * EXPERTS]
            nblk = cum[:, 0, 4:12]
            tot = n_e
            then(nc.vector.tensor_scalar(nblk, tot, float(P), None, ALU.is_gt))
            for k in range(2, OVER + 1):
                then(nc.vector.scalar_tensor_tensor(out=nblk, in0=tot, scalar=float(k * P), in1=nblk,
                                                    op0=ALU.is_gt, op1=ALU.add))
            for k in range(3):
                sh = 1 << k
                then(nc.vector.tensor_tensor(cum[:, k + 1, 4:12], cum[:, k, 4:12], cum[:, k, 4 - sh:12 - sh], ALU.add))
            end = cum[:, 3, 4:12]
            first = rt[:, R_FIRST, 0:EXPERTS]

            def every_token(a):
                return a.unsqueeze(1).to_broadcast([P, NT, EXPERTS])

            then(nc.vector.scalar_tensor_tensor(out=first, in0=cum[:, 3, 3:11], scalar=float(P),
                                                in1=rt[:, R_TOTAL, 0:EXPERTS], op0=ALU.mult, op1=ALU.add))
            cnt = ps[:, 6, 0:NT * EXPERTS]
            then(nc.vector.scalar_tensor_tensor(out=tile3(R_RANK), in0=cnt.rearrange("p (t e) -> p t e", t=NT),
                                                scalar=float(P), in1=every_token(first),
                                                op0=ALU.is_ge, op1=ALU.mult))
            then(nc.vector.tensor_tensor(tile3(R_RANK), tile3(R_RANK),
                                         every_token(rt[:, R_FIRST, EXPERTS:2 * EXPERTS]), ALU.add))
            then(nc.vector.tensor_tensor(rt[:, R_RANK, :], rt[:, R_RANK, :], cnt, ALU.add))
            then(nc.vector.tensor_tensor(tile3(R_RANK), tile3(R_RANK), hot3, ALU.mult))
            then(nc.vector.reduce_sum(rt[:, R_POS, 0:NT], tile3(R_RANK), AX_X))
            nc.vector.tensor_copy(posi[:], rt[:, R_POS, 0:NT]).then_inc(pos_done, 1)
            for t in range(NT):
                ins = nc.vector.tensor_scalar(place[:, t, :], cst[:, C_IOTA:C_IOTA + P], rt[:, R_POS, t:t + 1],
                                              None, ALU.is_equal)
            ins.then_inc(place_done, 1)

            def routes():
                over = slote[:, 0, 0:OVER]
                slots = cst[:, C_SLOT:C_SLOT + OVER * EXPERTS].rearrange("p (s e) -> p s e", s=OVER)
                then(nc.vector.tensor_tensor(slotc[:], end.unsqueeze(1).to_broadcast([P, OVER, EXPERTS]), slots,
                                             ALU.is_le))
                then(nc.vector.reduce_sum(over, slotc[:], AX_X))
                then(nc.vector.tensor_scalar(slote[:, 1, EXPERTS:SLOTS], over, float(EXPERTS - 1), None, ALU.min))
                then(nc.vector.tensor_scalar(slote[:, 2, EXPERTS:SLOTS], slote[:, 1, EXPERTS:SLOTS],
                                             cst[:, C_EXP:C_EXP + 1], None, ALU.is_equal))
                then(nc.vector.tensor_scalar(rowi[:, 0:OVER], slote[:, 1, EXPERTS:SLOTS], float(QE * P), None,
                                             ALU.mult))
                nc.vector.tensor_copy(rowi[:, OVER:OVER + 1], cum[:, 3, 11:12]).then_inc(route_done, 1)

            def second_bias(t):
                dve.wait_ge(b2_ready, t + 1)
                nc.vector.scalar_tensor_tensor(out=tok[:, t, :], in0=whole(4 + 2 * (t % 2)),
                                               scalar=rt[:, R_PROB, t:t + 1], in1=tok[:, t, :],
                                               op0=ALU.mult, op1=ALU.add).then_inc(b2_added, 1)

            xt, y_no, ht, slot_no = Tally(2 * NT), Tally(), Tally(), Tally()

            def split_first(h):
                dve.wait_ge(x0_hi, h + 1)
                sl = slice(h * HALF, (h + 1) * HALF)
                lo(xsp[:, 1, sl], ps[:, 2 + h, :], xsp[:, 0, sl]).then_inc(x0_lo, 1)

            def split_slot():
                dve.wait_ge(tr_hi, xt.add())
                lo(xsp[:, 1, :], whole(2), xsp[:, 0, :]).then_inc(tr_free, 1)

            def split_hidden():
                dve.wait_ge(ht_hi, ht.add())
                lo(hts[:, 1, :], ps[:, 1, :], hts[:, 0, :]).then_inc(ht_lo, 1)

            def second_half_of_y(i):
                dve.wait_ge(y_ready, y_no.add())
                if not isinstance(i, int) or i:
                    dve.wait_ge(y_out, i * 16)
                nc.vector.tensor_copy(y_buf[:, HALF:D], ps[:, 5, :]).then_inc(y_half1, 1)

            for _ in range(2):
                prep_x()
            split_first(0)
            split_first(1)
            for _ in range(2):
                prep_x()
            routes()
            for _ in range(RING - 1):
                prep_x()
            second_bias(0)
            second_bias(1)
            split_slot()
            second_bias(2)
            dve.wait_ge(h_ready, 1)
            hot_slot(1)
            split_hidden()
            prep_x()

            def slot_turn(i, ahead):
                if ahead:
                    split_slot()
                    for _ in range(RING):
                        prep_x()
                    dve.wait_ge(h_ready, hot_no.add())
                    hot_slot(i + 2)
                second_half_of_y(i)
                split_hidden()
                for _ in range(RING):
                    prep_x()

            hot_no = Tally(1)
            slot_turn(0, True)
            with repeat(dve, EXPERTS - 3, {q_no: QE, xt: 1, y_no: 1, ht: 1, hot_no: 1}) as i:
                slot_turn(i + 1, True)
            slot_turn(EXPERTS - 2, False)
            second_half_of_y(EXPERTS - 1)

            over = dve.value_load(rowi[0:1, OVER:OVER + 1], min_val=0, max_val=OVER)
            with dve.If(over > 0):
                for o in range(OVER):
                    for _ in range(RING):
                        prep_x()
                    split_slot()
                    dve.wait_ge(h_ready, hot_no.add())
                    hot_slot(EXPERTS + o)
                    split_hidden()
                    for _ in range(RING):
                        prep_x()
                    second_half_of_y(EXPERTS + o)

            dve.wait_ge(b2_added, NT)
            for t in range(NT):
                dve.wait_ge(yg_in[t], 16)
                nc.vector.scalar_tensor_tensor(out=tok[:, t, :], in0=x2[t], scalar=rt[:, R_PROB, t:t + 1],
                                               in1=tok[:, t, :], op0=ALU.mult, op1=ALU.add).then_inc(sum_done, 1)

        @block.tensor
        def _(pe):
            q_no, acc = Tally(), Tally()

            def open_quarter():
                pe.wait_ge(w_lo, q_no.add())

            def open_acc():
                bank = acc.n % 2
                if acc.i is not None or acc.n >= 2:
                    pe.wait_ge(acc_free, acc.value - 1)
                acc.add()
                return bank

            def feature_major(slot, moving, between=None, after=3):
                open_quarter()
                bank = open_acc()
                for k in range(KT):
                    if between and k == after:
                        between()
                    for n, (a, b) in enumerate(PASSES):
                        ins = nc.tensor.matmul(ps[:, bank, 0:N], wsp[:, a, slot, k * P:(k + 1) * P],
                                               moving[:, b, k, :], start=(k == 0 and n == 0),
                                               stop=(k == KT - 1 and n == 2))
                        if k == 0 and n == 0:
                            ins.then_inc(w_started, 1)
                ins.then_inc(acc_ready, 1)

            def token_major(slot, j, stationary, banks, ready):
                open_quarter()
                for t in range(NT):
                    for kk in range(2):
                        k = 2 * j + kk
                        for n, (a, b) in enumerate(PASSES):
                            ins = nc.tensor.matmul(ps[:, banks + t, :], stationary[:, b, k, t * P:(t + 1) * P],
                                                   wsp[:, a, slot, kk * HALF:(kk + 1) * HALF],
                                                   start=(k == 0 and n == 0), stop=(k == KT - 1 and n == 2))
                            if t == 0 and kk == 0 and n == 0:
                                ins.then_inc(w_started, 1)
                    if j == 3:
                        ins.then_inc(ready, 1)

            turn = {q_no: RING, acc: RING}

            pe.wait_ge(const_in, 32)
            for t in range(NT):
                pe.wait_ge(xn_done, t + 1)
                for k in range(KT):
                    ins = nc.tensor.transpose(set_banks(t)[:, k, :], tok[:, t, k * P:(k + 1) * P], ident)
                ins.then_inc(tr_ready, 1)
            pe.wait_ge(tr_free, NT)

            for m in range(1):
                for j in range(RING):
                    feature_major(j, feat[0])
            with repeat(pe, 3, turn):
                for j in range(RING):
                    feature_major(j, feat[0])
            for h in range(2):
                for j in range(RING):
                    token_major(j, j, feat[0], 2 + 3 * h, tm_ready)

            pe.wait_ge(elu_lo, 2 * KT)
            for mt in range(NT):
                bank = open_acc()
                for k in range(KT):
                    for n, (a, b) in enumerate(PASSES):
                        ins = nc.tensor.matmul(ps[:, bank, 0:N], feat[2][:, a, k, mt * P:(mt + 1) * P],
                                               feat[1][:, b, k, :], start=(k == 0 and n == 0),
                                               stop=(k == KT - 1 and n == 2))
                ins.then_inc(acc_ready, 1)
            pe.wait_ge(acc_free, acc.value)
            pe.wait_ge(tm_lo, 2 * NT)
            pe.wait_ge(ones_set, 1)
            for t in range(NT):
                b0 = 2 + 3 * (t % 2)
                if t == 2:
                    pe.wait_ge(num_free, 1)
                for mt in range(NT):
                    for a in range(2):
                        nc.tensor.matmul(ps[:, b0 + 2, 0:2], pt[:, a, mt, t * P:(t + 1) * P], ones_r[:],
                                         start=(mt == 0 and a == 0), stop=(mt == NT - 1 and a == 1))
                for h in range(2):
                    for mt in range(NT):
                        for n, (a, b) in enumerate(PASSES):
                            ins = nc.tensor.matmul(ps[:, b0 + h, :], pt[:, a, mt, t * P:(t + 1) * P],
                                                   tokv[3][:, b, mt, h * HALF:(h + 1) * HALF],
                                                   start=(mt == 0 and n == 0), stop=(mt == NT - 1 and n == 2))
                ins.then_inc(num_ready, 1)

            for _ in range(3):
                with repeat(pe, 2, turn):
                    for j in range(RING):
                        feature_major(j, feat[0])

            pe.wait_ge(num_free, NT)
            for t in range(NT):
                pe.wait_ge(x1_done, t + 1)
                for k in range(KT):
                    ins = nc.tensor.transpose(set_banks(t)[:, k, :], tok[:, t, k * P:(k + 1) * P], ident)
                ins.then_inc(tr_ready, 1)
            feature_major(slot_of(Q_PAIR0), feat[1])
            feature_major(slot_of(Q_PAIR0 + 1), feat[2])
            pe.wait_ge(tr_free, 2 * NT)
            feature_major(slot_of(Q_GU), feat[0])
            for q in range(Q_GU + 1, Q_DOWN - 1):
                feature_major(slot_of(q), feat[0])
            feature_major(slot_of(Q_DOWN - 1), feat[3])
            values_acc = acc.value
            pe.wait_ge(hid_lo, FHT)
            for t in range(NT):
                for h in range(2):
                    for k in range(FHT):
                        blk = h * FHT + k
                        slot, kk = slot_of(Q_DOWN + blk // 2), blk % 2
                        if t == 0 and kk == 0:
                            open_quarter()
                        for n, (a, b) in enumerate(PASSES):
                            ins = nc.tensor.matmul(ps[:, 2 + 2 * t + h, :], pt[:, b, k, t * P:(t + 1) * P],
                                                   wsp[:, a, slot, kk * HALF:(kk + 1) * HALF],
                                                   start=(k == 0 and n == 0), stop=(k == FHT - 1 and n == 2))
                            if t == 0 and n == 0 and kk == 0:
                                ins.then_inc(w_started, 1)
                ins.then_inc(down_ready, 1)

            pt_no, norm_no, s_no = Tally(), Tally(), Tally()

            def transpose_probs(s, bank=None):
                b = 2 + 3 * s if bank is None else bank
                pe.wait_ge(s_norm, norm_no.add())
                for mt in range(NT):
                    for t in range(NT):
                        ins = nc.tensor.transpose(ps[:, b + mt, t * P:(t + 1) * P],
                                                  probs[:, s, t, mt * P:(mt + 1) * P], ident)
                ins.then_inc(pt_ready, 1)

            def attend(s):
                pe.wait_ge(pt_lo, pt_no.add())
                bank = open_acc()
                for mt in range(NT):
                    for n, (a, b) in enumerate(PASSES):
                        ins = nc.tensor.matmul(ps[:, bank, 0:N], vp[:, a, mt, :], pt[:, b, mt, :],
                                               start=(mt == 0 and n == 0), stop=(mt == NT - 1 and n == 2))
                ins.then_inc(acc_ready, 1)

            def scores():
                for t in range(NT):
                    for n, (a, b) in enumerate(PASSES):
                        for s in range(2):
                            rows = slice(s * DH, (s + 1) * DH)
                            ins = nc.tensor.matmul(ps[:, 2 + 3 * s + t, 0:N], qp[rows, a, t * P:(t + 1) * P],
                                                   kp[rows, b, :], start=(n == 0), stop=(n == 2))
                ins.then_inc(s_ready, 1)

            def transpose_values():
                bank = open_acc()
                for mt in range(NT):
                    ins = nc.tensor.transpose(ps[:, bank, mt * P:(mt + 1) * P], vt[:, mt * P:(mt + 1) * P], ident)
                ins.then_inc(acc_ready, 1)

            def pair():
                feature_major(1, feat[1])
                feature_major(2, feat[2], lambda: transpose_probs(0))
                attend(0)
                transpose_probs(1)
                feature_major(3, feat[3])
                attend(1)
                pe.wait_ge(acc_free, acc.value - 1)
                transpose_values()
                scores()

            pe.wait_ge(acc_free, values_acc)
            transpose_values()
            pe.wait_ge(down_sum, NT)
            scores()
            with repeat(pe, PAIRS - 2, {q_no: 3, acc: 6, norm_no: 2, pt_no: 2}):
                pair()
            pair()
            def project(h, j):
                token_major(slot_of(Q_WO + WO_ORDER.index((h, j))), j, feat[0], 5 - 3 * h, wo_ready)

            pe.wait_ge(s_max, HEADS)
            project(0, 0)
            transpose_probs(0)
            project(0, 1)
            pe.wait_ge(acc_free, acc.value)
            attend(0)
            transpose_probs(1, 2)
            project(0, 2)
            attend(1)
            project(1, 0)
            pe.wait_ge(acc_free, acc.value)
            for h, j in WO_ORDER[4:]:
                project(h, j)

            pe.wait_ge(wo_sum, 2 * NT)
            for t in range(NT):
                pe.wait_ge(x2_done, t + 1)
                for k in range(KT):
                    ins = nc.tensor.transpose(set_banks(t)[:, k, :], x2[t][:, k * P:(k + 1) * P], ident)
                ins.then_inc(x2t_ready, 1)
            for t in range(NT):
                pe.wait_ge(x2t_copied, t + 1)
                for k in range(KT):
                    ins = nc.tensor.matmul(ps[0:EXPERTS, 0, t * P:(t + 1) * P], swt[:, k, :],
                                           x2t[t][:, k * P:(k + 1) * P], start=(k == 0), stop=(k == KT - 1))
            ins.then_inc(lt_ready, 1)
            pe.wait_ge(lt_copied, 1)
            for t in range(NT):
                ins = nc.tensor.transpose(ps[:, 1, t * EXPERTS:(t + 1) * EXPERTS],
                                          logits_t[:, t * P:(t + 1) * P], ident[0:EXPERTS, 0:EXPERTS])
            ins.then_inc(logits_ready, 1)
            pe.wait_ge(tri_set, 1)
            pe.wait_ge(hot_done, 1)
            for t in range(NT):
                for u in range(t + 1):
                    nc.tensor.matmul(ps[:, 6, t * EXPERTS:(t + 1) * EXPERTS],
                                     tri_r[:, 0:P] if u == t else tri_r[:, P:2 * P],
                                     hot_r[:, u * EXPERTS:(u + 1) * EXPERTS], start=(u == 0), stop=(u == t))
            for u in range(NT):
                ins = nc.tensor.matmul(ps[:, 6, NT * EXPERTS:(NT + 1) * EXPERTS], tri_r[:, P:2 * P],
                                       hot_r[:, u * EXPERTS:(u + 1) * EXPERTS], start=(u == 0), stop=(u == NT - 1))
            ins.then_inc(count_ready, 1)
            for t in range(NT):
                ins = nc.tensor.transpose(ps[0:EXPERTS, 1, t * P:(t + 1) * P],
                                          hot_r[:, t * EXPERTS:(t + 1) * EXPERTS].bitcast(F32), ident)
            ins.then_inc(hott_ready, 1)
            pe.wait_ge(place_done, 1)
            for k in range(KT):
                for t in range(NT):
                    ins = nc.tensor.matmul(whole(2)[:, k * P:(k + 1) * P], x2[t][:, k * P:(k + 1) * P],
                                           place[:, t, :], start=(t == 0), stop=(t == NT - 1))
                if k % 4 == 3:
                    ins.then_inc(x0_ready, 1)

            def second_bias(t):
                for h in range(2):
                    for b in range(2):
                        ins = nc.tensor.matmul(ps[:, 4 + 2 * (t % 2) + h, :], pt[0:EXPERTS, 0, 0, t * P:(t + 1) * P],
                                               b12r[:, b, F + h * HALF:F + (h + 1) * HALF],
                                               start=(b == 0), stop=(b == 1))
                ins.then_inc(b2_ready, 1)

            xs_no, xt, slot_no, h_act_no, ht_no, y_no = Tally(), Tally(2 * NT), Tally(), Tally(), Tally(), Tally()
            xst = xsp[:].rearrange("p h (k n) -> p h k n", k=KT)
            htk = hts.rearrange("p h (k n) -> p h k n", k=F // P)

            def load_tokens(src):
                for k in range(KT):
                    ins = nc.tensor.transpose(whole(2)[:, k * P:(k + 1) * P], src[:, k * P:(k + 1) * P], ident)
                ins.then_inc(tr_ready, 1)

            def late_tokens():
                pe.wait_ge(xs_late_in, xs_no.add(16))
                load_tokens(rowbuf[:, 0, :])

            def up(first, base):
                if first:
                    pe.wait_ge(x0_lo, 1)
                else:
                    pe.wait_ge(tr_free, xt.add())
                    pe.wait_ge(h_act, h_act_no.add())
                for j in range(4):
                    open_quarter()
                    if first and j == 2:
                        pe.wait_ge(x0_lo, 2)
                    for kk in range(2):
                        k = 2 * j + kk
                        for n, (a, b) in enumerate(PASSES):
                            ins = nc.tensor.matmul(ps[:, 0, :], xst[:, b, k, :],
                                                   split_of(base + j, a)[:, kk * HALF:(kk + 1) * HALF],
                                                   start=(k == 0 and n == 0), stop=False)
                            if kk == 0 and n == 0:
                                ins.then_inc(w_started, 1)
                pe.wait_ge(slot_set, slot_no.add())
                for b in range(2):
                    ins = nc.tensor.matmul(ps[:, 0, :], slot_hot[0:EXPERTS, :], b12r[:, b, 0:F],
                                           start=False, stop=(b == 1))
                ins.then_inc(h_ready, 1)

            def down(first, base):
                pe.wait_ge(ht_lo, ht_no.add())
                if not first:
                    pe.wait_ge(y_half0, y_no.add())
                    pe.wait_ge(y_half1, y_no.value)
                for j in range(4):
                    open_quarter()
                    h = j // 2
                    for kk in range(2):
                        k = 2 * (j % 2) + kk
                        for n, (a, b) in enumerate(PASSES):
                            ins = nc.tensor.matmul(ps[:, 4 + h, :], htk[:, b, k, :],
                                                   split_of(base + j, a)[:, kk * HALF:(kk + 1) * HALF],
                                                   start=(k == 0 and n == 0), stop=(k == 3 and n == 2))
                            if kk == 0 and n == 0:
                                ins.then_inc(w_started, 1)
                ins.then_inc(y_ready, 1)

            def transpose_hidden():
                pe.wait_ge(h_act, h_act_no.value + 1)
                for k in range(F // P):
                    ins = nc.tensor.transpose(ps[:, 1, k * P:(k + 1) * P], h_buf[:, k * P:(k + 1) * P], ident)
                ins.then_inc(ht_ready, 1)

            pe.wait_ge(b12_lo, 1)
            up(True, RING)
            pe.wait_ge(hott_copied, 1)
            second_bias(0)
            second_bias(1)
            pe.wait_ge(xs_in, 16)
            load_tokens(xs_all[:, 0, :])
            transpose_hidden()
            pe.wait_ge(b2_added, 1)
            second_bias(2)
            pe.wait_ge(b2_added, NT)

            def slot_turn(first, tokens=None):
                up(False, 0)
                if tokens:
                    tokens()
                down(first, RING)
                transpose_hidden()

            slot_turn(True, lambda: load_tokens(xs_all[:, 1, :]))
            for n in range(2, AHEAD):
                slot_turn(False, lambda: load_tokens(xs_all[:, n, :]))
            slot_turn(False, late_tokens)
            slot_turn(False)
            down(False, 0)

            over = pe.value_load(rowi[0:1, OVER:OVER + 1], min_val=0, max_val=OVER)
            with pe.If(over > 0):
                for o in range(OVER):
                    late_tokens()
                    up(False, RING)
                    transpose_hidden()
                    down(False, 0)


def _feature_quarters(w):
    k, n = w.shape
    return w.reshape(k // 128, 128, n // 128, 128).transpose(2, 1, 0, 3).reshape(-1, 1024)


def _token_quarters(w):
    k, n = w.shape
    return w.reshape(k // 256, 2, 128, n // 512, 512).transpose(3, 0, 2, 1, 4).reshape(-1, 1024)


def kernel(**inputs):
    import numpy as _np
    import concourse.bacc as _bacc
    from concourse import mybir as _mybir
    from concourse.bass_utils import run_bass_kernel_spmd as _run

    a = {k: _np.asarray(v) for k, v in inputs.items()}
    f32 = _np.float32
    g = lambda name: a["L0_gnn_" + name]
    mx = lambda name: a["L0_mix_" + name]
    ff = lambda name: a["L0_ffn_" + name]

    pad = FHT * P - FH
    wqkv = mx("Wqkv")
    wg = _np.pad(mx("Wg"), ((0, 0), (0, pad)))
    wu = _np.pad(mx("Wu"), ((0, 0), (0, pad)))
    gate_up = _np.stack([_feature_quarters(wg).reshape(FHT, P, D), _feature_quarters(wu).reshape(FHT, P, D)], 1)
    wd = _np.pad(mx("Wd"), ((0, pad), (0, 0)))
    down = wd.reshape(FHT, P, 2, HALF).transpose(2, 0, 1, 3).reshape(3, 2, P, HALF).transpose(0, 2, 1, 3)
    pairs = _np.stack([_feature_quarters(g(n).T).reshape(PAIRS, P, D) for n in ("wiq", "wik", "wiv")], 1)
    stream = _np.concatenate([
        _feature_quarters(wqkv[:, 0:D]), _feature_quarters(wqkv[:, D:2 * D]), _token_quarters(wqkv[:, 2 * D:]),
        _feature_quarters(g("wq").T), _feature_quarters(g("wk").T), _feature_quarters(g("wv").T),
        pairs[0, 0:2].reshape(-1, D), gate_up.reshape(-1, D), pairs[0, 2], down.reshape(-1, D),
        pairs[1:].reshape(-1, D),
        _token_quarters(g("wo").T).reshape(2, 4, P, D)[tuple(_np.array(WO_ORDER).T)].reshape(-1, D)])
    w1, w2 = ff("w1"), ff("w2")
    experts = _np.concatenate(
        [_np.concatenate([_token_quarters(w1[e]), _token_quarters(w2[e])]) for e in range(EXPERTS)])

    col = lambda v: _np.pad(v, (0, -len(v) % P)).reshape(-1, P).T
    bq = mx("bqkv")
    cols = _np.concatenate([col(bq[0:D]), col(bq[D:2 * D])] + [col(g(n)) for n in
                           ("bq", "bk", "bv", "biq", "bik", "biv")] + [col(mx("bg")), col(mx("bu"))], 1)
    row8 = _np.zeros(D, f32)
    row8[0:NT * EXPERTS] = _np.tile(ff("switch_b"), NT)
    rowb = _np.stack([bq[2 * D:], mx("g1"), mx("b1"), mx("bd"), mx("g2"), mx("b2"), g("bo"), row8])

    r = _np.arange(P)
    consts = _np.concatenate([
        _np.eye(P), (r[:, None] < r[None, :]).astype(f32), _np.ones((P, P)),
        _np.tile(_np.arange(EXPERTS, 0, -1), (P, 1)),
        _np.tile(_np.arange(EXPERTS), (P, 1)), _np.tile(_np.repeat(_np.arange(OVER), EXPERTS), (P, 1)), r[:, None],
        _np.tile(r, (P, 1)), N * N + r[:, None] + P * _np.arange(EC)[None, :]], 1).astype(f32)
    later = (_np.arange(N)[None, None, :] > (_np.arange(GROUP) * P)[None, :, None] + r[:, None, None]).astype(f32)

    c = _np.ascontiguousarray
    arrays = {
        "x": a["x"], "rowb": rowb, "cols": c(cols), "consts": consts, "later": later,
        "src_rows": a["src"], "dst_rows": a["dst"],
        "src_cols": c(a["src"].reshape(EC, P).T), "dst_cols": c(a["dst"].reshape(EC, P).T),
        "type_cols": c(a["edge_type_5"].reshape(EC, P).T), "type_weights": g("edge_type_weights"),
        "w_stream": stream, "w_experts": experts,
        "switch_w": c(ff("switch_w").reshape(KT, P, EXPERTS).transpose(1, 0, 2)),
        "b12": _np.concatenate([ff("b1"), ff("b2")], 1),
    }
    nc = _bacc.Bacc("TRN2", target_bir_lowering=False, num_devices=1)
    aps = [nc.dram_tensor("in_" + k, v.shape, _mybir.dt.from_np(v.dtype), kind="ExternalInput").ap()
           for k, v in arrays.items()]
    out = nc.dram_tensor("out_dram", (N, D), _mybir.dt.float32, kind="ExternalOutput").ap()
    graph_layer(nc, *aps, out)
    got = _run(nc, [{"in_" + k: v for k, v in arrays.items()}], core_ids=[0])
    return got.results[0]["out_dram"]
```
